# Optimizing a Trainium2 kernel written in Bass

```python
import numpy as np
import jax
import jax.numpy as jnp

def _softmax(x, axis=-1):
    return jax.nn.softmax(x, axis=axis)

def _gelu(x):
    return jax.nn.gelu(x, approximate=True)

def _silu(x):
    return jax.nn.silu(x)

def _sigmoid(x):
    return jax.nn.sigmoid(x)

def _layernorm(x, axis=-1, eps=1e-05):
    m = jnp.mean(x, axis=axis, keepdims=True)
    v = jnp.var(x, axis=axis, keepdims=True)
    return (x - m) / jnp.sqrt(v + eps)

def _scatter_add(tgt, idx, src, axis=0):
    return tgt.at[idx].add(src)

def _segment_sum(src, seg, n):
    return jax.ops.segment_sum(src, seg, n)
kernel_name = 'mk_gnn_preln_d4_gnn_r64_623f81'

def setup_inputs(seed: int=0):
    np.random.seed(seed)
    _w = jnp.asarray

    def _rec_inputs():
        import jax
        import jax.numpy as jnp
        _gk = jax.random.key(seed)
        x = -0.000202 + 1 * jax.random.normal(jax.random.fold_in(_gk, 1), (100000, 64), jnp.float32)
        src = jax.random.randint(jax.random.fold_in(_gk, 2), (25000,), 0, 100000, jnp.int32)
        dst = jax.random.randint(jax.random.fold_in(_gk, 3), (25000,), 0, 100000, jnp.int32)
        _o = jnp.argsort(dst, stable=True)
        src = src[_o]
        dst = dst[_o]
        edge_attr_32 = -5.16925e-05 + 1.00005 * jax.random.normal(jax.random.fold_in(_gk, 13), (25000, 32), jnp.float32)
        edge_weight = -1.20086e-11 + 0.13101 * jax.random.normal(jax.random.fold_in(_gk, 15), (25000,), jnp.float32)
        edge_weight1 = 0.000614103 + 0.999867 * jax.random.normal(jax.random.fold_in(_gk, 16), (25000, 1), jnp.float32)
        return (x, src, dst, edge_attr_32, edge_weight, edge_weight1)
    x, src, dst, edge_attr_32, edge_weight, edge_weight1 = _rec_inputs()

    def _L0_gnn_setup():
        import jax, jax.numpy as jnp
        import numpy as np
        N = 100000
        E = 25000
        C_IN = 64
        C_HID = 2 * C_IN
        C_OUT = 64

        def _sgconv(x, W, b, src, dst, n):
            loop = jnp.arange(n, dtype=src.dtype)
            s = jnp.concatenate([src, loop])
            d = jnp.concatenate([dst, loop])
            w = jnp.ones(s.shape[0], dtype=x.dtype)
            deg = jax.ops.segment_sum(w, d, num_segments=n)
            dinv = jnp.where(deg > 0, jax.lax.rsqrt(deg), 0.0)
            norm = dinv[s] * dinv[d]
            msgs = norm[:, None] * x[s]
            agg = jax.ops.segment_sum(msgs, d, num_segments=n)
            return agg @ W.T + b
        key = jax.random.key(seed)
        k1, k2, k3, k4, k5, k6, k7 = jax.random.split(key, 7)
        x = jax.random.normal(k1, (N, C_IN), dtype=jnp.float32)
        edge_index = jax.random.randint(k2, (2, E), 0, N, dtype=jnp.int64)
        lim3 = 1.0 / np.sqrt(C_IN)
        W3 = jax.random.uniform(k3, (C_HID, C_IN), jnp.float32, -lim3, lim3)
        b3 = jax.random.uniform(k4, (C_HID,), jnp.float32, -lim3, lim3)
        lim4 = 1.0 / np.sqrt(C_HID)
        W4 = jax.random.uniform(k5, (C_OUT, C_HID), jnp.float32, -lim4, lim4)
        b4 = jax.random.uniform(k6, (C_OUT,), jnp.float32, -lim4, lim4)
        return {'x': x, 'edge_index': edge_index, 'W3': W3, 'b3': b3, 'W4': W4, 'b4': b4}
    _L0_gnn_all = _L0_gnn_setup()
    _L0_gnn_in = {k: v for k, v in _L0_gnn_all.items() if k in ('W3', 'b3', 'W4', 'b4')}
    del _L0_gnn_all

    def _L1_gnn_setup():
        import jax, jax.numpy as jnp
        import numpy as np
        N = 50000
        C = 64
        E_OFF = 12500
        N_SUB = 4
        M_TERMS = 20

        def _expm_multiply(x, edge_src, edge_dst, edge_w, t):
            n = x.shape[0]
            scale = -(t[0] / N_SUB)

            def A_apply(v):
                return scale * jax.ops.segment_sum(edge_w[:, None] * v[edge_dst], edge_src, num_segments=n)
            ks = jnp.arange(1, M_TERMS + 1, dtype=x.dtype)

            def substep(v, _):

                def taylor(carry, k):
                    term, acc = carry
                    term = A_apply(term) / k
                    return ((term, acc + term), None)
                (_, acc), _ = jax.lax.scan(taylor, (v, v), ks)
                return (acc, None)
            out, _ = jax.lax.scan(substep, x, None, length=N_SUB)
            return out
        key = jax.random.key(seed)
        k1, k2, k3, k4, k5 = jax.random.split(key, 5)
        src = jax.random.randint(k1, (E_OFF,), 0, N)
        dst = jax.random.randint(k2, (E_OFF,), 0, N)
        w = jax.random.uniform(k3, (E_OFF,), dtype=jnp.float32) / 16.0
        deg = jax.ops.segment_sum(w, src, num_segments=N)
        edge_src = jnp.concatenate([src, jnp.arange(N, dtype=src.dtype)])
        edge_dst = jnp.concatenate([dst, jnp.arange(N, dtype=dst.dtype)])
        edge_w = jnp.concatenate([-w, deg])
        x = jax.random.normal(k4, (N, C), dtype=jnp.float32)
        t = jax.random.uniform(k5, (1,), dtype=jnp.float32) * 0.2 + 1e-08
        return {'x': x, 'edge_src': edge_src, 'edge_dst': edge_dst, 'edge_w': edge_w, 't': t}
    _L1_gnn_all = _L1_gnn_setup()
    _L1_gnn_in = {k: v for k, v in _L1_gnn_all.items() if k in ('t',)}
    del _L1_gnn_all

    def _L2_gnn_setup():
        import jax, jax.numpy as jnp
        import numpy as np
        N_NODES = 100000
        N_EDGES = 50000
        EDGE_OUT = 32
        HID = 128
        NODE_OUT = 64
        N_GRAPHS = 16
        key = jax.random.key(seed)
        ks = jax.random.split(key, 9)
        x = jax.random.normal(ks[0], (N_NODES, 64), dtype=jnp.float32)
        edge_index = jax.random.randint(ks[1], (2, N_EDGES), 0, N_NODES, dtype=jnp.int64)
        edge_attr = jax.random.normal(ks[2], (N_EDGES, EDGE_OUT), dtype=jnp.float32)
        u = jax.random.normal(ks[3], (N_GRAPHS, 1), dtype=jnp.float32)
        batch = jnp.sort(jax.random.randint(ks[4], (N_NODES,), 0, N_GRAPHS, dtype=jnp.int64))
        d_in = 3 * EDGE_OUT + 1
        W1 = jax.random.normal(ks[5], (d_in, HID), dtype=jnp.float32) / np.sqrt(d_in)
        b1 = jnp.zeros((HID,), dtype=jnp.float32)
        W2 = jax.random.normal(ks[6], (HID, NODE_OUT), dtype=jnp.float32) / np.sqrt(HID)
        b2 = jnp.zeros((NODE_OUT,), dtype=jnp.float32)
        return {'x': x, 'edge_index': edge_index, 'edge_attr': edge_attr, 'u': u, 'batch': batch, 'W1': W1, 'b1': b1, 'W2': W2, 'b2': b2}
    _L2_gnn_all = _L2_gnn_setup()
    _L2_gnn_in = {k: v for k, v in _L2_gnn_all.items() if k in ('u', 'W1', 'b1', 'W2', 'b2')}
    del _L2_gnn_all

    def _L3_gnn_setup():
        import jax, jax.numpy as jnp
        import numpy as np
        N_NODES = 50000
        DEG = 16
        N_EDGES = N_NODES * DEG
        C_IN = 64
        C_OUT = 64
        key = jax.random.key(seed)
        k_x, k_src, k_ea, k_w, k_b = jax.random.split(key, 5)
        x = jax.random.normal(k_x, (N_NODES, C_IN), dtype=jnp.float32)
        dst = jnp.repeat(jnp.arange(N_NODES, dtype=jnp.int32), DEG)
        src = jax.random.randint(k_src, (N_EDGES,), 0, N_NODES, dtype=jnp.int32)
        edge_index = jnp.stack([src, dst], axis=0)
        edge_attr = jax.random.normal(k_ea, (N_EDGES, 1), dtype=jnp.float32)
        W = jax.random.normal(k_w, (C_OUT, 2 * C_IN), dtype=jnp.float32) * (1.0 / np.sqrt(2 * C_IN))
        b = jax.random.normal(k_b, (C_OUT,), dtype=jnp.float32) * 0.01
        return {'x': x, 'edge_index': edge_index, 'edge_attr': edge_attr, 'W': W, 'b': b}
    _L3_gnn_all = _L3_gnn_setup()
    _L3_gnn_in = {k: v for k, v in _L3_gnn_all.items() if k in ('W', 'b')}
    del _L3_gnn_all
    return {'x': x, 'src': src, 'dst': dst, 'edge_attr_32': edge_attr_32, 'edge_weight': edge_weight, 'edge_weight1': edge_weight1, 'L0_gnn_W3': _L0_gnn_in['W3'], 'L0_gnn_b3': _L0_gnn_in['b3'], 'L0_gnn_W4': _L0_gnn_in['W4'], 'L0_gnn_b4': _L0_gnn_in['b4'], 'L1_gnn_t': _L1_gnn_in['t'], 'L2_gnn_u': _L2_gnn_in['u'], 'L2_gnn_W1': _L2_gnn_in['W1'], 'L2_gnn_b1': _L2_gnn_in['b1'], 'L2_gnn_W2': _L2_gnn_in['W2'], 'L2_gnn_b2': _L2_gnn_in['b2'], 'L3_gnn_W': _L3_gnn_in['W'], 'L3_gnn_b': _L3_gnn_in['b']}

def reference(x, src, dst, edge_attr_32, edge_weight, edge_weight1, L0_gnn_W3, L0_gnn_b3, L0_gnn_W4, L0_gnn_b4, L1_gnn_t, L2_gnn_u, L2_gnn_W1, L2_gnn_b1, L2_gnn_W2, L2_gnn_b2, L3_gnn_W, L3_gnn_b):
    import jax
    import jax.numpy as jnp

    def _L0_gnn_ref(x, edge_index, W3, b3, W4, b4):
        import jax, jax.numpy as jnp
        import numpy as np
        N = 100000
        E = 25000
        C_IN = 64
        C_HID = 2 * C_IN
        C_OUT = 64

        def _sgconv(x, W, b, src, dst, n):
            loop = jnp.arange(n, dtype=src.dtype)
            s = jnp.concatenate([src, loop])
            d = jnp.concatenate([dst, loop])
            w = jnp.ones(s.shape[0], dtype=x.dtype)
            deg = jax.ops.segment_sum(w, d, num_segments=n)
            dinv = jnp.where(deg > 0, jax.lax.rsqrt(deg), 0.0)
            norm = dinv[s] * dinv[d]
            msgs = norm[:, None] * x[s]
            agg = jax.ops.segment_sum(msgs, d, num_segments=n)
            return agg @ W.T + b
        src, dst = (edge_index[0], edge_index[1])
        n = x.shape[0]
        h = jax.nn.relu(_sgconv(x, W3, b3, src, dst, n))
        return _sgconv(h, W4, b4, src, dst, n)

    def _L1_gnn_ref(x, edge_src, edge_dst, edge_w, t):
        import jax, jax.numpy as jnp
        import numpy as np
        N = 50000
        C = 64
        E_OFF = 12500
        N_SUB = 4
        M_TERMS = 20

        def _expm_multiply(x, edge_src, edge_dst, edge_w, t):
            n = x.shape[0]
            scale = -(t[0] / N_SUB)

            def A_apply(v):
                return scale * jax.ops.segment_sum(edge_w[:, None] * v[edge_dst], edge_src, num_segments=n)
            ks = jnp.arange(1, M_TERMS + 1, dtype=x.dtype)

            def substep(v, _):

                def taylor(carry, k):
                    term, acc = carry
                    term = A_apply(term) / k
                    return ((term, acc + term), None)
                (_, acc), _ = jax.lax.scan(taylor, (v, v), ks)
                return (acc, None)
            out, _ = jax.lax.scan(substep, x, None, length=N_SUB)
            return out
        t = jnp.clip(t, 1e-08)
        return _expm_multiply(x, edge_src, edge_dst, edge_w, t)

    def _L2_gnn_ref(x, edge_index, edge_attr, u, batch, W1, b1, W2, b2):
        import jax, jax.numpy as jnp
        import numpy as np
        N_NODES = 100000
        N_EDGES = 50000
        EDGE_OUT = 32
        HID = 128
        NODE_OUT = 64
        N_GRAPHS = 16
        N = x.shape[0]
        row = edge_index[0]
        seg_sum = jax.ops.segment_sum(edge_attr, row, num_segments=N)
        seg_max = jax.ops.segment_max(edge_attr, row, num_segments=N)
        cnt = jax.ops.segment_sum(jnp.ones((edge_attr.shape[0], 1), edge_attr.dtype), row, num_segments=N)
        seg_mean = seg_sum / jnp.maximum(cnt, 1.0)
        seg_max = jnp.where(cnt > 0, seg_max, 0.0)
        h = jnp.concatenate([seg_sum, seg_max, seg_mean, u[batch]], axis=1)
        h = jax.nn.relu(h @ W1 + b1)
        return h @ W2 + b2

    def _L3_gnn_ref(x, edge_index, edge_attr, W, b):
        import jax, jax.numpy as jnp
        import numpy as np
        N_NODES = 50000
        DEG = 16
        N_EDGES = N_NODES * DEG
        C_IN = 64
        C_OUT = 64
        src = edge_index[0]
        dst = edge_index[1]
        x_i = x[dst]
        x_j = x[src]
        feat = jnp.concatenate([x_i, x_j - x_i], axis=-1)
        msg = jax.nn.relu(feat @ W.T + b)
        out = jax.ops.segment_max(msg, dst, num_segments=x.shape[0])
        return jnp.where(jnp.isneginf(out), 0.0, out)
    edge_index = jnp.stack([src, dst])
    batch0 = jnp.zeros((100000,), jnp.int32)
    h = jnp.maximum(_layernorm(x, axis=-1), 0.0)
    x = x + _L0_gnn_ref(h, edge_index, L0_gnn_W3, L0_gnn_b3, L0_gnn_W4, L0_gnn_b4)
    h = jnp.maximum(_layernorm(x, axis=-1), 0.0)
    x = x + _L1_gnn_ref(h, src, dst, edge_weight, L1_gnn_t)
    h = jnp.maximum(_layernorm(x, axis=-1), 0.0)
    x = x + _L2_gnn_ref(h, edge_index, edge_attr_32, L2_gnn_u, batch0, L2_gnn_W1, L2_gnn_b1, L2_gnn_W2, L2_gnn_b2)
    h = jnp.maximum(_layernorm(x, axis=-1), 0.0)
    x = x + _L3_gnn_ref(h, edge_index, edge_weight1, L3_gnn_W, L3_gnn_b)
    return x

_drawn_inputs = setup_inputs


def setup_inputs(seed=0):
    import zlib

    import numpy as np

    out = dict(_drawn_inputs(seed))
    spreads = {'L2_gnn_b1': (0.0, 0.1), 'L2_gnn_b2': (0.0, 0.1)}
    factors = {'edge_weight': 64.0, 'L3_gnn_b': 31.597}
    for name, (base, spread) in spreads.items():
        noise = np.random.default_rng([zlib.crc32(name.encode()), seed]).standard_normal(out[name].shape)
        drawn = base * np.exp(spread * noise) if base else spread * noise
        out[name] = jnp.asarray(drawn.astype(out[name].dtype))
    for name, factor in factors.items():
        out[name] = (out[name] * factor).astype(out[name].dtype)
    return out
```

```python
import concourse.bass as bass
from concourse import mybir
from contextlib import ExitStack

N, C, E = 100000, 64, 25000
HID = 128
ATTR = 32
P = 125
T = E // P
U = 4
CE = U * P
CHUNKS = T // U
PAIRS = CHUNKS // 2
ND = N // P
HALF = ND // 2
PAYW = 4 + ATTR
N_SUB, M_TERMS = 4, 20
TERMS = N_SUB * M_TERMS
EPS = 1e-5
BIG = 3.0e38


def taylor_ratios():
    term = [1]
    for k in range(M_TERMS, 0, -1):
        term.append(term[-1] * k)
    term.reverse()
    c = [1]
    for _ in range(N_SUB):
        new = [0] * (len(c) + M_TERMS)
        for i, a in enumerate(c):
            for k, b in enumerate(term):
                new[i + k] += a * b
        c = new
    return [0.0] + [c[k] / c[k - 1] for k in range(1, TERMS + 1)]


class Chain:

    def __init__(self, eng, sem, base=0):
        self.eng, self.sem, self.base, self.n = eng, sem, base, 0

    def link(self, ins):
        self.n += 1
        ins.then_inc(self.sem, 1)
        self.eng.wait_ge(self.sem, self.base + self.n)


def gnn(nc, x, src_pad, dst_pad, attr, w, w3t, b3, w4t, b4, t_in, u_in, w1, b1, w2, b2, wl3, bl3, ratios, out):
    f32, i32, u8, f16 = mybir.dt.float32, mybir.dt.int32, mybir.dt.uint8, mybir.dt.float16
    ALU, ACT, AX = mybir.AluOpType, mybir.ActivationFunctionType, mybir.AxisListType

    qs = nc.dram_tensor("qs_table", [N, C], f32).ap()
    x1 = nc.dram_tensor("x1_table", [N, C], f32).ap()
    dinv_tab = nc.dram_tensor("dinv_table", [N, 1], f32).ap()
    endp_tab = nc.dram_tensor("endp_table", [N, 1], f32).ap()
    pay = nc.dram_tensor("sorted_edges", [E, PAYW], f32).ap()
    srcs_pad = nc.dram_tensor("sorted_src", [E + 2], f32).ap()
    terms = [nc.dram_tensor(f"terms{i}", [E + 1, C], f32).ap() for i in range(2)]

    tile_major = lambda a: a.rearrange("(t p) -> p t", p=P)
    chunk_rows = lambda a, c: a[bass.ds(c * CE, CE), :].rearrange("(u p) f -> p u f", p=P)

    ctx = ExitStack()
    with ctx:
        ctx.enter_context(nc.allow_non_contiguous_dma("index columns and broadcasts"))

        def alloc(stack):
            used = []

            def sem(name):
                used.append(nc.alloc_semaphore(name))
                return used[-1]

            def end():
                if used:
                    nc.clear_and_free_semaphores(used)
                    nc.all_engine_barrier()

            stack.callback(end)
            return (lambda name, shape, dt=f32: stack.enter_context(nc.sbuf_tensor(name, shape, dt)),
                    sem, lambda name: [sem(f"{name}_{b}") for b in range(2)])

        sb = lambda name, shape, dt=f32: ctx.enter_context(nc.sbuf_tensor(name, shape, dt))
        two = [ctx.enter_context(nc.psum_tensor(f"banks{i}", [128, 2, 512], f32)) for i in range(4)]
        bank = [two[i // 2][:, i % 2, :] for i in range(8)]

        pool_went_on, pe_went_on = (ctx.enter_context(nc.semaphore(n)) for n in ("pool_went_on", "pe_went_on"))

        ident = sb("ident", [128, 128])
        src_i, dst_i = sb("src_i", [P, T], i32), sb("dst_i", [P, T], i32)
        dst_end = sb("dst_end", [P, T], i32)
        dinv_d = sb("dinv_d", [P, T])
        w_s = sb("w_s", [P, T])
        gi_i = sb("gi_i", [P, T], i32)
        srcS_i, dstS_i, srcS_end = sb("srcS_i", [P, T], i32), sb("dstS_i", [P, T], i32), sb("srcS_end", [P, T], i32)
        mask_d, mask_s = sb("mask_d", [C + 1, E], u8), sb("mask_s", [C + 1, E], u8)
        w3_sb, w4_sb = sb("w3_sb", [C, HID]), sb("w4_sb", [HID, C])
        w1_sb, w1u = sb("w1_sb", [ATTR, 3, HID]), sb("w1u", [HID, 1])
        w2_sb = sb("w2_sb", [HID, C])
        wl3_sb, wu_sb = sb("wl3_sb", [C, 2, C]), sb("wu_sb", [C, C])
        b3_sb, b1_sb, b1u, bl3_sb = sb("b3_sb", [HID, 1]), sb("b1_sb", [HID, 1]), sb("b1u", [HID, 1]), sb("bl3_sb", [C, 1])
        b4B, b2B, c0B = sb("b4B", [P, C]), sb("b2B", [P, C]), sb("c0B", [P, C])
        rat = sb("rat", [P, TERMS + 1])
        tB, uB, scale = sb("tB", [P, 1]), sb("uB", [HID, 1]), sb("scale", [P, 1])
        eps = sb("eps", [P, 1])
        one = sb("one", [P, 1])

        def brd(a, n, f=C):
            return a.unsqueeze(2).to_broadcast([P, n, f])

        def rows(a, n):
            return a.unsqueeze(1).to_broadcast([P, n, a.shape[-1]])

        def ln_centre(dve, link, X, s, xc, n):
            link(dve.tensor_reduce(out=s, in_=X, axis=AX.X, op=ALU.add))
            return dve.scalar_tensor_tensor(out=xc, in0=brd(s, n), scalar=-1.0 / C, in1=X, op0=ALU.mult, op1=ALU.add)

        def ln_square(act, xc, sq):
            return act.activation(sq, xc, ACT.Square)

        def ln_var(dve, sq, v):
            return dve.tensor_reduce(out=v, in_=sq, axis=AX.X, op=ALU.add)

        def ln_std(act, v, sd):
            return act.activation(sd, v, ACT.Sqrt, bias=eps[:, :], scale=1.0 / C)

        def ln_relu(dve, link, sd, rs, xc, h, n):
            link(dve.reciprocal(rs, sd))
            return dve.scalar_tensor_tensor(out=h, in0=xc, scalar=0.0, in1=brd(rs, n), op0=ALU.max, op1=ALU.mult)

        def fwd(pe, ps, X, f, last_sem):
            pe.sem_inc(pe_went_on, 1)
            for u in range(U):
                ins = pe.transpose(ps[0:f, u * P:(u + 1) * P], X[:, u, 0:f], ident[0:P, 0:P])
            ins.then_inc(last_sem, 1)

        def back(pe, ps, S, f, last_sem):
            pe.sem_inc(pe_went_on, 1)
            for u in range(U):
                ins = pe.transpose(ps[0:P, u * f:(u + 1) * f], S[0:f, u * P:(u + 1) * P], ident[0:f, 0:f])
            ins.then_inc(last_sem, 1)

        def prows(ps, f=C):
            return ps[0:P, 0:U * f].rearrange("p (u f) -> p u f", f=f)

        with ExitStack() as st:
            sb, sem, sems = alloc(st)
            attr_sb = sb("attr_sb", [P, T, PAYW])
            dnx_i = sb("dnx_i", [P, T], i32)
            key = [sb("srcF", [P, T]), sb("dstF", [P, T])]
            hi, lo = [sb(f"hi{k}", [P, T]) for k in range(2)], [sb(f"lo{k}", [P, T]) for k in range(2)]
            q_i, tmp, tmp2 = sb("q_i", [P, T], i32), sb("tmp", [P, T]), sb("tmp2", [P, T])
            pos_f, pos_i = sb("pos_f", [P, T]), sb("pos_i", [P, T], i32)
            gi_f = sb("gi_f", [P, T])
            khl = sb("khl", [P, T, 3])
            khl_t = [sb(f"khl_t{b}", [P, 3]) for b in range(2)]
            occ, pos_t = ([sb(f"{n}{b}", [P, 1]) for b in range(2)] for n in ("occ", "pos_t"))
            iota_i, iota_lo, iota_hi = sb("iota_i", [P, ND], i32), sb("iota_lo", [P, ND], f16), sb("iota_hi", [P, P], f16)
            tri, tri_lt = sb("tri", [P, P]), sb("tri_lt", [P, P])
            h0 = sb("h0", [HID, P])
            lo_hot = [[sb(f"lo_hot{k}{b}", [P, ND], f16) for b in range(2)] for k in range(2)]
            hi_hot = [[sb(f"hi_hot{k}{b}", [P, P], f16) for b in range(2)] for k in range(2)]
            place = sb("place", [P, ND])
            cnt, incl, ones = sb("cnt", [P, ND]), sb("incl", [P, ND]), sb("ones", [P, ND])
            dinv_n, endp_n = sb("dinv_n", [P, ND]), sb("endp_n", [P, ND])
            offs = sb("offs", [P, 1])
            zrow = sb("zrow", [2, C])
            hiT = [sb(f"hiT{b}", [P, P]) for b in range(2)]
            hd = [sb(f"hd{b}", [P, P]) for b in range(2)]
            h800 = sb("h800", [P, 1])
            eqj, eqk = ([sb(f"{n}{b}", [P, P]) for b in range(2)] for n in ("eqj", "eqk"))
            ttj = sb("ttj", [P, 2, HALF])
            node0 = sb("node0", [P, 1], i32)
            hist = [bank[0], bank[1], bank[2], bank[3]]

            loaded, built, stored = sem("loaded"), sem("built"), sem("stored")
            dlink = sem("dve_link")
            head_ready, c0_mm = sem("head_ready"), sem("c0_mm")
            hot_ready, hot_used, hist_done = sems("hot_ready"), sems("hot_used"), sem("hist_done")
            offs_in, offs_mm, place_ready = sem("offs_in"), sem("offs_mm"), sem("place_ready")
            place_mm = sem("place_mm")
            tabs_ready = sem("tabs_ready")
            LOADS = 27
            v3 = lambda t: t[:, :].rearrange("p (a c) -> p a c", a=2)
            with nc.Block() as block:
                @block.sync
                def _(sp):
                    col = lambda a: a.rearrange("(n o) -> n o", o=1)
                    for dst_sb, a in (
                            (src_i[:, :], tile_major(src_pad[1:E + 1])), (dst_i[:, :], tile_major(dst_pad[1:E + 1])),
                            (dnx_i[:, :], tile_major(dst_pad[2:E + 2])), (attr_sb[:, :, 3:4], w.rearrange("(t p o) -> p t o", p=P, o=1)),
                            (attr_sb[:, :, 4:PAYW], attr.rearrange("(t p) a -> p t a", p=P)),
                            (w3_sb[:, :], w3t), (w4_sb[:, :], w4t), (w2_sb[:, :], w2),
                            (w1_sb[:, :, :], w1[0:3 * ATTR, :].rearrange("(s a) h -> a s h", s=3)),
                            (w1u[:, :], w1[3 * ATTR:3 * ATTR + 1, :].rearrange("o h -> h o")),
                            (wl3_sb[:, :, :], wl3.rearrange("(s c) o -> c s o", s=2)),
                            (b3_sb[:, :], col(b3)), (b1_sb[:, :], col(b1)), (bl3_sb[:, :], col(bl3)),
                            (b4B[:, :], b4.partition_broadcast(P)), (b2B[:, :], b2.partition_broadcast(P)),
                            (rat[:, :], ratios.partition_broadcast(P)), (tB[:, :], t_in.partition_broadcast(P)),
                            (uB[:, :], u_in[0, :].partition_broadcast(HID))):
                        sp.dma_start(dst_sb, a).then_inc(loaded, 16)
                    sp.wait_ge(tabs_ready, 2)
                    sp.dma_start(dinv_tab.rearrange("(p c) o -> p (c o)", p=P), dinv_n[:, :]).then_inc(stored, 16)
                    sp.dma_start(endp_tab.rearrange("(p c) o -> p (c o)", p=P), endp_n[:, :]).then_inc(stored, 16)
                    for i in range(2):
                        sp.dma_start(terms[i][E:E + 1, :], zrow[0:1, :]).then_inc(stored, 16)
                    sp.wait_ge(stored, 64)

                NLOAD = 16 * 19

                @block.gpsimd
                def _(pool):
                    pool.memset(ident[:, :], 0.0).then_inc(built, 1)
                    pool.memset(tri[:, :], 1.0).then_inc(built, 1)
                    pool.memset(tri_lt[:, :], 1.0).then_inc(built, 1)
                    pool.iota(iota_i[:, :], pattern=[[1, ND]], base=0, channel_multiplier=0).then_inc(built, 1)
                    pool.iota(node0[:, :], pattern=[[1, 1]], base=0, channel_multiplier=ND).then_inc(built, 1)
                    pool.wait_ge(built, 5)
                    pool.affine_select(out=ident[:, :], in_=ident[:, :], compare_op=ALU.not_equal, fill=1.0, base=0,
                                       pattern=[[-1, 128]], channel_multiplier=1).then_inc(built, 1)
                    pool.affine_select(out=tri[:, :], in_=tri[:, :], compare_op=ALU.is_gt, fill=0.0, base=0,
                                       pattern=[[1, P]], channel_multiplier=-1).then_inc(built, 1)
                    pool.affine_select(out=tri_lt[:, :], in_=tri_lt[:, :], compare_op=ALU.is_gt, fill=0.0, base=0,
                                       pattern=[[-1, P]], channel_multiplier=1).then_inc(built, 1)

                @block.scalar
                def _(act):
                    act.wait_ge(hist_done, 1)
                    for a in range(2):
                        ins = act.activation(dinv_n[:, a * HALF:(a + 1) * HALF], hist[2 + a][0:P, 0:HALF], ACT.Sqrt, bias=one[:, :])
                    ins.then_inc(head_ready, 1)

                @block.tensor
                def _(pe):
                    pe.wait_ge(head_ready, 1)
                    pe.matmul(bank[4][0:P, 0:C], h0[:, :], w2_sb[:, :], start=True, stop=True).then_inc(c0_mm, 1)
                    z = None
                    with pe.Fori(0, T // 2 - 1) as j:
                        for b in range(2):
                            pe.wait_ge(hot_ready[b], j + 1)
                            for k in range(2):
                                for a in range(2):
                                    ins = pe.matmul(hist[2 * k + a][0:P, 0:HALF], hi_hot[k][b][:, :],
                                                    lo_hot[k][b][:, a * HALF:(a + 1) * HALF], start=False, stop=False,
                                                    skip_group_check=True)
                            ins.then_inc(hot_used[b], 1)
                    for b in range(2):
                        pe.wait_ge(hot_ready[b], T // 2)
                        for k in range(2):
                            for a in range(2):
                                ins = pe.matmul(hist[2 * k + a][0:P, 0:HALF], hi_hot[k][b][:, :],
                                                lo_hot[k][b][:, a * HALF:(a + 1) * HALF], start=False, stop=b == 1,
                                                skip_group_check=True)
                        if b == 0:
                            ins.then_inc(hot_used[b], 1)
                    ins.then_inc(hist_done, 1)
                    pe.wait_ge(offs_in, 1)
                    pe.matmul(bank[4][0:P, 128:129], tri[:, :], incl[:, ND - 1:ND], start=True, stop=True).then_inc(offs_mm, 1)

                @block.vector
                def _(dve):
                    ch = Chain(dve, dlink)
                    link = ch.link
                    for k in range(4):
                        link(dve.memset(hist[k][:, :], 0.0))
                    dve.memset(eps[:, :], EPS)
                    dve.memset(one[:, :], 1.0)
                    dve.memset(ones[:, :], 1.0)
                    link(dve.memset(zrow[:, :], 0.0))
                    dve.wait_ge(loaded, NLOAD)
                    dve.wait_ge(built, 8)
                    dve.tensor_copy(iota_lo[:, :], iota_i[:, :])
                    dve.tensor_copy(iota_hi[:, :], iota_i[:, 0:P])
                    link(dve.tensor_copy(h800[:, :], node0[:, :]))
                    dve.tensor_tensor(out=wu_sb[:, :], in0=wl3_sb[:, 0, :], in1=wl3_sb[:, 1, :], op=ALU.subtract)
                    dve.tensor_scalar(scale[:, :], tB[:, :], 1e-8, -1.0 / N_SUB, ALU.max, ALU.mult)
                    link(dve.scalar_tensor_tensor(out=b1u[:, :], in0=w1u[:, :], scalar=uB[:, 0:1], in1=b1_sb[:, :],
                                                  op0=ALU.mult, op1=ALU.add))
                    dve.tensor_scalar(h0[:, :], b1u[:, 0:1].to_broadcast([HID, P]), 0.0, None, ALU.max).then_inc(head_ready, 1)
                    for k, key_i in enumerate((src_i, dst_i)):
                        link(dve.tensor_copy(key[k][:, :], key_i[:, :]))
                        link(dve.tensor_scalar(q_i[:, :], key[k][:, :], 1.0 / ND, None, ALU.mult))
                        link(dve.tensor_copy(hi[k][:, :], q_i[:, :]))
                        link(dve.scalar_tensor_tensor(out=lo[k][:, :], in0=hi[k][:, :], scalar=-float(ND), in1=key[k][:, :],
                                                      op0=ALU.mult, op1=ALU.add))
                        link(dve.tensor_scalar(tmp[:, :], lo[k][:, :], 0.0, None, ALU.is_lt))
                        link(dve.tensor_tensor(out=hi[k][:, :], in0=hi[k][:, :], in1=tmp[:, :], op=ALU.subtract))
                        link(dve.scalar_tensor_tensor(out=lo[k][:, :], in0=hi[k][:, :], scalar=-float(ND), in1=key[k][:, :],
                                                      op0=ALU.mult, op1=ALU.add))
                        link(dve.tensor_scalar(tmp[:, :], lo[k][:, :], float(ND), None, ALU.is_ge))
                        link(dve.tensor_tensor(out=hi[k][:, :], in0=hi[k][:, :], in1=tmp[:, :], op=ALU.add))
                        link(dve.scalar_tensor_tensor(out=lo[k][:, :], in0=hi[k][:, :], scalar=-float(ND), in1=key[k][:, :],
                                                      op0=ALU.mult, op1=ALU.add))
                    for i, a in enumerate((key[0], hi[0], lo[0])):
                        dve.tensor_copy(khl[:, :, i], a[:, :])
                    link(dve.tensor_tensor(out=tmp[:, :], in0=dst_i[:, :], in1=dnx_i[:, :], op=ALU.not_equal))
                    link(dve.scalar_tensor_tensor(out=tmp2[:, :], in0=key[1][:, :], scalar=-float(N), in1=tmp[:, :],
                                                  op0=ALU.add, op1=ALU.mult))
                    link(dve.tensor_scalar(dst_end[:, :], tmp2[:, :], float(N), None, ALU.add))
                    dve.memset(attr_sb[:, :, 2], 0.0)
                    dve.tensor_copy(attr_sb[:, :, 0], key[0][:, :])
                    dve.tensor_copy(attr_sb[:, :, 1], key[1][:, :])
                    link(dve.tensor_scalar(attr_sb[:, :, 3], attr_sb[:, :, 3], scale[:, 0:1], None, ALU.mult))
                    dve.wait_ge(c0_mm, 1)
                    link(dve.tensor_tensor(out=c0B[:, :], in0=bank[4][0:P, 0:C], in1=b2B[:, :], op=ALU.add))
                    with dve.Fori(0, T // 2) as j:
                        for b in range(2):
                            t = j * 2 + b
                            dve.wait_ge(hot_used[b], j)
                            for k in range(2):
                                dve.tensor_scalar(hi_hot[k][b][:, :], iota_hi[:, :], hi[k][:, bass.ds(t, 1)], None, ALU.is_equal)
                                ins = dve.tensor_scalar(lo_hot[k][b][:, :], iota_lo[:, :], lo[k][:, bass.ds(t, 1)], None, ALU.is_equal)
                            ins.then_inc(hot_ready[b], 1)
                    dve.wait_ge(hist_done, 1)
                    for a in range(2):
                        ins = dve.tensor_copy(cnt[:, a * HALF:(a + 1) * HALF], hist[a][0:P, 0:HALF])
                    link(ins)
                    dve.tensor_tensor_scan(incl[:, :], ones[:, :], cnt[:, :], 0.0, ALU.mult, ALU.add).then_inc(offs_in, 1)
                    dve.wait_ge(offs_mm, 1)
                    link(dve.tensor_copy(offs[:, :], bank[4][0:P, 128:129]))
                    link(dve.tensor_scalar(endp_n[:, :], incl[:, :], offs[:, 0:1], None, ALU.add))
                    link(dve.tensor_tensor(out=place[:, :], in0=endp_n[:, :], in1=cnt[:, :], op=ALU.subtract))
                    link(dve.tensor_scalar(cnt[:, :], cnt[:, :], 0.0, None, ALU.is_gt))
                    link(dve.scalar_tensor_tensor(out=endp_n[:, :], in0=endp_n[:, :], scalar=-float(E + 1), in1=cnt[:, :],
                                                  op0=ALU.add, op1=ALU.mult))
                    dve.tensor_scalar(endp_n[:, :], endp_n[:, :], float(E), None, ALU.add).then_inc(tabs_ready, 1)
                    dve.wait_ge(head_ready, 2)
                    dve.reciprocal(dinv_n[:, :], dinv_n[:, :]).then_inc(tabs_ready, 1)

            with ExitStack() as s2:
                sb, sem, sems = alloc(s2)
                src_b = [sb(f"src_b{b}", [P, P], i32) for b in range(2)]
                src_bf = [sb(f"src_bf{b}", [P, P]) for b in range(2)]
                src_loaded, src_free = sems("src_loaded"), sems("src_free")
                hots_ready, sel_done, pos_done = sems("hots_ready"), sems("sel_done"), sem("pos_done")
                place_copied, place_added = sem("place_copied"), sem("place_added")
                dl = sem("place_link")
                run, sel = two[0], [two[1], two[2]]
                with nc.Block() as block:
                    @block.sync
                    def _(sp):
                        with sp.Fori(0, T // 2) as j:
                            for b in range(2):
                                sp.wait_ge(src_free[b], j)
                                sp.dma_start(src_b[b][:, :], src_pad[bass.ds((j * 2 + b) * P + 1, P)].partition_broadcast(P))\
                                  .then_inc(src_loaded[b], 16)

                    @block.tensor
                    def _(pe):
                        for a in range(2):
                            ins = pe.matmul(run[0:P, a, 0:HALF], ident[0:P, 0:P], place[:, a * HALF:(a + 1) * HALF],
                                            start=True, stop=False, skip_group_check=True)
                        ins.then_inc(place_added, 1)
                        with pe.Fori(0, T // 2) as j:
                            for b in range(2):
                                pe.wait_ge(hots_ready[b], j + 1)
                                pe.wait_ge(place_copied, j * 2 + b + 1)
                                for a in range(2):
                                    ins = pe.matmul(sel[b][0:P, a, 0:HALF], hiT[b][:, :], place[:, a * HALF:(a + 1) * HALF],
                                                    start=True, stop=True)
                                ins.then_inc(sel_done[b], 1)
                                for a in range(2):
                                    ins = pe.matmul(run[0:P, a, 0:HALF], hi_hot[0][b][:, :], lo_hot[0][b][:, a * HALF:(a + 1) * HALF],
                                                    start=False, stop=False, skip_group_check=True)
                                ins.then_inc(place_added, 1)

                    @block.scalar
                    def _(act):
                        with act.Fori(0, T // 2) as j:
                            for b in range(2):
                                act.wait_ge(place_added, j * 2 + b + 1)
                                act.activation(place[:, :].rearrange("p (a c) -> p a c", a=2), run[0:P, :, 0:HALF], ACT.Copy)\
                                   .then_inc(place_copied, 1)

                    @block.vector
                    def _(dve):
                        def one_hots(link, b, t, j):
                            dve.wait_ge(src_loaded[b], j * 16 + 16)
                            dve.tensor_copy(src_bf[b][:, :], src_b[b][:, :])
                            link(dve.tensor_copy(khl_t[b][:, :], khl[:, bass.ds(t, 1), :]))
                            link(dve.tensor_scalar(hd[b][:, :], src_bf[b][:, :], h800[:, 0:1], None, ALU.subtract))
                            link(dve.tensor_scalar(eqj[b][:, :], hd[b][:, :], float(ND), None, ALU.is_lt))
                            dve.scalar_tensor_tensor(out=hiT[b][:, :], in0=hd[b][:, :], scalar=0.0, in1=eqj[b][:, :],
                                                     op0=ALU.is_ge, op1=ALU.mult).then_inc(src_free[b], 1)
                            dve.tensor_scalar(hi_hot[0][b][:, :], iota_hi[:, :], khl_t[b][:, 1:2], None, ALU.is_equal)
                            dve.tensor_scalar(lo_hot[0][b][:, :], iota_lo[:, :], khl_t[b][:, 2:3], None, ALU.is_equal)\
                               .then_inc(hots_ready[b], 1)
                            link(dve.scalar_tensor_tensor(out=eqk[b][:, :], in0=src_bf[b][:, :], scalar=khl_t[b][:, 0:1],
                                                          in1=tri_lt[:, :], op0=ALU.is_equal, op1=ALU.mult,
                                                          accum_out=occ[b][:, :]))

                        def places(link, b, t, j):
                            dve.wait_ge(sel_done[b], j + 1)
                            link(dve.tensor_tensor_reduce(out=ttj[:, :, :], in0=v3(lo_hot[0][b]), in1=sel[b][0:P, :, 0:HALF],
                                                          scale=1.0, scalar=occ[b][:, 0:1], op0=ALU.mult, op1=ALU.add,
                                                          accum_out=pos_t[b][:, :]))
                            dve.tensor_copy(pos_f[:, bass.ds(t, 1)], pos_t[b][:, :]).then_inc(pos_done, 1)

                        LAST = T // 2 - 1
                        ch = Chain(dve, dl)
                        one_hots(ch.link, 0, 0, 0)
                        n0 = ch.n
                        KB = n0 + 1
                        with dve.Fori(0, LAST) as j:
                            ch = Chain(dve, dl, j * (2 * KB) + n0)
                            dve.wait_ge(place_added, j * 2 + 1)
                            one_hots(ch.link, 1, j * 2 + 1, j)
                            places(ch.link, 0, j * 2, j)
                            dve.wait_ge(place_added, j * 2 + 2)
                            one_hots(ch.link, 0, j * 2 + 2, j + 1)
                            places(ch.link, 1, j * 2 + 1, j)
                            assert ch.n == 2 * KB
                        ch = Chain(dve, dl, LAST * 2 * KB + n0)
                        dve.wait_ge(place_added, T - 1)
                        one_hots(ch.link, 1, T - 1, LAST)
                        places(ch.link, 0, T - 2, LAST)
                        places(ch.link, 1, T - 1, LAST)
                        dve.wait_ge(pos_done, T)
                        ch.link(dve.tensor_copy(pos_i[:, :], pos_f[:, :]))

            with ExitStack() as s2:
                sb, sem, sems = alloc(s2)
                ixd = [sb(f"ixd{b}", [P, U], i32) for b in range(2)]
                ixp = [sb(f"ixp{b}", [P, U], i32) for b in range(2)]
                gv = [sb(f"gv{b}", [P, U]) for b in range(2)]
                rec = [sb(f"rec{b}", [P, U * PAYW]) for b in range(2)]
                sentinel = sb("sentinel", [1, 2])
                ix_ready, got, rec_ready, sent = sems("ix_ready"), sems("got"), sems("rec_ready"), sems("sent")
                begun, pads, rlink = sem("begun"), sem("pads"), sem("record_link")
                with nc.Block() as block:
                    @block.sync
                    def _(sp):
                        sp.wait_ge(begun, 2)
                        sp.dma_start(srcs_pad[0:1].rearrange("(o n) -> o n", o=1), sentinel[0:1, 0:1]).then_inc(pads, 16)
                        sp.dma_start(srcs_pad[E + 1:E + 2].rearrange("(o n) -> o n", o=1), sentinel[0:1, 1:2]).then_inc(pads, 16)
                        sp.wait_ge(pads, 32)

                    @block.gpsimd
                    def _(pool):
                        pool.memset(sentinel[:, :], -1.0).then_inc(begun, 1)
                        pool.sem_inc(begun, 1)
                        def gather(b, j):
                            pool.wait_ge(ix_ready[b], j + 1)
                            pool.sem_inc(pool_went_on, 1)
                            for u in range(U):
                                pool.indirect_dma_start(out=gv[b][:, u:u + 1], out_offset=None, in_=endp_tab,
                                                        in_offset=bass.IndirectOffsetOnAxis(ap=ixd[b][:, u:u + 1], axis=0))\
                                    .then_inc(got[b], 16)
                        def scatter(b, j):
                            pool.wait_ge(rec_ready[b], j + 1)
                            pool.sem_inc(pool_went_on, 1)
                            for u in range(U):
                                pool.indirect_dma_start(out=pay, out_offset=bass.IndirectOffsetOnAxis(ap=ixp[b][:, u:u + 1], axis=0),
                                                        in_=rec[b][:, u * PAYW:(u + 1) * PAYW], in_offset=None)\
                                    .then_inc(sent[b], 16)
                        with pool.Fori(0, PAIRS) as j:
                            gather(0, j)
                            gather(1, j)
                            scatter(0, j)
                            scatter(1, j)
                        for b in range(2):
                            pool.wait_ge(sent[b], 16 * U * PAIRS)

                    @block.scalar
                    def _(act):
                        with act.Fori(0, PAIRS) as j:
                            for b in range(2):
                                c = j * 2 + b
                                act.wait_ge(sent[b], j * 16 * U)
                                act.activation(ixp[b][:, :], pos_i[:, bass.ds(c * U, U)], ACT.Copy)
                                act.activation(ixd[b][:, :], dst_i[:, bass.ds(c * U, U)], ACT.Copy).then_inc(ix_ready[b], 1)

                    @block.vector
                    def _(dve):
                        with dve.Fori(0, PAIRS) as j:
                            for b in range(2):
                                c = j * 2 + b
                                dve.wait_ge(ix_ready[b], j + 1)
                                r3 = rec[b][:, :].rearrange("p (u k) -> p u k", u=U)
                                dve.tensor_copy(r3[:, :, :], attr_sb[:, bass.ds(c * U, U), :]).then_inc(rlink, 1)
                                dve.wait_ge(rlink, j * 2 + b + 1)
                                dve.wait_ge(got[b], j * 16 * U + 16 * U)
                                dve.tensor_copy(r3[:, :, 2], gv[b][:, :]).then_inc(rec_ready[b], 1)


        def gather(pool, rows_sb, f, table, ix, sem_):
            for u in range(U):
                pool.indirect_dma_start(out=rows_sb[:, u * f:(u + 1) * f], out_offset=None, in_=table,
                                        in_offset=bass.IndirectOffsetOnAxis(ap=ix[:, u:u + 1], axis=0)).then_inc(sem_, 16)

        def scatter(pool, table, ix, rows_sb, f, sem_):
            for u in range(U):
                pool.indirect_dma_start(out=table, out_offset=bass.IndirectOffsetOnAxis(ap=ix[:, u:u + 1], axis=0),
                                        in_=rows_sb[:, u * f:(u + 1) * f], in_offset=None,
                                        bounds_check=N - 1, oob_is_err=False).then_inc(sem_, 16)

        def pair_of_scans(b, j, s_r):
            return (s_r[1], j) if b == 0 else (s_r[0], j + 1)

        r3 = lambda a, n=U: a[:, :].rearrange("p (u f) -> p u f", u=n)

        with ExitStack() as st:
            sb, sem, sems = alloc(st)
            cur = [[sb(f"cur{k}{b}", [C + 1, CE], dt) for b in range(2)] for k, dt in enumerate((i32, f32))]
            prv = [[sb(f"prv{k}{b}", [C + 1, CE], dt) for b in range(2)] for k, dt in enumerate((i32, f32))]
            recs, nxt = sb("recs", [P, T, 4]), sb("nxt", [P, T])
            tmp, tmp2 = sb("tmp_m", [P, T]), sb("tmp_m2", [P, T])
            keys_in, keys_used, recs_in, stored, dl = sems("keys_in"), sems("keys_used"), sem("recs_in"), sem("srcs_stored"), sem("mask_link")
            with nc.Block() as block:
                @block.sync
                def _(sp):
                    sp.dma_start(recs[:, :, :], pay[:, 0:4].rearrange("(t p) a -> p t a", p=P)).then_inc(recs_in, 16)
                    sp.wait_ge(recs_in, 16)
                    sp.dma_start(tile_major(srcs_pad[1:E + 1]), recs[:, :, 0]).then_inc(stored, 16)
                    sp.wait_ge(stored, 16)
                    sp.dma_start(nxt[:, :], tile_major(srcs_pad[2:E + 2])).then_inc(recs_in, 16)
                    with sp.Fori(0, PAIRS) as j:
                        for b in range(2):
                            c = j * 2 + b
                            sp.wait_ge(keys_used[b], j)
                            for k, a in enumerate((dst_pad, srcs_pad)):
                                sp.dma_start(cur[k][b][:, :], a[bass.ds(c * CE + 1, CE)].partition_broadcast(C + 1)).then_inc(keys_in[b], 16)
                                sp.dma_start(prv[k][b][:, :], a[bass.ds(c * CE, CE)].partition_broadcast(C + 1)).then_inc(keys_in[b], 16)

                @block.vector
                def _(dve):
                    with dve.Fori(0, PAIRS) as j:
                        for b in range(2):
                            c = j * 2 + b
                            dve.wait_ge(keys_in[b], j * 64 + 64)
                            for k, m in enumerate((mask_d, mask_s)):
                                ins = dve.tensor_tensor(out=m[:, bass.ds(c * CE, CE)], in0=cur[k][b][:, :], in1=prv[k][b][:, :], op=ALU.is_equal)
                            ins.then_inc(keys_used[b], 1)
                    dve.wait_ge(recs_in, 32)
                    ch = Chain(dve, dl)
                    dve.tensor_copy(srcS_i[:, :], recs[:, :, 0])
                    dve.tensor_copy(dstS_i[:, :], recs[:, :, 1])
                    dve.tensor_copy(gi_i[:, :], recs[:, :, 2])
                    dve.tensor_copy(w_s[:, :], recs[:, :, 3])
                    ch.link(dve.tensor_tensor(out=tmp[:, :], in0=recs[:, :, 0], in1=nxt[:, :], op=ALU.not_equal))
                    ch.link(dve.scalar_tensor_tensor(out=tmp2[:, :], in0=recs[:, :, 0], scalar=-float(N), in1=tmp[:, :],
                                                     op0=ALU.add, op1=ALU.mult))
                    ch.link(dve.tensor_scalar(srcS_end[:, :], tmp2[:, :], float(N), None, ALU.add))

        GN = ND // U
        by_node = lambda a: a.rearrange("(p c) f -> p c f", p=P)
        with ExitStack() as st:
            sb, sem, sems = alloc(st)
            X, XO, Q, O, H, SQ, XC = ([sb(f"dn_{n}{b}", [P, U * C]) for b in range(2)] for n in ("x", "x1", "q", "o", "h", "sq", "xc"))
            s_, v_, sd_, rs_ = ([sb(f"dn_{n}{b}", [P, U]) for b in range(2)] for n in ("sum", "var", "std", "rstd"))
            HT, Z = [sb(f"dn_hT{b}", [C, CE]) for b in range(2)], [sb(f"dn_z{b}", [HID, CE]) for b in range(2)]
            x_in, x_used = sems("x_in"), sems("x_used")
            centred, squared, var_r, std_r, h_r = sems("centred"), sems("squared"), sems("var_r"), sems("std_r"), sems("h_r")
            hT_mm, hT_r, z_mm, z_r, q_mm = sems("hT_mm"), sems("hT_r"), sems("z_mm"), sems("z_r"), sems("q_mm")
            q_r, x1_r, o_r = sems("q_r"), sems("x1_r"), sems("o_r")
            centred2, squared2, var2, std2 = sems("centred2"), sems("squared2"), sems("var2"), sems("std2")
            stored = sems("rows_stored")
            dl = sem("dense_link")
            L = GN // 2
            with nc.Block() as block:
                @block.sync
                def _(sp):
                    with sp.Fori(0, L) as j:
                        for b in range(2):
                            g = j * 2 + b
                            sp.wait_ge(x_used[b], j)
                            sp.dma_start(r3(X[b]), by_node(x)[:, bass.ds(g * U, U), :]).then_inc(x_in[b], 16)
                        for b in range(2):
                            g = j * 2 + b
                            sp.wait_ge(x1_r[b], j + 1)
                            sp.dma_start(by_node(qs)[:, bass.ds(g * U, U), :], r3(Q[b])).then_inc(stored[b], 16)
                            sp.dma_start(by_node(x1)[:, bass.ds(g * U, U), :], r3(XO[b])).then_inc(stored[b], 16)
                            sp.wait_ge(o_r[b], j + 1)
                            sp.dma_start(by_node(out)[:, bass.ds(g * U, U), :], r3(O[b])).then_inc(stored[b], 16)
                    for b in range(2):
                        sp.wait_ge(stored[b], 48 * L)

                @block.vector
                def _(dve):
                    K = 2 * 6
                    with dve.Fori(0, L) as j:
                        ch = Chain(dve, dl, j * K)
                        for b in range(2):
                            dve.wait_ge(x_in[b], j * 16 + 16)
                            ln_centre(dve, ch.link, r3(X[b]), s_[b][:, :], r3(XC[b]), U).then_inc(centred[b], 1)
                        for b in range(2):
                            dve.wait_ge(squared[b], j + 1)
                            ln_var(dve, r3(SQ[b]), v_[b][:, :]).then_inc(var_r[b], 1)
                        for b in range(2):
                            dve.wait_ge(std_r[b], j + 1)
                            ln_relu(dve, ch.link, sd_[b][:, :], rs_[b][:, :], r3(XC[b]), r3(H[b]), U).then_inc(h_r[b], 1)
                        for b in range(2):
                            dve.wait_ge(q_mm[b], j + 1)
                            dve.wait_ge(stored[b], j * 48)
                            dve.tensor_copy(Q[b][:, :], bank[3 + 4 * b][0:P, 0:U * C]).then_inc(q_r[b], 1)
                            dve.tensor_tensor(out=r3(XO[b]), in0=r3(X[b]), in1=rows(b4B[:, :], U), op=ALU.add).then_inc(x_used[b], 1)
                            dve.wait_ge(x_used[b], j + 1)
                            dve.tensor_tensor(out=XO[b][:, :], in0=XO[b][:, :], in1=bank[3 + 4 * b][0:P, 0:U * C], op=ALU.add).then_inc(x1_r[b], 1)
                            dve.wait_ge(x1_r[b], j + 1)
                            ln_centre(dve, ch.link, r3(XO[b]), s_[b][:, :], r3(XC[b]), U).then_inc(centred2[b], 1)
                        for b in range(2):
                            dve.wait_ge(squared2[b], j + 1)
                            ln_var(dve, r3(SQ[b]), v_[b][:, :]).then_inc(var2[b], 1)
                        for b in range(2):
                            dve.wait_ge(std2[b], j + 1)
                            ch.link(dve.reciprocal(rs_[b][:, :], sd_[b][:, :]))
                            ch.link(dve.scalar_tensor_tensor(out=r3(H[b]), in0=r3(XC[b]), scalar=0.0, in1=brd(rs_[b][:, :], U), op0=ALU.max, op1=ALU.mult))
                            ch.link(dve.tensor_tensor(out=H[b][:, :], in0=H[b][:, :], in1=XO[b][:, :], op=ALU.add))
                            dve.tensor_tensor(out=r3(O[b]), in0=r3(H[b]), in1=rows(c0B[:, :], U), op=ALU.add).then_inc(o_r[b], 1)
                        assert ch.n == K, ch.n

                @block.scalar
                def _(act):
                    with act.Fori(0, L) as j:
                        for b in range(2):
                            act.wait_ge(centred[b], j + 1)
                            ln_square(act, XC[b][:, :], SQ[b][:, :]).then_inc(squared[b], 1)
                        for b in range(2):
                            act.wait_ge(var_r[b], j + 1)
                            ln_std(act, v_[b][:, :], sd_[b][:, :]).then_inc(std_r[b], 1)
                        for b in range(2):
                            act.wait_ge(hT_mm[b], j + 1)
                            act.activation(HT[b][:, :], bank[1 + 4 * b][0:C, 0:CE], ACT.Copy).then_inc(hT_r[b], 1)
                        for b in range(2):
                            act.wait_ge(z_mm[b], j + 1)
                            act.activation(Z[b][:, :], bank[2 + 4 * b][0:HID, 0:CE], ACT.Relu, bias=b3_sb[:, :]).then_inc(z_r[b], 1)
                        for b in range(2):
                            act.wait_ge(centred2[b], j + 1)
                            ln_square(act, XC[b][:, :], SQ[b][:, :]).then_inc(squared2[b], 1)
                        for b in range(2):
                            act.wait_ge(var2[b], j + 1)
                            ln_std(act, v_[b][:, :], sd_[b][:, :]).then_inc(std2[b], 1)

                @block.tensor
                def _(pe):
                    with pe.Fori(0, L) as j:
                        for b in range(2):
                            pe.wait_ge(h_r[b], j + 1)
                            fwd(pe, bank[1 + 4 * b], r3(H[b]), C, hT_mm[b])
                        for b in range(2):
                            pe.wait_ge(hT_r[b], j + 1)
                            pe.matmul(bank[2 + 4 * b][0:HID, 0:CE], w3_sb[:, :], HT[b][:, :], start=True, stop=True).then_inc(z_mm[b], 1)
                        for b in range(2):
                            pe.wait_ge(z_r[b], j + 1)
                            for u in range(U):
                                ins = pe.matmul(bank[3 + 4 * b][0:P, u * C:(u + 1) * C], Z[b][:, u * P:(u + 1) * P], w4_sb[:, :], start=True, stop=True)
                            ins.then_inc(q_mm[b], 1)

        with ExitStack() as st:
            sb, sem, sems = alloc(st)
            XD, QSD = sb("x_dst", [P, T, C]), sb("qs_dst", [P, T, C])
            with ExitStack() as s2:
                sb, sem, sems = alloc(s2)
                F1 = C + 1
                G, XC, SQ, H = ([sb(f"c1_{n}{b}", [P, 2 * U * C]) for b in range(2)] for n in ("g", "xc", "sq", "h"))
                s_, v_, sd_, rs_ = ([sb(f"c1_{n}{b}", [P, 2 * U]) for b in range(2)] for n in ("sum", "var", "std", "rstd"))
                dv, M = [sb(f"c1_dv{b}", [P, U]) for b in range(2)], [sb(f"c1_m{b}", [P, U * F1]) for b in range(2)]
                S, AT, Z = [sb(f"c1_s{b}", [F1, CE]) for b in range(2)], [sb(f"c1_aT{b}", [C, CE]) for b in range(2)], [sb(f"c1_z{b}", [HID, CE]) for b in range(2)]
                A, QO = [sb(f"c1_a{b}", [P, U * C]) for b in range(2)], [sb(f"c1_q{b}", [P, U * C]) for b in range(2)]
                dd, dq = [sb(f"c1_dd{b}", [P, U]) for b in range(2)], [sb(f"c1_dq{b}", [P, U]) for b in range(2)]
                ixs, ixd, ixe = ([sb(f"c1_{n}{b}", [P, U], i32) for b in range(2)] for n in ("ixs", "ixd", "ixe"))
                ix_r, got, centred, squared, var_r, std_r, m_r = (sems(f"c1_{n}") for n in ("ix_ready", "gathered", "centred", "squared", "var", "std", "messages"))
                mT, s_r, s_back, cnt_r, a_r, aT_mm, aT_r, z_mm, z_r, q_mm, q_r, sent = (sems(f"c1_{n}") for n in (
                    "mT", "scanned", "sums_back", "count", "agg", "aT_mm", "aT", "z_mm", "z", "q_mm", "q", "sent"))
                ixe_r, x_kept = sems("c1_ixe"), sems("c1_x_kept")
                dl, m1 = sem("c1_link"), sem("c1_ones")
                with nc.Block() as block:
                    @block.gpsimd
                    def _(pool):
                        def gathers(b, j):
                            pool.wait_ge(ix_r[b], j + 1)
                            pool.wait_ge(m_r[b], j)
                            pool.wait_ge(x_kept[b], j)
                            pool.sem_inc(pool_went_on, 1)
                            gather(pool, G[b], C, x, ixs[b], got[b])
                            gather(pool, G[b][:, U * C:], C, x, ixd[b], got[b])
                            gather(pool, dv[b], 1, dinv_tab, ixs[b], got[b])
                        def scatters(b, j):
                            pool.wait_ge(q_r[b], j * 2 + 1)
                            pool.wait_ge(ixe_r[b], j + 1)
                            pool.sem_inc(pool_went_on, 1)
                            scatter(pool, qs, ixe[b], QO[b], C, sent[b])
                        with pool.Fori(0, PAIRS) as j:
                            gathers(0, j)
                            gathers(1, j)
                            scatters(0, j)
                            scatters(1, j)
                        for b in range(2):
                            pool.wait_ge(sent[b], 16 * U * PAIRS)

                    @block.vector
                    def _(dve):
                        for b in range(2):
                            dve.memset(M[b][:, :], 1.0)
                            ins = dve.memset(S[b][:, :], 0.0)
                        ins.then_inc(m1, 1)
                        dve.wait_ge(m1, 1)
                        K = 2 * 5
                        with dve.Fori(0, PAIRS) as j:
                            ch = Chain(dve, dl, j * K)
                            for b in range(2):
                                dve.wait_ge(got[b], j * (48 * U) + 48 * U)
                                ln_centre(dve, ch.link, r3(G[b], 2 * U), s_[b][:, :], r3(XC[b], 2 * U), 2 * U).then_inc(centred[b], 1)
                                dve.wait_ge(squared[b], j + 1)
                                ln_var(dve, r3(SQ[b], 2 * U), v_[b][:, :]).then_inc(var_r[b], 1)
                                dve.wait_ge(std_r[b], j + 1)
                                ch.link(ln_relu(dve, ch.link, sd_[b][:, :], rs_[b][:, :], r3(XC[b], 2 * U), r3(H[b], 2 * U), 2 * U))
                                dve.tensor_tensor(out=r3(M[b])[:, :, 0:C], in0=r3(H[b], 2 * U)[:, 0:U, :], in1=brd(dv[b][:, :], U), op=ALU.mult)\
                                   .then_inc(m_r[b], 1)
                                dve.wait_ge(mT[b], j + 1)
                                dve.wait_ge(*pair_of_scans(b, j, s_r))
                                dve.tensor_tensor_scan(S[b][:, :], mask_d[:, bass.ds((j * 2 + b) * CE, CE)], bank[4 * b][0:F1, 0:CE],
                                                       S[1 - b][:, CE - 1:CE], ALU.mult, ALU.add).then_inc(s_r[b], 1)
                                dve.wait_ge(cnt_r[b], j + 1)
                                ch.link(dve.reciprocal(dd[b][:, :], dq[b][:, :]))
                                dve.tensor_copy(dinv_d[:, bass.ds((j * 2 + b) * U, U)], dd[b][:, :])
                                ch.link(dve.tensor_tensor(out=r3(A[b]), in0=r3(H[b], 2 * U)[:, U:2 * U, :], in1=brd(dd[b][:, :], U), op=ALU.mult))
                                dve.tensor_tensor(out=r3(A[b]), in0=r3(A[b]), in1=prows(bank[4 * b + 1], F1)[:, :, 0:C], op=ALU.add).then_inc(a_r[b], 1)
                                dve.wait_ge(a_r[b], j * 2 + 1)
                                dve.tensor_tensor(out=r3(A[b]), in0=r3(A[b]), in1=brd(dd[b][:, :], U), op=ALU.mult).then_inc(a_r[b], 1)
                                dve.wait_ge(q_mm[b], j + 1)
                                dve.wait_ge(sent[b], j * (16 * U))
                                dve.tensor_tensor(out=r3(QO[b]), in0=prows(bank[4 * b + 3]), in1=brd(dd[b][:, :], U), op=ALU.mult).then_inc(q_r[b], 1)
                                dve.wait_ge(q_r[b], j * 2 + 1)
                                dve.tensor_copy(QSD[:, bass.ds((j * 2 + b) * U, U), :], r3(QO[b])).then_inc(q_r[b], 1)
                            assert ch.n == K, ch.n

                    @block.scalar
                    def _(act):
                        with act.Fori(0, PAIRS) as j:
                            for b in range(2):
                                c = j * 2 + b
                                if b == 0:
                                    for i in range(2):
                                        act.wait_ge(got[i], j * (48 * U))
                                        act.activation(ixs[i][:, :], src_i[:, bass.ds((j * 2 + i) * U, U)], ACT.Copy)
                                        act.activation(ixd[i][:, :], dst_i[:, bass.ds((j * 2 + i) * U, U)], ACT.Copy).then_inc(ix_r[i], 1)
                                act.wait_ge(sent[b], j * (16 * U))
                                act.activation(ixe[b][:, :], dst_end[:, bass.ds(c * U, U)], ACT.Copy).then_inc(ixe_r[b], 1)
                                act.wait_ge(centred[b], j + 1)
                                ln_square(act, XC[b][:, :], SQ[b][:, :]).then_inc(squared[b], 1)
                                act.activation(XD[:, bass.ds(c * U, U), :], r3(G[b], 2 * U)[:, U:2 * U, :], ACT.Copy).then_inc(x_kept[b], 1)
                                act.wait_ge(var_r[b], j + 1)
                                ln_std(act, v_[b][:, :], sd_[b][:, :]).then_inc(std_r[b], 1)
                                act.wait_ge(s_back[b], j + 1)
                                act.activation(dq[b][:, :], prows(bank[4 * b + 1], F1)[:, :, C], ACT.Sqrt, bias=one[:, :]).then_inc(cnt_r[b], 1)
                                act.wait_ge(aT_mm[b], j + 1)
                                act.activation(AT[b][:, :], bank[4 * b + 2][0:C, 0:CE], ACT.Copy).then_inc(aT_r[b], 1)
                                act.wait_ge(z_mm[b], j + 1)
                                act.activation(Z[b][:, :], bank[4 * b + 3][0:HID, 0:CE], ACT.Relu, bias=b3_sb[:, :]).then_inc(z_r[b], 1)

                    @block.tensor
                    def _(pe):
                        with pe.Fori(0, PAIRS) as j:
                            for b in range(2):
                                pe.wait_ge(m_r[b], j + 1)
                                pe.wait_ge(q_r[b], j * 2)
                                fwd(pe, bank[4 * b], r3(M[b]), F1, mT[b])
                                pe.wait_ge(s_r[b], j + 1)
                                back(pe, bank[4 * b + 1], S[b], F1, s_back[b])
                                pe.wait_ge(a_r[b], j * 2 + 2)
                                fwd(pe, bank[4 * b + 2], r3(A[b]), C, aT_mm[b])
                                pe.wait_ge(aT_r[b], j + 1)
                                pe.matmul(bank[4 * b + 3][0:HID, 0:CE], w3_sb[:, :], AT[b][:, :], start=True, stop=True).then_inc(z_mm[b], 1)
                                pe.wait_ge(z_r[b], j + 1)
                                for u in range(U):
                                    ins = pe.matmul(bank[4 * b + 3][0:P, u * C:(u + 1) * C], Z[b][:, u * P:(u + 1) * P], w4_sb[:, :], start=True, stop=True)
                                ins.then_inc(q_mm[b], 1)

            with ExitStack() as s2:
                sb, sem, sems = alloc(s2)
                G, Y, XC, SQ, H, O = ([sb(f"c2_{n}{b}", [P, U * C]) for b in range(2)] for n in ("g", "y", "xc", "sq", "h", "o"))
                s_, v_, sd_, rs_ = ([sb(f"c2_{n}{b}", [P, U]) for b in range(2)] for n in ("sum", "var", "std", "rstd"))
                S = [sb(f"c2_s{b}", [C, CE]) for b in range(2)]
                ixs, ixe = ([sb(f"c2_{n}{b}", [P, U], i32) for b in range(2)] for n in ("ixs", "ixe"))
                ix_r, ixe_r, got, gT, s_r, s_back, y_r, centred, squared, var_r, std_r, o_r, sent = (sems(f"c2_{n}") for n in (
                    "ix_ready", "ixe_ready", "gathered", "gT", "scanned", "sums_back", "x1", "centred", "squared", "var", "std", "rows", "sent"))
                dl, m1 = sem("c2_link"), sem("c2_zero")
                with nc.Block() as block:
                    @block.gpsimd
                    def _(pool):
                        def gathers(b, j):
                            pool.wait_ge(ix_r[b], j + 1)
                            pool.wait_ge(gT[b], j)
                            pool.sem_inc(pool_went_on, 1)
                            gather(pool, G[b], C, qs, ixs[b], got[b])
                        def scatters(b, j):
                            pool.wait_ge(o_r[b], j + 1)
                            pool.wait_ge(ixe_r[b], j + 1)
                            pool.sem_inc(pool_went_on, 1)
                            scatter(pool, x1, ixe[b], Y[b], C, sent[b])
                            scatter(pool, out, ixe[b], O[b], C, sent[b])
                        with pool.Fori(0, PAIRS) as j:
                            gathers(0, j)
                            gathers(1, j)
                            scatters(0, j)
                            scatters(1, j)
                        for b in range(2):
                            pool.wait_ge(sent[b], 32 * U * PAIRS)

                    @block.vector
                    def _(dve):
                        for b in range(2):
                            ins = dve.memset(S[b][:, :], 0.0)
                        ins.then_inc(m1, 1)
                        dve.wait_ge(m1, 1)
                        K = 2 * 8
                        with dve.Fori(0, PAIRS) as j:
                            ch = Chain(dve, dl, j * K)
                            for b in range(2):
                                cols = bass.ds((j * 2 + b) * U, U)
                                dve.wait_ge(gT[b], j + 1)
                                dve.wait_ge(*pair_of_scans(b, j, s_r))
                                dve.tensor_tensor_scan(S[b][:, :], mask_d[0:C, bass.ds((j * 2 + b) * CE, CE)], bank[4 * b][0:C, 0:CE],
                                                       S[1 - b][:, CE - 1:CE], ALU.mult, ALU.add).then_inc(s_r[b], 1)
                                dve.wait_ge(s_back[b], j + 1)
                                dve.wait_ge(sent[b], j * (32 * U))
                                ch.link(dve.tensor_tensor(out=r3(Y[b]), in0=QSD[:, cols, :], in1=prows(bank[4 * b + 1]), op=ALU.add))
                                ch.link(dve.tensor_tensor(out=r3(Y[b]), in0=r3(Y[b]), in1=brd(dinv_d[:, cols], U), op=ALU.mult))
                                ch.link(dve.tensor_tensor(out=r3(Y[b]), in0=r3(Y[b]), in1=rows(b4B[:, :], U), op=ALU.add))
                                ch.link(dve.tensor_tensor(out=r3(Y[b]), in0=r3(Y[b]), in1=XD[:, cols, :], op=ALU.add))
                                ln_centre(dve, ch.link, r3(Y[b]), s_[b][:, :], r3(XC[b]), U).then_inc(centred[b], 1)
                                dve.wait_ge(squared[b], j + 1)
                                ln_var(dve, r3(SQ[b]), v_[b][:, :]).then_inc(var_r[b], 1)
                                dve.wait_ge(std_r[b], j + 1)
                                ch.link(ln_relu(dve, ch.link, sd_[b][:, :], rs_[b][:, :], r3(XC[b]), r3(H[b]), U))
                                ch.link(dve.tensor_tensor(out=H[b][:, :], in0=H[b][:, :], in1=Y[b][:, :], op=ALU.add))
                                dve.tensor_tensor(out=r3(O[b]), in0=r3(H[b]), in1=rows(c0B[:, :], U), op=ALU.add).then_inc(o_r[b], 1)
                            assert ch.n == K, ch.n

                    @block.scalar
                    def _(act):
                        with act.Fori(0, PAIRS) as j:
                            for i in range(2):
                                act.wait_ge(got[i], j * (16 * U))
                                act.activation(ixs[i][:, :], src_i[:, bass.ds((j * 2 + i) * U, U)], ACT.Copy).then_inc(ix_r[i], 1)
                            for b in range(2):
                                act.wait_ge(sent[b], j * (32 * U))
                                act.activation(ixe[b][:, :], dst_end[:, bass.ds((j * 2 + b) * U, U)], ACT.Copy).then_inc(ixe_r[b], 1)
                                act.wait_ge(centred[b], j + 1)
                                ln_square(act, XC[b][:, :], SQ[b][:, :]).then_inc(squared[b], 1)
                                act.wait_ge(var_r[b], j + 1)
                                ln_std(act, v_[b][:, :], sd_[b][:, :]).then_inc(std_r[b], 1)

                    @block.tensor
                    def _(pe):
                        with pe.Fori(0, PAIRS) as j:
                            for b in range(2):
                                pe.wait_ge(got[b], j * (16 * U) + 16 * U)
                                fwd(pe, bank[4 * b], r3(G[b]), C, gT[b])
                                pe.wait_ge(s_r[b], j + 1)
                                pe.wait_ge(centred[b], j)
                                back(pe, bank[4 * b + 1], S[b], C, s_back[b])

        with ExitStack() as st:
            sb, sem, sems = alloc(st)
            DEL = sb("series", [P, T, C])
            wk = sb("wk", [P, T])
            with ExitStack() as s2:
                sb, sem, sems = alloc(s2)
                G, XC, SQ, H, TR = ([sb(f"t1_{n}{b}", [P, U * C]) for b in range(2)] for n in ("g", "xc", "sq", "h", "tr"))
                s_, v_, sd_, rs_ = ([sb(f"t1_{n}{b}", [P, U]) for b in range(2)] for n in ("sum", "var", "std", "rstd"))
                S = [sb(f"t1_s{b}", [C, CE]) for b in range(2)]
                ixs = [sb(f"t1_ix{b}", [P, U], i32) for b in range(2)]
                ix_r, got, centred, squared, var_r, std_r, m_r, mT, s_r, s_back, row_r, stored, d_r = (sems(f"t1_{n}") for n in (
                    "ix_ready", "gathered", "centred", "squared", "var", "std", "messages", "mT", "scanned", "sums_back", "rows", "stored", "kept"))
                dl, m1 = sem("t1_link"), sem("t1_zero")
                with nc.Block() as block:
                    @block.gpsimd
                    def _(pool):
                        with pool.Fori(0, PAIRS) as j:
                            for b in range(2):
                                pool.wait_ge(ix_r[b], j + 1)
                                pool.wait_ge(centred[b], j)
                                pool.sem_inc(pool_went_on, 1)
                                gather(pool, G[b], C, x1, ixs[b], got[b])

                    @block.vector
                    def _(dve):
                        for b in range(2):
                            ins = dve.memset(S[b][:, :], 0.0)
                        ins.then_inc(m1, 1)
                        dve.wait_ge(m1, 1)
                        dve.tensor_scalar(wk[:, :], w_s[:, :], rat[:, 1:2], None, ALU.mult).then_inc(m1, 1)
                        dve.wait_ge(m1, 2)
                        K = 2 * 3
                        with dve.Fori(0, PAIRS) as j:
                            ch = Chain(dve, dl, j * K)
                            for b in range(2):
                                cols = bass.ds((j * 2 + b) * U, U)
                                dve.wait_ge(got[b], j * (16 * U) + 16 * U)
                                ln_centre(dve, ch.link, r3(G[b]), s_[b][:, :], r3(XC[b]), U).then_inc(centred[b], 1)
                                dve.wait_ge(squared[b], j + 1)
                                ln_var(dve, r3(SQ[b]), v_[b][:, :]).then_inc(var_r[b], 1)
                                dve.wait_ge(std_r[b], j + 1)
                                ch.link(ln_relu(dve, ch.link, sd_[b][:, :], rs_[b][:, :], r3(XC[b]), r3(H[b]), U))
                                dve.tensor_tensor(out=r3(H[b]), in0=r3(H[b]), in1=brd(wk[:, cols], U), op=ALU.mult).then_inc(m_r[b], 1)
                                dve.wait_ge(mT[b], j + 1)
                                dve.wait_ge(*pair_of_scans(b, j, s_r))
                                dve.tensor_tensor_scan(S[b][:, :], mask_s[0:C, bass.ds((j * 2 + b) * CE, CE)], bank[4 * b][0:C, 0:CE],
                                                       S[1 - b][:, CE - 1:CE], ALU.mult, ALU.add).then_inc(s_r[b], 1)
                                dve.wait_ge(row_r[b], j + 1)
                                dve.tensor_copy(DEL[:, cols, :], r3(TR[b])).then_inc(d_r[b], 1)
                            assert ch.n == K, ch.n

                    @block.scalar
                    def _(act):
                        with act.Fori(0, PAIRS) as j:
                            for i in range(2):
                                act.wait_ge(got[i], j * (16 * U))
                                act.activation(ixs[i][:, :], dstS_i[:, bass.ds((j * 2 + i) * U, U)], ACT.Copy).then_inc(ix_r[i], 1)
                            for b in range(2):
                                act.wait_ge(centred[b], j + 1)
                                ln_square(act, XC[b][:, :], SQ[b][:, :]).then_inc(squared[b], 1)
                                act.wait_ge(var_r[b], j + 1)
                                ln_std(act, v_[b][:, :], sd_[b][:, :]).then_inc(std_r[b], 1)
                                act.wait_ge(s_back[b], j + 1)
                                act.wait_ge(stored[b], j * 16)
                                act.wait_ge(d_r[b], j)
                                act.activation(TR[b][:, :], bank[4 * b + 1][0:P, 0:U * C], ACT.Copy).then_inc(row_r[b], 1)

                    @block.tensor
                    def _(pe):
                        with pe.Fori(0, PAIRS) as j:
                            for b in range(2):
                                pe.wait_ge(m_r[b], j + 1)
                                fwd(pe, bank[4 * b], r3(H[b]), C, mT[b])
                                pe.wait_ge(s_r[b], j + 1)
                                pe.wait_ge(row_r[b], j)
                                back(pe, bank[4 * b + 1], S[b], C, s_back[b])

                    @block.sync
                    def _(sp):
                        with sp.Fori(0, PAIRS) as j:
                            for b in range(2):
                                sp.wait_ge(row_r[b], j + 1)
                                sp.dma_start(chunk_rows(terms[1], j * 2 + b), r3(TR[b])).then_inc(stored[b], 16)
                        for b in range(2):
                            sp.wait_ge(stored[b], 16 * PAIRS)

            for first, STEPS in ((2, TERMS // 2), (2 + TERMS // 2, TERMS // 2 - 1)):
                with ExitStack() as s2:
                    sb, sem, sems = alloc(s2)
                    G, M, TR = ([sb(f"tk{first}_{n}{b}", [P, U * C]) for b in range(2)] for n in ("g", "m", "tr"))
                    S = [sb(f"tk{first}_s{b}", [C, CE]) for b in range(2)]
                    ixs = [sb(f"tk{first}_ix{b}", [P, U], i32) for b in range(2)]
                    ix_r, got, m_r, mT, s_r, s_back, row_r, stored, d_r = (sems(f"tk{first}_{n}") for n in (
                        "ix_ready", "gathered", "messages", "mT", "scanned", "sums_back", "rows", "stored", "added"))
                    wk_r, m1 = sem(f"tk{first}_weights"), sem(f"tk{first}_zero")
                    with nc.Block() as block:
                        @block.gpsimd
                        def _(pool):
                            def step(i, par):
                                for b in range(2):
                                    pool.wait_ge(stored[b], i * (16 * PAIRS))
                                pool.sem_inc(pool_went_on, 1)
                                with pool.Fori(0, PAIRS) as j:
                                    for b in range(2):
                                        pool.wait_ge(ix_r[b], i * PAIRS + j + 1)
                                        pool.wait_ge(m_r[b], i * PAIRS + j)
                                        pool.sem_inc(pool_went_on, 1)
                                        gather(pool, G[b], C, terms[1 - par], ixs[b], got[b])
                            with pool.Fori(0, STEPS // 2) as h:
                                step(h * 2, 0)
                                step(h * 2 + 1, 1)
                            if STEPS % 2:
                                step(STEPS - 1, 0)

                        @block.vector
                        def _(dve):
                            for b in range(2):
                                ins = dve.memset(S[b][:, :], 0.0)
                            ins.then_inc(m1, 1)
                            dve.wait_ge(m1, 1)
                            def step(i, par):
                                for b in range(2):
                                    dve.wait_ge(m_r[b], i * PAIRS)
                                dve.tensor_scalar(wk[:, :], w_s[:, :], rat[:, bass.ds(i + first, 1)], None, ALU.mult).then_inc(wk_r, 1)
                                with dve.Fori(0, PAIRS) as j:
                                    n = i * PAIRS + j
                                    dve.wait_ge(wk_r, i + 1)
                                    for b in range(2):
                                        cols = bass.ds((j * 2 + b) * U, U)
                                        dve.wait_ge(got[b], n * (16 * U) + 16 * U)
                                        dve.wait_ge(mT[b], n)
                                        dve.tensor_tensor(out=r3(M[b]), in0=r3(G[b]), in1=brd(wk[:, cols], U), op=ALU.mult).then_inc(m_r[b], 1)
                                        dve.wait_ge(mT[b], n + 1)
                                        dve.wait_ge(*pair_of_scans(b, n, s_r))
                                        dve.tensor_tensor_scan(S[b][:, :], mask_s[0:C, bass.ds((j * 2 + b) * CE, CE)], bank[4 * b][0:C, 0:CE],
                                                               S[1 - b][:, CE - 1:CE], ALU.mult, ALU.add).then_inc(s_r[b], 1)
                                        dve.wait_ge(row_r[b], n + 1)
                                        dve.tensor_tensor(out=DEL[:, cols, :], in0=DEL[:, cols, :], in1=r3(TR[b]), op=ALU.add).then_inc(d_r[b], 1)
                            with dve.Fori(0, STEPS // 2) as h:
                                step(h * 2, 0)
                                step(h * 2 + 1, 1)
                            if STEPS % 2:
                                step(STEPS - 1, 0)

                        @block.scalar
                        def _(act):
                            def step(i, par):
                                with act.Fori(0, PAIRS) as j:
                                    n = i * PAIRS + j
                                    for b in range(2):
                                        act.wait_ge(got[b], n * (16 * U))
                                        act.activation(ixs[b][:, :], gi_i[:, bass.ds((j * 2 + b) * U, U)], ACT.Copy).then_inc(ix_r[b], 1)
                                    for b in range(2):
                                        act.wait_ge(s_back[b], n + 1)
                                        act.wait_ge(stored[b], n * 16)
                                        act.wait_ge(d_r[b], n)
                                        act.activation(TR[b][:, :], bank[4 * b + 1][0:P, 0:U * C], ACT.Copy).then_inc(row_r[b], 1)
                            with act.Fori(0, STEPS // 2) as h:
                                step(h * 2, 0)
                                step(h * 2 + 1, 1)
                            if STEPS % 2:
                                step(STEPS - 1, 0)

                        @block.tensor
                        def _(pe):
                            def step(i, par):
                                with pe.Fori(0, PAIRS) as j:
                                    n = i * PAIRS + j
                                    for b in range(2):
                                        pe.wait_ge(m_r[b], n + 1)
                                        fwd(pe, bank[4 * b], r3(M[b]), C, mT[b])
                                        pe.wait_ge(s_r[b], n + 1)
                                        pe.wait_ge(row_r[b], n)
                                        back(pe, bank[4 * b + 1], S[b], C, s_back[b])
                            with pe.Fori(0, STEPS // 2) as h:
                                step(h * 2, 0)
                                step(h * 2 + 1, 1)
                            if STEPS % 2:
                                step(STEPS - 1, 0)

                        @block.sync
                        def _(sp):
                            def step(i, par):
                                with sp.Fori(0, PAIRS) as j:
                                    n = i * PAIRS + j
                                    for b in range(2):
                                        sp.wait_ge(row_r[b], n + 1)
                                        sp.dma_start(chunk_rows(terms[par], j * 2 + b), r3(TR[b])).then_inc(stored[b], 16)
                            with sp.Fori(0, STEPS // 2) as h:
                                step(h * 2, 0)
                                step(h * 2 + 1, 1)
                            if STEPS % 2:
                                step(STEPS - 1, 0)
                            for b in range(2):
                                sp.wait_ge(stored[b], 16 * PAIRS * STEPS)

            with ExitStack() as s2:
                sb, sem, sems = alloc(s2)
                G, XC, SQ, H, O = ([sb(f"l2_{n}{b}", [P, U * C]) for b in range(2)] for n in ("g", "xc", "sq", "h", "o"))
                s_, v_, sd_, rs_ = ([sb(f"l2_{n}{b}", [P, U]) for b in range(2)] for n in ("sum", "var", "std", "rstd"))
                ixs, ixe = ([sb(f"l2_{n}{b}", [P, U], i32) for b in range(2)] for n in ("ixs", "ixe"))
                AR = [sb(f"l2_attr{b}", [P, U * ATTR]) for b in range(2)]
                AS, AM, CN, MEAN = ([sb(f"l2_{n}{b}", [ATTR, CE]) for b in range(2)] for n in ("seg_sum", "seg_max", "seg_cnt", "mean"))
                BM = [sb(f"l2_big{b}", [ATTR, CE]) for b in range(2)]
                ones = sb("l2_ones", [ATTR, CE])
                Z = [sb(f"l2_z{b}", [HID, CE]) for b in range(2)]
                ix_r, ixe_r, got, a_in, a_T, big_r, sc_r, mean_r, z_mm, z_r, l2_mm, centred, squared, var_r, std_r, o_r, sent = (sems(f"l2_{n}") for n in (
                    "ix_ready", "ixe_ready", "gathered", "attr_in", "attr_T", "big", "scanned", "mean", "z_mm", "z", "rows_mm", "centred", "squared", "var", "std", "rows", "sent"))
                dl, m1 = sem("l2_link"), sem("l2_zero")
                with nc.Block() as block:
                    @block.gpsimd
                    def _(pool):
                        def gathers(b, j):
                            pool.wait_ge(ix_r[b], j + 1)
                            pool.wait_ge(o_r[b], j)
                            pool.sem_inc(pool_went_on, 1)
                            gather(pool, G[b], C, x1, ixs[b], got[b])
                        def scatters(b, j):
                            pool.wait_ge(o_r[b], j + 1)
                            pool.wait_ge(ixe_r[b], j + 1)
                            pool.sem_inc(pool_went_on, 1)
                            scatter(pool, out, ixe[b], O[b], C, sent[b])
                        with pool.Fori(0, PAIRS) as j:
                            gathers(0, j)
                            gathers(1, j)
                            scatters(0, j)
                            scatters(1, j)
                        for b in range(2):
                            pool.wait_ge(sent[b], 16 * U * PAIRS)

                    @block.sync
                    def _(sp):
                        with sp.Fori(0, PAIRS) as j:
                            for b in range(2):
                                sp.wait_ge(a_T[b], j)
                                sp.dma_start(r3(AR[b]), chunk_rows(pay, j * 2 + b)[:, :, 4:PAYW]).then_inc(a_in[b], 16)

                    @block.vector
                    def _(dve):
                        dve.memset(ones[:, :], 1.0)
                        for b in range(2):
                            dve.memset(AS[b][:, :], 0.0)
                            dve.memset(AM[b][:, :], 0.0)
                            ins = dve.memset(CN[b][:, :], 0.0)
                        ins.then_inc(m1, 1)
                        dve.wait_ge(m1, 1)
                        K = 2 * 8
                        with dve.Fori(0, PAIRS) as j:
                            ch = Chain(dve, dl, j * K)
                            for b in range(2):
                                c = j * 2 + b
                                cols = bass.ds(c * U, U)
                                mask = mask_s[0:ATTR, bass.ds(c * CE, CE)]
                                ch.link(dve.tensor_scalar(BM[b][:, :], mask, 1.0, BIG, ALU.subtract, ALU.mult))
                                dve.wait_ge(a_T[b], j + 1)
                                dve.wait_ge(*pair_of_scans(b, j, sc_r))
                                dve.wait_ge(z_mm[b], j)
                                dve.tensor_tensor_scan(AS[b][:, :], mask, bank[4 * b][0:ATTR, 0:CE], AS[1 - b][:, CE - 1:CE], ALU.mult, ALU.add)
                                dve.tensor_tensor_scan(AM[b][:, :], BM[b][:, :], bank[4 * b][0:ATTR, 0:CE], AM[1 - b][:, CE - 1:CE], ALU.add, ALU.max)
                                dve.tensor_tensor_scan(CN[b][:, :], mask, ones[:, :], CN[1 - b][:, CE - 1:CE], ALU.mult, ALU.add).then_inc(sc_r[b], 1)
                                dve.wait_ge(sc_r[b], j + 1)
                                ch.link(dve.reciprocal(MEAN[b][:, :], CN[b][:, :]))
                                dve.tensor_tensor(out=MEAN[b][:, :], in0=MEAN[b][:, :], in1=AS[b][:, :], op=ALU.mult).then_inc(mean_r[b], 1)
                                dve.wait_ge(got[b], j * (16 * U) + 16 * U)
                                ln_centre(dve, ch.link, r3(G[b]), s_[b][:, :], r3(XC[b]), U).then_inc(centred[b], 1)
                                dve.wait_ge(squared[b], j + 1)
                                ln_var(dve, r3(SQ[b]), v_[b][:, :]).then_inc(var_r[b], 1)
                                dve.wait_ge(std_r[b], j + 1)
                                ch.link(ln_relu(dve, ch.link, sd_[b][:, :], rs_[b][:, :], r3(XC[b]), r3(H[b]), U))
                                ch.link(dve.tensor_tensor(out=r3(H[b]), in0=r3(H[b]), in1=DEL[:, cols, :], op=ALU.add))
                                ch.link(dve.tensor_tensor(out=H[b][:, :], in0=H[b][:, :], in1=G[b][:, :], op=ALU.add))
                                ch.link(dve.tensor_tensor(out=r3(H[b]), in0=r3(H[b]), in1=rows(b2B[:, :], U), op=ALU.add))
                                dve.wait_ge(l2_mm[b], j + 1)
                                dve.wait_ge(sent[b], j * (16 * U))
                                dve.tensor_tensor(out=O[b][:, :], in0=H[b][:, :], in1=bank[4 * b + 2][0:P, 0:U * C], op=ALU.add).then_inc(o_r[b], 1)
                            assert ch.n == K, ch.n

                    @block.scalar
                    def _(act):
                        with act.Fori(0, PAIRS) as j:
                            for i in range(2):
                                act.wait_ge(got[i], j * (16 * U))
                                act.activation(ixs[i][:, :], srcS_i[:, bass.ds((j * 2 + i) * U, U)], ACT.Copy).then_inc(ix_r[i], 1)
                            for b in range(2):
                                act.wait_ge(sent[b], j * (16 * U))
                                act.activation(ixe[b][:, :], srcS_end[:, bass.ds((j * 2 + b) * U, U)], ACT.Copy).then_inc(ixe_r[b], 1)
                                act.wait_ge(z_mm[b], j + 1)
                                act.activation(Z[b][:, :], bank[4 * b + 1][0:HID, 0:CE], ACT.Relu, bias=b1u[:, :]).then_inc(z_r[b], 1)
                                act.wait_ge(centred[b], j + 1)
                                ln_square(act, XC[b][:, :], SQ[b][:, :]).then_inc(squared[b], 1)
                                act.wait_ge(var_r[b], j + 1)
                                ln_std(act, v_[b][:, :], sd_[b][:, :]).then_inc(std_r[b], 1)

                    @block.tensor
                    def _(pe):
                        with pe.Fori(0, PAIRS) as j:
                            for b in range(2):
                                pe.wait_ge(a_in[b], j * 16 + 16)
                                pe.wait_ge(sc_r[b], j)
                                fwd(pe, bank[4 * b], r3(AR[b]), ATTR, a_T[b])
                                pe.wait_ge(mean_r[b], j + 1)
                                for i, a in enumerate((AS, AM, MEAN)):
                                    ins = pe.matmul(bank[4 * b + 1][0:HID, 0:CE], w1_sb[:, i, :], a[b][:, :], start=i == 0, stop=i == 2)
                                ins.then_inc(z_mm[b], 1)
                                pe.wait_ge(z_r[b], j + 1)
                                pe.wait_ge(o_r[b], j)
                                for u in range(U):
                                    ins = pe.matmul(bank[4 * b + 2][0:P, u * C:(u + 1) * C], Z[b][:, u * P:(u + 1) * P], w2_sb[:, :], start=True, stop=True)
                                ins.then_inc(l2_mm[b], 1)

        with ExitStack() as st:
            sb, sem, sems = alloc(st)
            RES = sb("res", [P, T, C])
            with ExitStack() as s2:
                sb, sem, sems = alloc(s2)
                G, XC, SQ, H = ([sb(f"l3_{n}{b}", [P, 2 * U * C]) for b in range(2)] for n in ("g", "xc", "sq", "h"))
                s_, v_, sd_, rs_ = ([sb(f"l3_{n}{b}", [P, 2 * U]) for b in range(2)] for n in ("sum", "var", "std", "rstd"))
                ixs, ixd = ([sb(f"l3_{n}{b}", [P, U], i32) for b in range(2)] for n in ("ixs", "ixd"))
                HT = [[sb(f"l3_hT{k}{b}", [C, CE]) for b in range(2)] for k in range(2)]
                MX, BM, XT, R = ([sb(f"l3_{n}{b}", [C, CE]) for b in range(2)] for n in ("max", "big", "uv", "r"))
                ix_r, got, centred, squared, var_r, std_r, h_r, hT_mm, hT_r, uv_mm, big_r, mx_r, sum_r, r_r, r_back, res_r = (sems(f"l3_{n}") for n in (
                    "ix_ready", "gathered", "centred", "squared", "var", "std", "h", "hT_mm", "hT", "uv_mm", "big", "max", "sum", "relu", "back", "res"))
                dl, m1 = sem("l3_link"), sem("l3_zero")
                with nc.Block() as block:
                    @block.gpsimd
                    def _(pool):
                        with pool.Fori(0, PAIRS) as j:
                            for b in range(2):
                                pool.wait_ge(ix_r[b], j + 1)
                                pool.wait_ge(res_r[b], j)
                                pool.sem_inc(pool_went_on, 1)
                                gather(pool, G[b], C, out, ixs[b], got[b])
                                gather(pool, G[b][:, U * C:], C, out, ixd[b], got[b])

                    @block.vector
                    def _(dve):
                        for b in range(2):
                            ins = dve.memset(MX[b][:, :], 0.0)
                        ins.then_inc(m1, 1)
                        dve.wait_ge(m1, 1)
                        K = 2 * 3
                        with dve.Fori(0, PAIRS) as j:
                            ch = Chain(dve, dl, j * K)
                            for b in range(2):
                                c = j * 2 + b
                                cols = bass.ds(c * U, U)
                                ch.link(dve.tensor_scalar(BM[b][:, :], mask_d[0:C, bass.ds(c * CE, CE)], 1.0, BIG, ALU.subtract, ALU.mult))
                                dve.wait_ge(got[b], j * (32 * U) + 32 * U)
                                ln_centre(dve, ch.link, r3(G[b], 2 * U), s_[b][:, :], r3(XC[b], 2 * U), 2 * U).then_inc(centred[b], 1)
                                dve.wait_ge(squared[b], j + 1)
                                ln_var(dve, r3(SQ[b], 2 * U), v_[b][:, :]).then_inc(var_r[b], 1)
                                dve.wait_ge(std_r[b], j + 1)
                                ln_relu(dve, ch.link, sd_[b][:, :], rs_[b][:, :], r3(XC[b], 2 * U), r3(H[b], 2 * U), 2 * U).then_inc(h_r[b], 1)
                                dve.wait_ge(uv_mm[b], j + 1)
                                dve.wait_ge(*pair_of_scans(b, j, mx_r))
                                dve.tensor_tensor_scan(MX[b][:, :], BM[b][:, :], bank[4 * b + 2][0:C, 0:CE], MX[1 - b][:, CE - 1:CE], ALU.add, ALU.max)\
                                   .then_inc(mx_r[b], 1)
                                dve.wait_ge(mx_r[b], j + 1)
                                dve.wait_ge(r_r[b], j)
                                dve.tensor_tensor(out=XT[b][:, :], in0=MX[b][:, :], in1=bank[4 * b + 3][0:C, 0:CE], op=ALU.add).then_inc(sum_r[b], 1)
                                dve.wait_ge(r_back[b], j + 1)
                                dve.tensor_tensor(out=RES[:, cols, :], in0=r3(G[b], 2 * U)[:, U:2 * U, :], in1=prows(bank[4 * b]), op=ALU.add).then_inc(res_r[b], 1)
                            assert ch.n == K, ch.n

                    @block.scalar
                    def _(act):
                        with act.Fori(0, PAIRS) as j:
                            for i in range(2):
                                act.wait_ge(got[i], j * (32 * U))
                                act.activation(ixs[i][:, :], src_i[:, bass.ds((j * 2 + i) * U, U)], ACT.Copy)
                                act.activation(ixd[i][:, :], dst_i[:, bass.ds((j * 2 + i) * U, U)], ACT.Copy).then_inc(ix_r[i], 1)
                            for b in range(2):
                                act.wait_ge(centred[b], j + 1)
                                ln_square(act, XC[b][:, :], SQ[b][:, :]).then_inc(squared[b], 1)
                                act.wait_ge(var_r[b], j + 1)
                                ln_std(act, v_[b][:, :], sd_[b][:, :]).then_inc(std_r[b], 1)
                                act.wait_ge(hT_mm[b], j + 1)
                                for k in range(2):
                                    ins = act.activation(HT[k][b][:, :], bank[4 * b + k][0:C, 0:CE], ACT.Copy)
                                ins.then_inc(hT_r[b], 1)
                                act.wait_ge(sum_r[b], j + 1)
                                act.wait_ge(r_back[b], j)
                                act.activation(R[b][:, :], XT[b][:, :], ACT.Relu, bias=bl3_sb[:, :]).then_inc(r_r[b], 1)

                    @block.tensor
                    def _(pe):
                        with pe.Fori(0, PAIRS) as j:
                            for b in range(2):
                                pe.wait_ge(h_r[b], j + 1)
                                pe.wait_ge(res_r[b], j)
                                pe.sem_inc(pe_went_on, 1)
                                for k in range(2):
                                    for u in range(U):
                                        ins = pe.transpose(bank[4 * b + k][0:C, u * P:(u + 1) * P], r3(H[b], 2 * U)[:, k * U + u, :], ident[0:P, 0:P])
                                ins.then_inc(hT_mm[b], 1)
                                pe.wait_ge(hT_r[b], j + 1)
                                pe.sem_inc(pe_went_on, 1)
                                pe.matmul(bank[4 * b + 2][0:C, 0:CE], wl3_sb[:, 1, :], HT[0][b][:, :], start=True, stop=True)
                                pe.matmul(bank[4 * b + 3][0:C, 0:CE], wu_sb[:, :], HT[1][b][:, :], start=True, stop=True).then_inc(uv_mm[b], 1)
                                pe.wait_ge(r_r[b], j + 1)
                                back(pe, bank[4 * b], R[b], C, r_back[b])

            with ExitStack() as s2:
                sb, sem, sems = alloc(s2)
                O = [sb(f"fin_o{b}", [P, U * C]) for b in range(2)]
                ixe = [sb(f"fin_ix{b}", [P, U], i32) for b in range(2)]
                o_r, sent, ixe_r = sems("fin_rows"), sems("fin_sent"), sems("fin_ix")
                with nc.Block() as block:
                    @block.gpsimd
                    def _(pool):
                        with pool.Fori(0, PAIRS) as j:
                            for b in range(2):
                                pool.wait_ge(o_r[b], j + 1)
                                pool.wait_ge(ixe_r[b], j + 1)
                                pool.sem_inc(pool_went_on, 1)
                                scatter(pool, out, ixe[b], O[b], C, sent[b])
                        for b in range(2):
                            pool.wait_ge(sent[b], 16 * U * PAIRS)

                    @block.vector
                    def _(dve):
                        with dve.Fori(0, PAIRS) as j:
                            for b in range(2):
                                dve.wait_ge(sent[b], j * (16 * U))
                                dve.tensor_copy(r3(O[b]), RES[:, bass.ds((j * 2 + b) * U, U), :]).then_inc(o_r[b], 1)

                    @block.scalar
                    def _(act):
                        with act.Fori(0, PAIRS) as j:
                            for b in range(2):
                                act.wait_ge(sent[b], j * (16 * U))
                                act.activation(ixe[b][:, :], dst_end[:, bass.ds((j * 2 + b) * U, U)], ACT.Copy).then_inc(ixe_r[b], 1)



_INS = ["x", "src_pad", "dst_pad", "edge_attr_32", "edge_weight", "w3t", "b3", "w4t", "b4", "t", "u", "w1", "b1", "w2", "b2",
        "wl3", "bl3", "ratios"]


def kernel(x, src, dst, edge_attr_32, edge_weight, edge_weight1, L0_gnn_W3, L0_gnn_b3, L0_gnn_W4, L0_gnn_b4, L1_gnn_t,
           L2_gnn_u, L2_gnn_W1, L2_gnn_b1, L2_gnn_W2, L2_gnn_b2, L3_gnn_W, L3_gnn_b):
    import numpy as np
    import concourse.bacc as bacc
    from concourse import mybir as mb
    from concourse.bass_utils import run_bass_kernel_spmd

    pad = lambda a: np.pad(np.asarray(a), 1, constant_values=-1)
    given = dict(x=x, src_pad=pad(src), dst_pad=pad(dst), edge_attr_32=edge_attr_32, edge_weight=edge_weight,
                 w3t=np.asarray(L0_gnn_W3).T, b3=L0_gnn_b3, w4t=np.asarray(L0_gnn_W4).T, b4=L0_gnn_b4, t=L1_gnn_t,
                 u=L2_gnn_u, w1=L2_gnn_W1, b1=L2_gnn_b1, w2=L2_gnn_W2, b2=L2_gnn_b2, wl3=np.asarray(L3_gnn_W).T,
                 bl3=L3_gnn_b, ratios=np.array(taylor_ratios(), np.float32))
    nc = bacc.Bacc("TRN2", target_bir_lowering=False, num_devices=1)
    arrays, args = {}, []
    for name in _INS:
        a = np.ascontiguousarray(given[name])
        arrays[f"in_{name}"] = a
        args.append(nc.dram_tensor(f"in_{name}", a.shape, mb.dt.from_np(a.dtype), kind="ExternalInput").ap())
    o = nc.dram_tensor("out_rows", (N, C), mb.dt.float32, kind="ExternalOutput").ap()
    gnn(nc, *args, o)
    r = run_bass_kernel_spmd(nc, [arrays], core_ids=[0])
    return r.results[0]["out_rows"]
```

```python
import concourse.bass as bass
from concourse import mybir
from contextlib import ExitStack

N, C, E = 100000, 64, 25000
HID = 128
ATTR = 32
P = 125
T = E // P
U = 4
CE = U * P
CHUNKS = T // U
PAIRS = CHUNKS // 2
ND = N // P
HALF = ND // 2
PAYW = 5 + ATTR
N_SUB, M_TERMS = 4, 20
TERMS = N_SUB * M_TERMS
EPS = 1e-5
TW = C + 1
LISTS = 6
U2 = 2
CE2 = U2 * P
NR = P * 205
NOWHERE = E + 2
BIG = 3.0e38


def taylor_ratios():
    term = [1]
    for k in range(M_TERMS, 0, -1):
        term.append(term[-1] * k)
    term.reverse()
    c = [1]
    for _ in range(N_SUB):
        new = [0] * (len(c) + M_TERMS)
        for i, a in enumerate(c):
            for k, b in enumerate(term):
                new[i + k] += a * b
        c = new
    return [0.0] + [c[k] / c[k - 1] for k in range(1, TERMS + 1)]


class Chain:

    def __init__(self, eng, sem, base=0):
        self.eng, self.sem, self.base, self.n = eng, sem, base, 0

    def put(self, ins):
        self.n += 1
        ins.then_inc(self.sem, 1)
        return self.n

    def need(self, n):
        self.eng.wait_ge(self.sem, self.base + n)

    def link(self, ins):
        self.need(self.put(ins))


def gnn(nc, x, src_pad, dst_pad, attr, w, w3t, b3, w4t, b4, t_in, u_in, w1, b1, w2, b2, wl3, bl3, ratios, out):
    f32, i32, u8, f16 = mybir.dt.float32, mybir.dt.int32, mybir.dt.uint8, mybir.dt.float16
    ALU, ACT, AX = mybir.AluOpType, mybir.ActivationFunctionType, mybir.AxisListType

    ratios_py = taylor_ratios()
    qs = nc.dram_tensor("qs_table", [N, C], f32).ap()
    x1 = nc.dram_tensor("x1_table", [N, C], f32).ap()
    dinv_tab = nc.dram_tensor("dinv_table", [N, 1], f32).ap()
    endp_tab = nc.dram_tensor("endp_table", [N, 1], f32).ap()
    pay = nc.dram_tensor("sorted_edges", [E, PAYW], f32).ap()
    srcs_pad = nc.dram_tensor("sorted_src", [E + 2], f32).ap()
    terms = [nc.dram_tensor(f"terms{i}", [NR, TW], f32).ap() for i in range(3)]
    series = nc.dram_tensor("series_by_place", [NR, C], f32).ap()
    lists = {k: nc.dram_tensor(f"list{k}", [NR, 4], f32).ap() for k in range(2, LISTS + 1)}

    tile_major = lambda a: a.rearrange("(t p) -> p t", p=P)
    chunk_rows = lambda a, c: a[bass.ds(c * CE, CE), :].rearrange("(u p) f -> p u f", p=P)

    ctx = ExitStack()
    with ctx:
        ctx.enter_context(nc.allow_non_contiguous_dma("index columns and broadcasts"))

        def alloc(stack):
            used = []

            def sem(name):
                used.append(nc.alloc_semaphore(name))
                return used[-1]

            def end():
                if used:
                    nc.clear_and_free_semaphores(used)
                    nc.all_engine_barrier()

            stack.callback(end)
            return (lambda name, shape, dt=f32: stack.enter_context(nc.sbuf_tensor(name, shape, dt)),
                    sem, lambda name: [sem(f"{name}_{b}") for b in range(2)])

        sb = lambda name, shape, dt=f32: ctx.enter_context(nc.sbuf_tensor(name, shape, dt))
        two = [ctx.enter_context(nc.psum_tensor(f"banks{i}", [128, 2, 512], f32)) for i in range(4)]
        bank = [two[i // 2][:, i % 2, :] for i in range(8)]

        pool_went_on, pe_went_on = (ctx.enter_context(nc.semaphore(n)) for n in ("pool_went_on", "pe_went_on"))

        ident = sb("ident", [128, 128])
        src_i, dst_i = sb("src_i", [P, T], i32), sb("dst_i", [P, T], i32)
        dst_end = sb("dst_end", [P, T], i32)
        dinv_d = sb("dinv_d", [P, T])
        w_s = sb("w_s", [P, T])
        own = sb("own", [P, T])
        counts = [sb(f"count{k}", [1, 2], i32) for k in range(LISTS + 1)]
        gi_i = sb("gi_i", [P, T], i32)
        srcS_i, dstS_i, srcS_end = sb("srcS_i", [P, T], i32), sb("dstS_i", [P, T], i32), sb("srcS_end", [P, T], i32)
        mask_d, mask_s = sb("mask_d", [C + 1, E], u8), sb("mask_s", [C + 1, E], u8)
        w3_sb, w4_sb = sb("w3_sb", [C, HID]), sb("w4_sb", [HID, C])
        w1_sb, w1u = sb("w1_sb", [ATTR, 3, HID]), sb("w1u", [HID, 1])
        w2_sb = sb("w2_sb", [HID, C])
        wl3_sb, wu_sb = sb("wl3_sb", [C, 2, C]), sb("wu_sb", [C, C])
        b3_sb, b1_sb, b1u, bl3_sb = sb("b3_sb", [HID, 1]), sb("b1_sb", [HID, 1]), sb("b1u", [HID, 1]), sb("bl3_sb", [C, 1])
        b4B, b2B, c0B = sb("b4B", [P, C]), sb("b2B", [P, C]), sb("c0B", [P, C])
        rat = sb("rat", [P, TERMS + 1])
        tB, uB, scale = sb("tB", [P, 1]), sb("uB", [HID, 1]), sb("scale", [P, 1])
        eps = sb("eps", [P, 1])
        one = sb("one", [P, 1])
        tri_k = sb("tri_k", [P, P])
        ones_pp, ones_t = sb("ones_pp", [P, P]), sb("ones_t", [P, T])
        nowhere = sb("nowhere", [P, 2 * U2])
        nowhere_i = sb("nowhere_i", [P, 2 * U2], i32)
        starts, starts_i = sb("starts", [1, CHUNKS]), sb("starts_i", [1, CHUNKS], i32)

        def brd(a, n, f=C):
            return a.unsqueeze(2).to_broadcast([P, n, f])

        def rows(a, n):
            return a.unsqueeze(1).to_broadcast([P, n, a.shape[-1]])

        def ln_centre(dve, link, X, s, xc, n):
            link(dve.tensor_reduce(out=s, in_=X, axis=AX.X, op=ALU.add))
            return dve.scalar_tensor_tensor(out=xc, in0=brd(s, n), scalar=-1.0 / C, in1=X, op0=ALU.mult, op1=ALU.add)

        def ln_square(act, xc, sq):
            return act.activation(sq, xc, ACT.Square)

        def ln_var(dve, sq, v):
            return dve.tensor_reduce(out=v, in_=sq, axis=AX.X, op=ALU.add)

        def ln_std(act, v, sd):
            return act.activation(sd, v, ACT.Sqrt, bias=eps[:, :], scale=1.0 / C)

        def ln_relu(dve, link, sd, rs, xc, h, n):
            link(dve.reciprocal(rs, sd))
            return dve.scalar_tensor_tensor(out=h, in0=xc, scalar=0.0, in1=brd(rs, n), op0=ALU.max, op1=ALU.mult)

        def fwd(pe, ps, X, f, last_sem):
            pe.sem_inc(pe_went_on, 1)
            for u in range(U):
                ins = pe.transpose(ps[0:f, u * P:(u + 1) * P], X[:, u, 0:f], ident[0:P, 0:P])
            ins.then_inc(last_sem, 1)

        def back(pe, ps, S, f, last_sem):
            pe.sem_inc(pe_went_on, 1)
            for u in range(U):
                ins = pe.transpose(ps[0:P, u * f:(u + 1) * f], S[0:f, u * P:(u + 1) * P], ident[0:f, 0:f])
            ins.then_inc(last_sem, 1)

        r3 = lambda a, n=U: a[:, :].rearrange("p (u f) -> p u f", u=n)

        def prows(ps, f=C):
            return ps[0:P, 0:U * f].rearrange("p (u f) -> p u f", f=f)

        with ExitStack() as st:
            sb, sem, sems = alloc(st)
            attr_sb = sb("attr_sb", [P, T, PAYW])
            dnx_i = sb("dnx_i", [P, T], i32)
            key = [sb("srcF", [P, T]), sb("dstF", [P, T])]
            hi, lo = [sb(f"hi{k}", [P, T]) for k in range(2)], [sb(f"lo{k}", [P, T]) for k in range(2)]
            q_i, tmp, tmp2 = sb("q_i", [P, T], i32), sb("tmp", [P, T]), sb("tmp2", [P, T])
            pos_f, pos_i = sb("pos_f", [P, T]), sb("pos_i", [P, T], i32)
            gi_f = sb("gi_f", [P, T])
            khl = sb("khl", [P, T, 3])
            khl_t = [sb(f"khl_t{b}", [P, 3]) for b in range(2)]
            occ, pos_t = ([sb(f"{n}{b}", [P, 1]) for b in range(2)] for n in ("occ", "pos_t"))
            iota_i, iota_lo, iota_hi = sb("iota_i", [P, ND], i32), sb("iota_lo", [P, ND], f16), sb("iota_hi", [P, P], f16)
            tri, tri_lt = tri_k, sb("tri_lt", [P, P])
            h0 = sb("h0", [HID, P])
            lo_hot = [[sb(f"lo_hot{k}{b}", [P, ND], f16) for b in range(2)] for k in range(2)]
            hi_hot = [[sb(f"hi_hot{k}{b}", [P, P], f16) for b in range(2)] for k in range(2)]
            place = sb("place", [P, ND])
            cnt, incl, ones = sb("cnt", [P, ND]), sb("incl", [P, ND]), sb("ones", [P, ND])
            dinv_n, endp_n = sb("dinv_n", [P, ND]), sb("endp_n", [P, ND])
            offs = sb("offs", [P, 1])
            hiT = [sb(f"hiT{b}", [P, P]) for b in range(2)]
            hd = [sb(f"hd{b}", [P, P]) for b in range(2)]
            h800 = sb("h800", [P, 1])
            eqj, eqk = ([sb(f"{n}{b}", [P, P]) for b in range(2)] for n in ("eqj", "eqk"))
            ttj = sb("ttj", [P, 2, HALF])
            node0 = sb("node0", [P, 1], i32)
            hist = [bank[0], bank[1], bank[2], bank[3]]

            loaded, built, stored = sem("loaded"), sem("built"), sem("stored")
            dlink = sem("dve_link")
            head_ready, c0_mm = sem("head_ready"), sem("c0_mm")
            hot_ready, hot_used, hist_done = sems("hot_ready"), sems("hot_used"), sem("hist_done")
            offs_in, offs_mm, place_ready = sem("offs_in"), sem("offs_mm"), sem("place_ready")
            place_mm = sem("place_mm")
            tabs_ready = sem("tabs_ready")
            v3 = lambda t: t[:, :].rearrange("p (a c) -> p a c", a=2)
            with nc.Block() as block:
                @block.sync
                def _(sp):
                    col = lambda a: a.rearrange("(n o) -> n o", o=1)
                    for dst_sb, a in (
                            (src_i[:, :], tile_major(src_pad[1:E + 1])), (dst_i[:, :], tile_major(dst_pad[1:E + 1])),
                            (dnx_i[:, :], tile_major(dst_pad[2:E + 2])), (attr_sb[:, :, 4:5], w.rearrange("(t p o) -> p t o", p=P, o=1)),
                            (attr_sb[:, :, 5:PAYW], attr.rearrange("(t p) a -> p t a", p=P)),
                            (w3_sb[:, :], w3t), (w4_sb[:, :], w4t), (w2_sb[:, :], w2),
                            (w1_sb[:, :, :], w1[0:3 * ATTR, :].rearrange("(s a) h -> a s h", s=3)),
                            (w1u[:, :], w1[3 * ATTR:3 * ATTR + 1, :].rearrange("o h -> h o")),
                            (wl3_sb[:, :, :], wl3.rearrange("(s c) o -> c s o", s=2)),
                            (b3_sb[:, :], col(b3)), (b1_sb[:, :], col(b1)), (bl3_sb[:, :], col(bl3)),
                            (b4B[:, :], b4.partition_broadcast(P)), (b2B[:, :], b2.partition_broadcast(P)),
                            (rat[:, :], ratios.partition_broadcast(P)), (tB[:, :], t_in.partition_broadcast(P)),
                            (uB[:, :], u_in[0, :].partition_broadcast(HID))):
                        sp.dma_start(dst_sb, a).then_inc(loaded, 16)
                    sp.wait_ge(tabs_ready, 2)
                    sp.dma_start(dinv_tab.rearrange("(p c) o -> p (c o)", p=P), dinv_n[:, :]).then_inc(stored, 16)
                    sp.dma_start(endp_tab.rearrange("(p c) o -> p (c o)", p=P), endp_n[:, :]).then_inc(stored, 16)
                    sp.wait_ge(stored, 32)

                NLOAD = 16 * 19

                @block.gpsimd
                def _(pool):
                    pool.memset(ident[:, :], 0.0).then_inc(built, 1)
                    pool.memset(tri[:, :], 1.0).then_inc(built, 1)
                    pool.memset(tri_lt[:, :], 1.0).then_inc(built, 1)
                    pool.iota(iota_i[:, :], pattern=[[1, ND]], base=0, channel_multiplier=0).then_inc(built, 1)
                    pool.iota(node0[:, :], pattern=[[1, 1]], base=0, channel_multiplier=ND).then_inc(built, 1)
                    pool.iota(nowhere_i[:, :], pattern=[[P, 2 * U2]], base=NOWHERE, channel_multiplier=1).then_inc(built, 1)
                    pool.iota(starts_i[:, :], pattern=[[2 * CE2, CHUNKS]], base=0, channel_multiplier=0).then_inc(built, 1)
                    pool.wait_ge(built, 7)
                    pool.affine_select(out=ident[:, :], in_=ident[:, :], compare_op=ALU.not_equal, fill=1.0, base=0,
                                       pattern=[[-1, 128]], channel_multiplier=1).then_inc(built, 1)
                    pool.affine_select(out=tri[:, :], in_=tri[:, :], compare_op=ALU.is_gt, fill=0.0, base=0,
                                       pattern=[[1, P]], channel_multiplier=-1).then_inc(built, 1)
                    pool.affine_select(out=tri_lt[:, :], in_=tri_lt[:, :], compare_op=ALU.is_gt, fill=0.0, base=0,
                                       pattern=[[-1, P]], channel_multiplier=1).then_inc(built, 1)

                @block.scalar
                def _(act):
                    act.wait_ge(hist_done, 1)
                    for a in range(2):
                        ins = act.activation(dinv_n[:, a * HALF:(a + 1) * HALF], hist[2 + a][0:P, 0:HALF], ACT.Sqrt, bias=one[:, :])
                    ins.then_inc(head_ready, 1)

                @block.tensor
                def _(pe):
                    pe.wait_ge(head_ready, 1)
                    pe.matmul(bank[4][0:P, 0:C], h0[:, :], w2_sb[:, :], start=True, stop=True).then_inc(c0_mm, 1)
                    with pe.Fori(0, T // 2 - 1) as j:
                        for b in range(2):
                            pe.wait_ge(hot_ready[b], j + 1)
                            for k in range(2):
                                for a in range(2):
                                    ins = pe.matmul(hist[2 * k + a][0:P, 0:HALF], hi_hot[k][b][:, :],
                                                    lo_hot[k][b][:, a * HALF:(a + 1) * HALF], start=False, stop=False,
                                                    skip_group_check=True)
                            ins.then_inc(hot_used[b], 1)
                    for b in range(2):
                        pe.wait_ge(hot_ready[b], T // 2)
                        for k in range(2):
                            for a in range(2):
                                ins = pe.matmul(hist[2 * k + a][0:P, 0:HALF], hi_hot[k][b][:, :],
                                                lo_hot[k][b][:, a * HALF:(a + 1) * HALF], start=False, stop=b == 1,
                                                skip_group_check=True)
                        if b == 0:
                            ins.then_inc(hot_used[b], 1)
                    ins.then_inc(hist_done, 1)
                    pe.wait_ge(offs_in, 1)
                    pe.matmul(bank[4][0:P, 128:129], tri[:, :], incl[:, ND - 1:ND], start=True, stop=True).then_inc(offs_mm, 1)

                @block.vector
                def _(dve):
                    ch = Chain(dve, dlink)
                    link = ch.link
                    for k in range(4):
                        link(dve.memset(hist[k][:, :], 0.0))
                    dve.memset(eps[:, :], EPS)
                    dve.memset(one[:, :], 1.0)
                    dve.memset(ones[:, :], 1.0)
                    dve.memset(ones_pp[:, :], 1.0)
                    dve.memset(ones_t[:, :], 1.0)
                    dve.wait_ge(loaded, NLOAD)
                    dve.wait_ge(built, 10)
                    dve.tensor_copy(iota_lo[:, :], iota_i[:, :])
                    dve.tensor_copy(iota_hi[:, :], iota_i[:, 0:P])
                    dve.tensor_copy(nowhere[:, :], nowhere_i[:, :])
                    dve.tensor_copy(starts[:, :], starts_i[:, :])
                    link(dve.tensor_copy(h800[:, :], node0[:, :]))
                    dve.tensor_tensor(out=wu_sb[:, :], in0=wl3_sb[:, 0, :], in1=wl3_sb[:, 1, :], op=ALU.subtract)
                    dve.tensor_scalar(scale[:, :], tB[:, :], 1e-8, -1.0 / N_SUB, ALU.max, ALU.mult)
                    link(dve.scalar_tensor_tensor(out=b1u[:, :], in0=w1u[:, :], scalar=uB[:, 0:1], in1=b1_sb[:, :],
                                                  op0=ALU.mult, op1=ALU.add))
                    dve.tensor_scalar(h0[:, :], b1u[:, 0:1].to_broadcast([HID, P]), 0.0, None, ALU.max).then_inc(head_ready, 1)
                    for k, key_i in enumerate((src_i, dst_i)):
                        link(dve.tensor_copy(key[k][:, :], key_i[:, :]))
                        link(dve.tensor_scalar(q_i[:, :], key[k][:, :], 1.0 / ND, None, ALU.mult))
                        link(dve.tensor_copy(hi[k][:, :], q_i[:, :]))
                        link(dve.scalar_tensor_tensor(out=lo[k][:, :], in0=hi[k][:, :], scalar=-float(ND), in1=key[k][:, :],
                                                      op0=ALU.mult, op1=ALU.add))
                        link(dve.tensor_scalar(tmp[:, :], lo[k][:, :], 0.0, None, ALU.is_lt))
                        link(dve.tensor_tensor(out=hi[k][:, :], in0=hi[k][:, :], in1=tmp[:, :], op=ALU.subtract))
                        link(dve.scalar_tensor_tensor(out=lo[k][:, :], in0=hi[k][:, :], scalar=-float(ND), in1=key[k][:, :],
                                                      op0=ALU.mult, op1=ALU.add))
                        link(dve.tensor_scalar(tmp[:, :], lo[k][:, :], float(ND), None, ALU.is_ge))
                        link(dve.tensor_tensor(out=hi[k][:, :], in0=hi[k][:, :], in1=tmp[:, :], op=ALU.add))
                        link(dve.scalar_tensor_tensor(out=lo[k][:, :], in0=hi[k][:, :], scalar=-float(ND), in1=key[k][:, :],
                                                      op0=ALU.mult, op1=ALU.add))
                    for i, a in enumerate((key[0], hi[0], lo[0])):
                        dve.tensor_copy(khl[:, :, i], a[:, :])
                    link(dve.tensor_tensor(out=tmp[:, :], in0=dst_i[:, :], in1=dnx_i[:, :], op=ALU.not_equal))
                    link(dve.scalar_tensor_tensor(out=tmp2[:, :], in0=key[1][:, :], scalar=-float(N), in1=tmp[:, :],
                                                  op0=ALU.add, op1=ALU.mult))
                    link(dve.tensor_scalar(dst_end[:, :], tmp2[:, :], float(N), None, ALU.add))
                    dve.memset(attr_sb[:, :, 2:4], 0.0)
                    dve.tensor_copy(attr_sb[:, :, 0], key[0][:, :])
                    dve.tensor_copy(attr_sb[:, :, 1], key[1][:, :])
                    link(dve.tensor_scalar(attr_sb[:, :, 4], attr_sb[:, :, 4], scale[:, 0:1], None, ALU.mult))
                    dve.wait_ge(c0_mm, 1)
                    link(dve.tensor_tensor(out=c0B[:, :], in0=bank[4][0:P, 0:C], in1=b2B[:, :], op=ALU.add))
                    with dve.Fori(0, T // 2) as j:
                        for b in range(2):
                            t = j * 2 + b
                            dve.wait_ge(hot_used[b], j)
                            for k in range(2):
                                dve.tensor_scalar(hi_hot[k][b][:, :], iota_hi[:, :], hi[k][:, bass.ds(t, 1)], None, ALU.is_equal)
                                ins = dve.tensor_scalar(lo_hot[k][b][:, :], iota_lo[:, :], lo[k][:, bass.ds(t, 1)], None, ALU.is_equal)
                            ins.then_inc(hot_ready[b], 1)
                    dve.wait_ge(hist_done, 1)
                    for a in range(2):
                        ins = dve.tensor_copy(cnt[:, a * HALF:(a + 1) * HALF], hist[a][0:P, 0:HALF])
                    link(ins)
                    dve.tensor_tensor_scan(incl[:, :], ones[:, :], cnt[:, :], 0.0, ALU.mult, ALU.add).then_inc(offs_in, 1)
                    dve.wait_ge(offs_mm, 1)
                    link(dve.tensor_copy(offs[:, :], bank[4][0:P, 128:129]))
                    link(dve.tensor_scalar(endp_n[:, :], incl[:, :], offs[:, 0:1], None, ALU.add))
                    link(dve.tensor_tensor(out=place[:, :], in0=endp_n[:, :], in1=cnt[:, :], op=ALU.subtract))
                    link(dve.tensor_scalar(cnt[:, :], cnt[:, :], 0.0, None, ALU.is_gt))
                    link(dve.scalar_tensor_tensor(out=endp_n[:, :], in0=endp_n[:, :], scalar=-float(E + 1), in1=cnt[:, :],
                                                  op0=ALU.add, op1=ALU.mult))
                    dve.tensor_scalar(endp_n[:, :], endp_n[:, :], float(E), None, ALU.add).then_inc(tabs_ready, 1)
                    dve.wait_ge(head_ready, 2)
                    dve.reciprocal(dinv_n[:, :], dinv_n[:, :]).then_inc(tabs_ready, 1)

            with ExitStack() as s2:
                sb, sem, sems = alloc(s2)
                src_b = [sb(f"src_b{b}", [P, P], i32) for b in range(2)]
                src_bf = [sb(f"src_bf{b}", [P, P]) for b in range(2)]
                src_loaded, src_free = sems("src_loaded"), sems("src_free")
                hots_ready, sel_done, pos_done = sems("hots_ready"), sems("sel_done"), sem("pos_done")
                place_copied, place_added = sem("place_copied"), sem("place_added")
                dl = sem("place_link")
                run, sel = two[0], [two[1], two[2]]
                with nc.Block() as block:
                    @block.sync
                    def _(sp):
                        with sp.Fori(0, T // 2) as j:
                            for b in range(2):
                                sp.wait_ge(src_free[b], j)
                                sp.dma_start(src_b[b][:, :], src_pad[bass.ds((j * 2 + b) * P + 1, P)].partition_broadcast(P))\
                                  .then_inc(src_loaded[b], 16)

                    @block.tensor
                    def _(pe):
                        for a in range(2):
                            ins = pe.matmul(run[0:P, a, 0:HALF], ident[0:P, 0:P], place[:, a * HALF:(a + 1) * HALF],
                                            start=True, stop=False, skip_group_check=True)
                        ins.then_inc(place_added, 1)
                        with pe.Fori(0, T // 2) as j:
                            for b in range(2):
                                pe.wait_ge(hots_ready[b], j + 1)
                                pe.wait_ge(place_copied, j * 2 + b + 1)
                                for a in range(2):
                                    ins = pe.matmul(sel[b][0:P, a, 0:HALF], hiT[b][:, :], place[:, a * HALF:(a + 1) * HALF],
                                                    start=True, stop=True)
                                ins.then_inc(sel_done[b], 1)
                                for a in range(2):
                                    ins = pe.matmul(run[0:P, a, 0:HALF], hi_hot[0][b][:, :], lo_hot[0][b][:, a * HALF:(a + 1) * HALF],
                                                    start=False, stop=False, skip_group_check=True)
                                ins.then_inc(place_added, 1)

                    @block.scalar
                    def _(act):
                        with act.Fori(0, T // 2) as j:
                            for b in range(2):
                                act.wait_ge(place_added, j * 2 + b + 1)
                                act.activation(place[:, :].rearrange("p (a c) -> p a c", a=2), run[0:P, :, 0:HALF], ACT.Copy)\
                                   .then_inc(place_copied, 1)

                    @block.vector
                    def _(dve):
                        def one_hots(link, b, t, j):
                            dve.wait_ge(src_loaded[b], j * 16 + 16)
                            dve.tensor_copy(src_bf[b][:, :], src_b[b][:, :])
                            link(dve.tensor_copy(khl_t[b][:, :], khl[:, bass.ds(t, 1), :]))
                            link(dve.tensor_scalar(hd[b][:, :], src_bf[b][:, :], h800[:, 0:1], None, ALU.subtract))
                            link(dve.tensor_scalar(eqj[b][:, :], hd[b][:, :], float(ND), None, ALU.is_lt))
                            dve.scalar_tensor_tensor(out=hiT[b][:, :], in0=hd[b][:, :], scalar=0.0, in1=eqj[b][:, :],
                                                     op0=ALU.is_ge, op1=ALU.mult).then_inc(src_free[b], 1)
                            dve.tensor_scalar(hi_hot[0][b][:, :], iota_hi[:, :], khl_t[b][:, 1:2], None, ALU.is_equal)
                            dve.tensor_scalar(lo_hot[0][b][:, :], iota_lo[:, :], khl_t[b][:, 2:3], None, ALU.is_equal)\
                               .then_inc(hots_ready[b], 1)
                            link(dve.scalar_tensor_tensor(out=eqk[b][:, :], in0=src_bf[b][:, :], scalar=khl_t[b][:, 0:1],
                                                          in1=tri_lt[:, :], op0=ALU.is_equal, op1=ALU.mult,
                                                          accum_out=occ[b][:, :]))

                        def places(link, b, t, j):
                            dve.wait_ge(sel_done[b], j + 1)
                            link(dve.tensor_tensor_reduce(out=ttj[:, :, :], in0=v3(lo_hot[0][b]), in1=sel[b][0:P, :, 0:HALF],
                                                          scale=1.0, scalar=occ[b][:, 0:1], op0=ALU.mult, op1=ALU.add,
                                                          accum_out=pos_t[b][:, :]))
                            dve.tensor_copy(pos_f[:, bass.ds(t, 1)], pos_t[b][:, :]).then_inc(pos_done, 1)

                        LAST = T // 2 - 1
                        ch = Chain(dve, dl)
                        one_hots(ch.link, 0, 0, 0)
                        n0 = ch.n
                        KB = n0 + 1
                        with dve.Fori(0, LAST) as j:
                            ch = Chain(dve, dl, j * (2 * KB) + n0)
                            dve.wait_ge(place_added, j * 2 + 1)
                            one_hots(ch.link, 1, j * 2 + 1, j)
                            places(ch.link, 0, j * 2, j)
                            dve.wait_ge(place_added, j * 2 + 2)
                            one_hots(ch.link, 0, j * 2 + 2, j + 1)
                            places(ch.link, 1, j * 2 + 1, j)
                            assert ch.n == 2 * KB
                        ch = Chain(dve, dl, LAST * 2 * KB + n0)
                        dve.wait_ge(place_added, T - 1)
                        one_hots(ch.link, 1, T - 1, LAST)
                        places(ch.link, 0, T - 2, LAST)
                        places(ch.link, 1, T - 1, LAST)
                        dve.wait_ge(pos_done, T)
                        ch.link(dve.tensor_copy(pos_i[:, :], pos_f[:, :]))

            with ExitStack() as s2:
                sb, sem, sems = alloc(s2)
                ixd, ixp, ixs = ([sb(f"{n}{b}", [P, U], i32) for b in range(2)] for n in ("ixd", "ixp", "ixs"))
                gv = [sb(f"gv{b}", [P, 2 * U]) for b in range(2)]
                rec = [sb(f"rec{b}", [P, U * PAYW]) for b in range(2)]
                sentinel = sb("sentinel", [1, 2])
                got, sent = sems("got"), sems("sent")
                begun, pads, rlink = sem("begun"), sem("pads"), sem("record_link")
                GC = 2 * U
                GN = ND // GC
                X, XB, Q, XO, XOC, H1, H2, O = ([sb(f"dn_{n}{b}", [P, GC * C]) for b in range(2)] for n in (
                    "x", "xb", "q", "x1", "x1c", "h", "h2", "o"))
                XC, SQ = [sb(f"dn_xc{i}", [P, GC * C]) for i in range(2)], [sb(f"dn_sq{i}", [P, GC * C]) for i in range(2)]
                s_, v_, sd_, rs_ = ([sb(f"dn_{n}{i}", [P, GC]) for i in range(2)] for n in ("sum", "var", "std", "rstd"))
                HT, Z = [sb(f"dn_hT{h}", [C, CE]) for h in range(2)], [sb(f"dn_z{h}", [HID, CE]) for h in range(2)]
                x_in, q_stored, x1_stored, o_stored = sems("x_in"), sems("q_stored"), sems("x1_stored"), sems("o_stored")
                centred, squared, var_r, std_r, h_r = sems("centred"), sems("squared"), sems("var_r"), sems("std_r"), sem("h_r")
                hT_mm, hT_r, z_mm, z_r, q_mm = sem("hT_mm"), sem("hT_r"), sem("z_mm"), sem("z_r"), sem("q_mm")
                xb_r, q_r, x1_r, o_r, dl = sem("xb_r"), sem("q_r"), sem("x1_r"), sem("o_r"), sem("dense_link")
                rG = lambda a: r3(a, GC)
                node_cols = lambda a, g: a.rearrange("(p c) f -> p c f", p=P)[:, bass.ds(g * GC, GC), :]

                def exists(m, k):
                    return not isinstance(m, int) or 0 <= 2 * m + k < GN

                def run(eng, turn):
                    turn(0, -1)
                    turn(0, 0)
                    turn(0, 1)
                    with eng.Fori(0, GN // 2 - 2) as j:
                        turn(j + 1, 0)
                        turn(j + 1, 1)
                    for k in range(4):
                        turn(GN // 2 - 1, k)

                with nc.Block() as block:
                    @block.gpsimd
                    def _(pool):
                        pool.memset(sentinel[:, :], -1.0).then_inc(begun, 1)
                        LINKS = 8
                        with pool.Fori(0, PAIRS) as j:
                            ch = Chain(pool, rlink, j * LINKS)
                            for b in range(2):
                                cols = bass.ds((j * 2 + b) * U, U)
                                pool.wait_ge(sent[b], j * 16 * U)
                                pool.sem_inc(pool_went_on, 1)
                                pool.tensor_copy(ixs[b][:, :], src_i[:, cols])
                                pool.tensor_copy(ixp[b][:, :], pos_i[:, cols])
                                ch.link(pool.tensor_copy(ixd[b][:, :], dst_i[:, cols]))
                                pool.sem_inc(pool_went_on, 1)
                                for u in range(U):
                                    for i, ix in enumerate((ixd, ixs)):
                                        pool.indirect_dma_start(out=gv[b][:, i * U + u:i * U + u + 1], out_offset=None, in_=endp_tab,
                                                                in_offset=bass.IndirectOffsetOnAxis(ap=ix[b][:, u:u + 1], axis=0))\
                                            .then_inc(got[b], 16)
                                ch.link(pool.tensor_copy(r3(rec[b]), attr_sb[:, cols, :]))
                            for b in range(2):
                                pool.wait_ge(got[b], j * (32 * U) + 32 * U)
                                pool.sem_inc(pool_went_on, 1)
                                ch.put(pool.tensor_copy(r3(rec[b])[:, :, 2], gv[b][:, 0:U]))
                                ch.link(pool.tensor_copy(r3(rec[b])[:, :, 3], gv[b][:, U:2 * U]))
                                pool.sem_inc(pool_went_on, 1)
                                for u in range(U):
                                    pool.indirect_dma_start(out=pay, out_offset=bass.IndirectOffsetOnAxis(ap=ixp[b][:, u:u + 1], axis=0),
                                                            in_=rec[b][:, u * PAYW:(u + 1) * PAYW], in_offset=None)\
                                        .then_inc(sent[b], 16)
                            assert ch.n == LINKS, ch.n
                        for b in range(2):
                            pool.wait_ge(sent[b], 16 * U * PAIRS)

                    @block.sync
                    def _(sp):
                        sp.wait_ge(begun, 1)
                        sp.dma_start(srcs_pad[0:1].rearrange("(o n) -> o n", o=1), sentinel[0:1, 0:1]).then_inc(pads, 16)
                        sp.dma_start(srcs_pad[E + 1:E + 2].rearrange("(o n) -> o n", o=1), sentinel[0:1, 1:2]).then_inc(pads, 16)
                        sp.wait_ge(pads, 32)
                        sp.dma_start(rG(X[0]), node_cols(x, 0)).then_inc(x_in[0], 16)

                        def turn(m, k):
                            if exists(m, k + 2):
                                b = k % 2
                                if exists(m, k):
                                    sp.wait_ge(xb_r, 2 * m + k + 1)
                                    sp.wait_ge(centred[0], 2 * m + k + 1)
                                sp.dma_start(rG(X[b]), node_cols(x, 2 * m + k + 2)).then_inc(x_in[b], 16)
                            if exists(m, k - 1):
                                b = (k - 1) % 2
                                sp.wait_ge(q_r, 2 * m + k)
                                sp.dma_start(node_cols(qs, 2 * m + k - 1), rG(Q[b])).then_inc(q_stored[b], 16)
                            if exists(m, k - 2):
                                b = k % 2
                                sp.wait_ge(o_r, 2 * m + k - 1)
                                sp.dma_start(node_cols(out, 2 * m + k - 2), rG(O[b])).then_inc(o_stored[b], 16)
                            if exists(m, k - 1):
                                b = (k - 1) % 2
                                sp.wait_ge(x1_r, 2 * m + k)
                                sp.dma_start(node_cols(x1, 2 * m + k - 1), rG(XO[b])).then_inc(x1_stored[b], 16)

                        run(sp, turn)
                        for stored in (q_stored, x1_stored, o_stored):
                            for b in range(2):
                                sp.wait_ge(stored[b], 16 * (GN // 2))

                    @block.vector
                    def _(dve):
                        LINKS = 5
                        linked = {-1: 0}

                        def turn(m, k):
                            if isinstance(m, int):
                                base = linked[2 * m + k]
                            else:
                                base = (m - 1) * (2 * LINKS) + linked[2] + k * LINKS
                            ch = Chain(dve, dl, base)
                            if exists(m, k):
                                dve.wait_ge(squared[0], 2 * m + k + 1)
                                ln_var(dve, rG(SQ[0]), v_[0][:, :]).then_inc(var_r[0], 1)
                            if exists(m, k - 2):
                                dve.wait_ge(squared[1], 2 * m + k - 1)
                                ln_var(dve, rG(SQ[1]), v_[1][:, :]).then_inc(var_r[1], 1)
                            if exists(m, k):
                                dve.wait_ge(std_r[0], 2 * m + k + 1)
                                if exists(m, k - 2):
                                    dve.wait_ge(hT_mm, (2 * m + k - 1) * 2)
                                ln_relu(dve, ch.link, sd_[0][:, :], rs_[0][:, :], rG(XC[0]), rG(H1[k % 2]), GC).then_inc(h_r, 1)
                            if exists(m, k - 2):
                                b = k % 2
                                dve.wait_ge(std_r[1], 2 * m + k - 1)
                                ch.link(ln_relu(dve, ch.link, sd_[1][:, :], rs_[1][:, :], rG(XC[1]), rG(H2[b]), GC))
                                if exists(m, k - 4):
                                    dve.wait_ge(o_stored[b], (m + (k - 4) // 2) * 16 + 16)
                                dve.tensor_tensor(out=O[b][:, :], in0=H2[b][:, :], in1=XOC[b][:, :], op=ALU.add).then_inc(o_r, 1)
                            if exists(m, k - 1):
                                b = (k - 1) % 2
                                dve.wait_ge(q_r, 2 * m + k)
                                dve.wait_ge(xb_r, 2 * m + k)
                                if exists(m, k - 3):
                                    dve.wait_ge(x1_stored[b], (m + (k - 3) // 2) * 16 + 16)
                                dve.tensor_tensor(out=XO[b][:, :], in0=XB[b][:, :], in1=Q[b][:, :], op=ALU.add).then_inc(x1_r, 1)
                            if exists(m, k + 1):
                                b = (k + 1) % 2
                                dve.wait_ge(x_in[b], (m + (k + 1) // 2) * 16 + 16)
                                summed = ch.put(dve.tensor_reduce(out=s_[0][:, :], in_=rG(X[b]), axis=AX.X, op=ALU.add))
                                if exists(m, k - 1):
                                    dve.wait_ge(x1_r, 2 * m + k)
                                dve.tensor_tensor(out=rG(XB[b]), in0=rG(X[b]), in1=rows(b4B[:, :], GC), op=ALU.add).then_inc(xb_r, 1)
                                ch.need(summed)
                                dve.scalar_tensor_tensor(out=rG(XC[0]), in0=brd(s_[0][:, :], GC), scalar=-1.0 / C, in1=rG(X[b]),
                                                         op0=ALU.mult, op1=ALU.add).then_inc(centred[0], 1)
                            if exists(m, k - 1):
                                b = (k - 1) % 2
                                dve.wait_ge(x1_r, 2 * m + k)
                                summed = ch.put(dve.tensor_reduce(out=s_[1][:, :], in_=rG(XO[b]), axis=AX.X, op=ALU.add))
                                dve.tensor_tensor(out=rG(XOC[b]), in0=rG(XO[b]), in1=rows(c0B[:, :], GC), op=ALU.add)
                                ch.need(summed)
                                dve.scalar_tensor_tensor(out=rG(XC[1]), in0=brd(s_[1][:, :], GC), scalar=-1.0 / C, in1=rG(XO[b]),
                                                         op0=ALU.mult, op1=ALU.add).then_inc(centred[1], 1)
                            if isinstance(m, int):
                                linked[2 * m + k + 1] = base + ch.n
                                if m == 0 and k == 1:
                                    linked[GN - 2] = base + ch.n + (GN - 4) * LINKS
                            assert isinstance(m, int) or ch.n == LINKS, ch.n

                        run(dve, turn)

                    @block.scalar
                    def _(act):
                        def turn(m, k):
                            if exists(m, k):
                                act.wait_ge(var_r[0], 2 * m + k + 1)
                                ln_std(act, v_[0][:, :], sd_[0][:, :]).then_inc(std_r[0], 1)
                            if exists(m, k - 2):
                                act.wait_ge(var_r[1], 2 * m + k - 1)
                                ln_std(act, v_[1][:, :], sd_[1][:, :]).then_inc(std_r[1], 1)
                            if exists(m, k - 1):
                                b = (k - 1) % 2
                                act.wait_ge(q_mm, 2 * m + k)
                                if exists(m, k - 3):
                                    act.wait_ge(q_stored[b], (m + (k - 3) // 2) * 16 + 16)
                                act.activation(Q[b][:, :], bank[4][0:P, 0:GC * C], ACT.Copy).then_inc(q_r, 1)
                            if exists(m, k):
                                for h in range(2):
                                    act.wait_ge(hT_mm, (2 * m + k) * 2 + h + 1)
                                    act.activation(HT[h][:, :], bank[h][0:C, 0:CE], ACT.Copy).then_inc(hT_r, 1)
                            if exists(m, k + 1):
                                act.wait_ge(centred[0], 2 * m + k + 2)
                                ln_square(act, XC[0][:, :], SQ[0][:, :]).then_inc(squared[0], 1)
                            if exists(m, k):
                                for h in range(2):
                                    act.wait_ge(z_mm, (2 * m + k) * 2 + h + 1)
                                    act.activation(Z[h][:, :], bank[2 + h][0:HID, 0:CE], ACT.Relu, bias=b3_sb[:, :]).then_inc(z_r, 1)
                            if exists(m, k - 1):
                                act.wait_ge(centred[1], 2 * m + k)
                                ln_square(act, XC[1][:, :], SQ[1][:, :]).then_inc(squared[1], 1)

                        run(act, turn)

                    @block.tensor
                    def _(pe):
                        def turn(m, k):
                            if not exists(m, k):
                                return
                            pe.wait_ge(h_r, 2 * m + k + 1)
                            for h in range(2):
                                fwd(pe, bank[h], rG(H1[k % 2])[:, h * U:(h + 1) * U, :], C, hT_mm)
                            for h in range(2):
                                pe.wait_ge(hT_r, (2 * m + k) * 2 + h + 1)
                                pe.matmul(bank[2 + h][0:HID, 0:CE], w3_sb[:, :], HT[h][:, :], start=True, stop=True).then_inc(z_mm, 1)
                            for h in range(2):
                                pe.wait_ge(z_r, (2 * m + k) * 2 + h + 1)
                                for u in range(U):
                                    ins = pe.matmul(bank[4][0:P, (h * U + u) * C:(h * U + u + 1) * C], Z[h][:, u * P:(u + 1) * P], w4_sb[:, :],
                                                    start=True, stop=True)
                            ins.then_inc(q_mm, 1)

                        run(pe, turn)


        def gather(pool, rows_sb, f, table, ix, sem_):
            for u in range(U):
                pool.indirect_dma_start(out=rows_sb[:, u * f:(u + 1) * f], out_offset=None, in_=table,
                                        in_offset=bass.IndirectOffsetOnAxis(ap=ix[:, u:u + 1], axis=0)).then_inc(sem_, 16)

        def scatter(pool, table, ix, rows_sb, f, sem_, limit=N):
            for u in range(U):
                pool.indirect_dma_start(out=table, out_offset=bass.IndirectOffsetOnAxis(ap=ix[:, u:u + 1], axis=0),
                                        in_=rows_sb[:, u * f:(u + 1) * f], in_offset=None,
                                        bounds_check=limit - 1, oob_is_err=False).then_inc(sem_, 16)

        def list_count(dve, link, n, fits, pairs_f, count):
            link(dve.tensor_scalar(fits, starts[0:1, :], n, 0.0, ALU.is_lt, ALU.add, accum_out=pairs_f))
            dve.tensor_copy(count[0:1, 1:2], n)
            link(dve.tensor_scalar(count[0:1, 0:1], pairs_f, 1.0, None, ALU.max))

        def pair_of_scans(b, j, s_r):
            return (s_r[1], j) if b == 0 else (s_r[0], j + 1)


        with ExitStack() as st:
            sb, sem, sems = alloc(st)
            cur = [[sb(f"cur{k}{b}", [C + 1, CE], dt) for b in range(2)] for k, dt in enumerate((i32, f32))]
            prv = [[sb(f"prv{k}{b}", [C + 1, CE], dt) for b in range(2)] for k, dt in enumerate((i32, f32))]
            recs, nxt = sb("recs", [P, T, 5]), sb("nxt", [P, T])
            tmp, tmp2 = sb("tmp_m", [P, T]), sb("tmp_m2", [P, T])
            zeros, none = sb("zeros", [P, TW]), sb("none", [P, 4])
            actv, pre, incl2, base_f, ixl = (sb(n, [P, T], i32 if n == "ixl" else f32) for n in ("actv", "pre", "incl2", "base_f", "ixl"))
            first, filled, act_r, pre_mm, list_r = sem("fill_ready"), sem("filled"), sem("actv_ready"), sem("pre_mm"), sem("list_ready")
            ixl_t = [sb(f"ixl_t{b}", [P, U], i32) for b in range(2)]
            lrec = [sb(f"lrec{b}", [P, U * 4]) for b in range(2)]
            lr_r, lr_sent, lk = sems("lrec_ready"), sems("lrec_sent"), sem("lrec_link")
            keys_in, keys_used, recs_in, stored, dl = sems("keys_in"), sems("keys_used"), sem("recs_in"), sem("srcs_stored"), sem("mask_link")
            with nc.Block() as block:
                @block.sync
                def _(sp):
                    sp.wait_ge(first, 2)
                    part = lambda a: a.rearrange("(p c) f -> p c f", p=P)
                    for table in (*terms, series):
                        n = table.shape[1]
                        sp.dma_start(part(table), zeros[:, 0:n].unsqueeze(1).to_broadcast([P, NR // P, n])).then_inc(filled, 16)
                    for table in lists.values():
                        sp.dma_start(part(table), none[:, :].unsqueeze(1).to_broadcast([P, NR // P, 4])).then_inc(filled, 16)
                    sp.wait_ge(filled, 16 * (4 + len(lists)))
                    sp.dma_start(recs[:, :, :], pay[:, 0:5].rearrange("(t p) a -> p t a", p=P)).then_inc(recs_in, 16)
                    sp.wait_ge(recs_in, 16)
                    sp.dma_start(tile_major(srcs_pad[1:E + 1]), recs[:, :, 0]).then_inc(stored, 16)
                    sp.wait_ge(stored, 16)
                    sp.dma_start(nxt[:, :], tile_major(srcs_pad[2:E + 2])).then_inc(recs_in, 16)
                    with sp.Fori(0, PAIRS) as j:
                        for b in range(2):
                            c = j * 2 + b
                            sp.wait_ge(keys_used[b], j)
                            for k, a in enumerate((dst_pad, srcs_pad)):
                                sp.dma_start(cur[k][b][:, :], a[bass.ds(c * CE + 1, CE)].partition_broadcast(C + 1)).then_inc(keys_in[b], 16)
                                sp.dma_start(prv[k][b][:, :], a[bass.ds(c * CE, CE)].partition_broadcast(C + 1)).then_inc(keys_in[b], 16)

                @block.vector
                def _(dve):
                    with dve.Fori(0, PAIRS) as j:
                        for b in range(2):
                            c = j * 2 + b
                            dve.wait_ge(keys_in[b], j * 64 + 64)
                            for k, m in enumerate((mask_d, mask_s)):
                                ins = dve.tensor_tensor(out=m[:, bass.ds(c * CE, CE)], in0=cur[k][b][:, :], in1=prv[k][b][:, :], op=ALU.is_equal)
                            ins.then_inc(keys_used[b], 1)
                    dve.wait_ge(recs_in, 32)
                    ch = Chain(dve, dl)
                    dve.tensor_copy(srcS_i[:, :], recs[:, :, 0])
                    dve.tensor_copy(dstS_i[:, :], recs[:, :, 1])
                    dve.tensor_copy(gi_i[:, :], recs[:, :, 2])
                    dve.tensor_copy(w_s[:, :], recs[:, :, 4])
                    dve.tensor_copy(own[:, :], recs[:, :, 3])
                    ch.link(dve.tensor_tensor(out=tmp[:, :], in0=recs[:, :, 0], in1=nxt[:, :], op=ALU.not_equal))
                    ch.link(dve.scalar_tensor_tensor(out=tmp2[:, :], in0=recs[:, :, 0], scalar=-float(N), in1=tmp[:, :],
                                                     op0=ALU.add, op1=ALU.mult))
                    ch.link(dve.tensor_scalar(srcS_end[:, :], tmp2[:, :], float(N), None, ALU.add))
                    ch.link(dve.tensor_scalar(actv[:, :], recs[:, :, 2], float(E), None, ALU.is_lt))
                    dve.memset(incl2[:, :], 0.0).then_inc(act_r, 1)
                    dve.wait_ge(pre_mm, 1)
                    ch.link(dve.tensor_copy(pre[:, :], bank[0][0:P, 0:T]))
                    ch.link(dve.tensor_copy(base_f[:, :], bank[1][0:P, 0:T]))
                    ch.link(dve.tensor_tensor_scan(incl2[:, :], ones_t[:, :], base_f[:, :], 0.0, ALU.mult, ALU.add))
                    list_count(dve, ch.link, incl2[0:1, T - 1:T], tmp[0:1, 0:CHUNKS], tmp[0:1, CHUNKS:CHUNKS + 1], counts[2])
                    ch.link(dve.tensor_tensor(out=base_f[:, :], in0=incl2[:, :], in1=base_f[:, :], op=ALU.subtract))
                    ch.link(dve.tensor_tensor(out=pre[:, :], in0=pre[:, :], in1=base_f[:, :], op=ALU.add))
                    ch.link(dve.tensor_scalar(tmp[:, :], pre[:, :], 1.0, nowhere[:, 0:1], ALU.add, ALU.subtract))
                    ch.link(dve.tensor_tensor(out=tmp[:, :], in0=tmp[:, :], in1=actv[:, :], op=ALU.mult))
                    ch.link(dve.tensor_scalar(ixl[:, :], tmp[:, :], nowhere[:, 0:1], None, ALU.add))
                    with dve.Fori(0, PAIRS) as j:
                        for b in range(2):
                            cols = bass.ds((j * 2 + b) * U, U)
                            dve.wait_ge(lr_sent[b], j * (16 * U))
                            dve.tensor_copy(ixl_t[b][:, :], ixl[:, cols])
                            dve.tensor_copy(r3(lrec[b])[:, :, 0], recs[:, cols, 3])
                            dve.tensor_copy(r3(lrec[b])[:, :, 1], recs[:, cols, 2])
                            dve.tensor_copy(r3(lrec[b])[:, :, 2], recs[:, cols, 4])
                            dve.tensor_copy(r3(lrec[b])[:, :, 3], recs[:, cols, 4]).then_inc(lr_r[b], 1)

                @block.tensor
                def _(pe):
                    pe.wait_ge(act_r, 1)
                    pe.matmul(bank[0][0:P, 0:T], tri_k[:, :], actv[:, :], start=True, stop=True)
                    pe.matmul(bank[1][0:P, 0:T], ones_pp[:, :], actv[:, :], start=True, stop=True).then_inc(pre_mm, 1)

                @block.gpsimd
                def _(pool):
                    pool.memset(zeros[:, :], 0.0).then_inc(first, 1)
                    pool.memset(none[:, :], 0.0).then_inc(lk, 1)
                    pool.wait_ge(lk, 1)
                    pool.memset(none[:, 0:1], -1.0).then_inc(lk, 1)
                    pool.wait_ge(lk, 2)
                    pool.memset(none[:, 1:2], float(E)).then_inc(first, 1)
                    with pool.Fori(0, PAIRS) as j:
                        for b in range(2):
                            pool.wait_ge(lr_r[b], j + 1)
                            pool.sem_inc(pool_went_on, 1)
                            scatter(pool, lists[2], ixl_t[b], lrec[b], 4, lr_sent[b], E + 1)
                    for b in range(2):
                        pool.wait_ge(lr_sent[b], 16 * U * PAIRS)

        with ExitStack() as st:
            sb, sem, sems = alloc(st)
            XD, QSD = sb("x_dst", [P, T, C]), sb("qs_dst", [P, T, C])
            with ExitStack() as s2:
                sb, sem, sems = alloc(s2)
                F1 = C + 1
                G, XC, SQ, H = ([sb(f"c1_{n}{b}", [P, 2 * U * C]) for b in range(2)] for n in ("g", "xc", "sq", "h"))
                s_, v_, sd_, rs_ = ([sb(f"c1_{n}{b}", [P, 2 * U]) for b in range(2)] for n in ("sum", "var", "std", "rstd"))
                dv, M = [sb(f"c1_dv{b}", [P, U]) for b in range(2)], [sb(f"c1_m{b}", [P, U * F1]) for b in range(2)]
                S, AT, Z = [sb(f"c1_s{b}", [F1, CE]) for b in range(2)], [sb(f"c1_aT{b}", [C, CE]) for b in range(2)], [sb(f"c1_z{b}", [HID, CE]) for b in range(2)]
                A, QO = [sb(f"c1_a{b}", [P, U * C]) for b in range(2)], [sb(f"c1_q{b}", [P, U * C]) for b in range(2)]
                dd, dq = [sb(f"c1_dd{b}", [P, U]) for b in range(2)], [sb(f"c1_dq{b}", [P, U]) for b in range(2)]
                ixs, ixd, ixe = ([sb(f"c1_{n}{b}", [P, U], i32) for b in range(2)] for n in ("ixs", "ixd", "ixe"))
                ix_r, got, centred, squared, var_r, std_r, m_r = (sems(f"c1_{n}") for n in ("ix_ready", "gathered", "centred", "squared", "var", "std", "messages"))
                mT, s_r, s_back, cnt_r, a_r, aT_mm, aT_r, z_mm, z_r, q_mm, q_r, sent = (sems(f"c1_{n}") for n in (
                    "mT", "scanned", "sums_back", "count", "agg", "aT_mm", "aT", "z_mm", "z", "q_mm", "q", "sent"))
                ixe_r, x_kept = sems("c1_ixe"), sems("c1_x_kept")
                dl, m1 = sem("c1_link"), sem("c1_ones")
                with nc.Block() as block:
                    @block.gpsimd
                    def _(pool):
                        def gathers(b, j):
                            pool.wait_ge(ix_r[b], j + 1)
                            pool.wait_ge(m_r[b], j)
                            pool.wait_ge(x_kept[b], j)
                            pool.sem_inc(pool_went_on, 1)
                            gather(pool, G[b], C, x, ixs[b], got[b])
                            gather(pool, G[b][:, U * C:], C, x, ixd[b], got[b])
                            gather(pool, dv[b], 1, dinv_tab, ixs[b], got[b])
                        def scatters(b, j):
                            pool.wait_ge(q_r[b], j * 2 + 1)
                            pool.wait_ge(ixe_r[b], j + 1)
                            pool.sem_inc(pool_went_on, 1)
                            scatter(pool, qs, ixe[b], QO[b], C, sent[b])
                        with pool.Fori(0, PAIRS) as j:
                            gathers(0, j)
                            gathers(1, j)
                            scatters(0, j)
                            scatters(1, j)
                        for b in range(2):
                            pool.wait_ge(sent[b], 16 * U * PAIRS)

                    @block.vector
                    def _(dve):
                        for b in range(2):
                            dve.memset(M[b][:, :], 1.0)
                            ins = dve.memset(S[b][:, :], 0.0)
                        ins.then_inc(m1, 1)
                        dve.wait_ge(m1, 1)
                        K = 2 * 5
                        with dve.Fori(0, PAIRS) as j:
                            ch = Chain(dve, dl, j * K)
                            for b in range(2):
                                dve.wait_ge(got[b], j * (48 * U) + 48 * U)
                                ln_centre(dve, ch.link, r3(G[b], 2 * U), s_[b][:, :], r3(XC[b], 2 * U), 2 * U).then_inc(centred[b], 1)
                                dve.wait_ge(squared[b], j + 1)
                                ln_var(dve, r3(SQ[b], 2 * U), v_[b][:, :]).then_inc(var_r[b], 1)
                                dve.wait_ge(std_r[b], j + 1)
                                ch.link(ln_relu(dve, ch.link, sd_[b][:, :], rs_[b][:, :], r3(XC[b], 2 * U), r3(H[b], 2 * U), 2 * U))
                                dve.tensor_tensor(out=r3(M[b])[:, :, 0:C], in0=r3(H[b], 2 * U)[:, 0:U, :], in1=brd(dv[b][:, :], U), op=ALU.mult)\
                                   .then_inc(m_r[b], 1)
                                dve.wait_ge(mT[b], j + 1)
                                dve.wait_ge(*pair_of_scans(b, j, s_r))
                                dve.tensor_tensor_scan(S[b][:, :], mask_d[:, bass.ds((j * 2 + b) * CE, CE)], bank[4 * b][0:F1, 0:CE],
                                                       S[1 - b][:, CE - 1:CE], ALU.mult, ALU.add).then_inc(s_r[b], 1)
                                dve.wait_ge(cnt_r[b], j + 1)
                                ch.link(dve.reciprocal(dd[b][:, :], dq[b][:, :]))
                                dve.tensor_copy(dinv_d[:, bass.ds((j * 2 + b) * U, U)], dd[b][:, :])
                                ch.link(dve.tensor_tensor(out=r3(A[b]), in0=r3(H[b], 2 * U)[:, U:2 * U, :], in1=brd(dd[b][:, :], U), op=ALU.mult))
                                dve.tensor_tensor(out=r3(A[b]), in0=r3(A[b]), in1=prows(bank[4 * b + 1], F1)[:, :, 0:C], op=ALU.add).then_inc(a_r[b], 1)
                                dve.wait_ge(a_r[b], j * 2 + 1)
                                dve.tensor_tensor(out=r3(A[b]), in0=r3(A[b]), in1=brd(dd[b][:, :], U), op=ALU.mult).then_inc(a_r[b], 1)
                                dve.wait_ge(q_mm[b], j + 1)
                                dve.wait_ge(sent[b], j * (16 * U))
                                dve.tensor_tensor(out=r3(QO[b]), in0=prows(bank[4 * b + 3]), in1=brd(dd[b][:, :], U), op=ALU.mult).then_inc(q_r[b], 1)
                                dve.wait_ge(q_r[b], j * 2 + 1)
                                dve.tensor_copy(QSD[:, bass.ds((j * 2 + b) * U, U), :], r3(QO[b])).then_inc(q_r[b], 1)
                            assert ch.n == K, ch.n

                    @block.scalar
                    def _(act):
                        with act.Fori(0, PAIRS) as j:
                            for b in range(2):
                                c = j * 2 + b
                                if b == 0:
                                    for i in range(2):
                                        act.wait_ge(got[i], j * (48 * U))
                                        act.activation(ixs[i][:, :], src_i[:, bass.ds((j * 2 + i) * U, U)], ACT.Copy)
                                        act.activation(ixd[i][:, :], dst_i[:, bass.ds((j * 2 + i) * U, U)], ACT.Copy).then_inc(ix_r[i], 1)
                                act.wait_ge(sent[b], j * (16 * U))
                                act.activation(ixe[b][:, :], dst_end[:, bass.ds(c * U, U)], ACT.Copy).then_inc(ixe_r[b], 1)
                                act.wait_ge(centred[b], j + 1)
                                ln_square(act, XC[b][:, :], SQ[b][:, :]).then_inc(squared[b], 1)
                                act.activation(XD[:, bass.ds(c * U, U), :], r3(G[b], 2 * U)[:, U:2 * U, :], ACT.Copy).then_inc(x_kept[b], 1)
                                act.wait_ge(var_r[b], j + 1)
                                ln_std(act, v_[b][:, :], sd_[b][:, :]).then_inc(std_r[b], 1)
                                act.wait_ge(s_back[b], j + 1)
                                act.activation(dq[b][:, :], prows(bank[4 * b + 1], F1)[:, :, C], ACT.Sqrt, bias=one[:, :]).then_inc(cnt_r[b], 1)
                                act.wait_ge(aT_mm[b], j + 1)
                                act.activation(AT[b][:, :], bank[4 * b + 2][0:C, 0:CE], ACT.Copy).then_inc(aT_r[b], 1)
                                act.wait_ge(z_mm[b], j + 1)
                                act.activation(Z[b][:, :], bank[4 * b + 3][0:HID, 0:CE], ACT.Relu, bias=b3_sb[:, :]).then_inc(z_r[b], 1)

                    @block.tensor
                    def _(pe):
                        with pe.Fori(0, PAIRS) as j:
                            for b in range(2):
                                pe.wait_ge(m_r[b], j + 1)
                                pe.wait_ge(q_r[b], j * 2)
                                fwd(pe, bank[4 * b], r3(M[b]), F1, mT[b])
                                pe.wait_ge(s_r[b], j + 1)
                                back(pe, bank[4 * b + 1], S[b], F1, s_back[b])
                                pe.wait_ge(a_r[b], j * 2 + 2)
                                fwd(pe, bank[4 * b + 2], r3(A[b]), C, aT_mm[b])
                                pe.wait_ge(aT_r[b], j + 1)
                                pe.matmul(bank[4 * b + 3][0:HID, 0:CE], w3_sb[:, :], AT[b][:, :], start=True, stop=True).then_inc(z_mm[b], 1)
                                pe.wait_ge(z_r[b], j + 1)
                                for u in range(U):
                                    ins = pe.matmul(bank[4 * b + 3][0:P, u * C:(u + 1) * C], Z[b][:, u * P:(u + 1) * P], w4_sb[:, :], start=True, stop=True)
                                ins.then_inc(q_mm[b], 1)

            with ExitStack() as s2:
                sb, sem, sems = alloc(s2)
                G, Y, XC, SQ, H, O = ([sb(f"c2_{n}{b}", [P, U * C]) for b in range(2)] for n in ("g", "y", "xc", "sq", "h", "o"))
                s_, v_, sd_, rs_ = ([sb(f"c2_{n}{b}", [P, U]) for b in range(2)] for n in ("sum", "var", "std", "rstd"))
                S = [sb(f"c2_s{b}", [C, CE]) for b in range(2)]
                ixs, ixe = ([sb(f"c2_{n}{b}", [P, U], i32) for b in range(2)] for n in ("ixs", "ixe"))
                ix_r, ixe_r, got, gT, s_r, s_back, y_r, centred, squared, var_r, std_r, o_r, sent = (sems(f"c2_{n}") for n in (
                    "ix_ready", "ixe_ready", "gathered", "gT", "scanned", "sums_back", "x1", "centred", "squared", "var", "std", "rows", "sent"))
                dl, m1 = sem("c2_link"), sem("c2_zero")
                with nc.Block() as block:
                    @block.gpsimd
                    def _(pool):
                        def gathers(b, j):
                            pool.wait_ge(ix_r[b], j + 1)
                            pool.wait_ge(gT[b], j)
                            pool.sem_inc(pool_went_on, 1)
                            gather(pool, G[b], C, qs, ixs[b], got[b])
                        def scatters(b, j):
                            pool.wait_ge(o_r[b], j + 1)
                            pool.wait_ge(ixe_r[b], j + 1)
                            pool.sem_inc(pool_went_on, 1)
                            scatter(pool, x1, ixe[b], Y[b], C, sent[b])
                            scatter(pool, out, ixe[b], O[b], C, sent[b])
                        with pool.Fori(0, PAIRS) as j:
                            gathers(0, j)
                            gathers(1, j)
                            scatters(0, j)
                            scatters(1, j)
                        for b in range(2):
                            pool.wait_ge(sent[b], 32 * U * PAIRS)

                    @block.vector
                    def _(dve):
                        for b in range(2):
                            ins = dve.memset(S[b][:, :], 0.0)
                        ins.then_inc(m1, 1)
                        dve.wait_ge(m1, 1)
                        K = 2 * 8
                        with dve.Fori(0, PAIRS) as j:
                            ch = Chain(dve, dl, j * K)
                            for b in range(2):
                                cols = bass.ds((j * 2 + b) * U, U)
                                dve.wait_ge(gT[b], j + 1)
                                dve.wait_ge(*pair_of_scans(b, j, s_r))
                                dve.tensor_tensor_scan(S[b][:, :], mask_d[0:C, bass.ds((j * 2 + b) * CE, CE)], bank[4 * b][0:C, 0:CE],
                                                       S[1 - b][:, CE - 1:CE], ALU.mult, ALU.add).then_inc(s_r[b], 1)
                                dve.wait_ge(s_back[b], j + 1)
                                dve.wait_ge(sent[b], j * (32 * U))
                                ch.link(dve.tensor_tensor(out=r3(Y[b]), in0=QSD[:, cols, :], in1=prows(bank[4 * b + 1]), op=ALU.add))
                                ch.link(dve.tensor_tensor(out=r3(Y[b]), in0=r3(Y[b]), in1=brd(dinv_d[:, cols], U), op=ALU.mult))
                                ch.link(dve.tensor_tensor(out=r3(Y[b]), in0=r3(Y[b]), in1=rows(b4B[:, :], U), op=ALU.add))
                                ch.link(dve.tensor_tensor(out=r3(Y[b]), in0=r3(Y[b]), in1=XD[:, cols, :], op=ALU.add))
                                ln_centre(dve, ch.link, r3(Y[b]), s_[b][:, :], r3(XC[b]), U).then_inc(centred[b], 1)
                                dve.wait_ge(squared[b], j + 1)
                                ln_var(dve, r3(SQ[b]), v_[b][:, :]).then_inc(var_r[b], 1)
                                dve.wait_ge(std_r[b], j + 1)
                                ch.link(ln_relu(dve, ch.link, sd_[b][:, :], rs_[b][:, :], r3(XC[b]), r3(H[b]), U))
                                ch.link(dve.tensor_tensor(out=H[b][:, :], in0=H[b][:, :], in1=Y[b][:, :], op=ALU.add))
                                dve.tensor_tensor(out=r3(O[b]), in0=r3(H[b]), in1=rows(c0B[:, :], U), op=ALU.add).then_inc(o_r[b], 1)
                            assert ch.n == K, ch.n

                    @block.scalar
                    def _(act):
                        with act.Fori(0, PAIRS) as j:
                            for i in range(2):
                                act.wait_ge(got[i], j * (16 * U))
                                act.activation(ixs[i][:, :], src_i[:, bass.ds((j * 2 + i) * U, U)], ACT.Copy).then_inc(ix_r[i], 1)
                            for b in range(2):
                                act.wait_ge(sent[b], j * (32 * U))
                                act.activation(ixe[b][:, :], dst_end[:, bass.ds((j * 2 + b) * U, U)], ACT.Copy).then_inc(ixe_r[b], 1)
                                act.wait_ge(centred[b], j + 1)
                                ln_square(act, XC[b][:, :], SQ[b][:, :]).then_inc(squared[b], 1)
                                act.wait_ge(var_r[b], j + 1)
                                ln_std(act, v_[b][:, :], sd_[b][:, :]).then_inc(std_r[b], 1)

                    @block.tensor
                    def _(pe):
                        with pe.Fori(0, PAIRS) as j:
                            for b in range(2):
                                pe.wait_ge(got[b], j * (16 * U) + 16 * U)
                                fwd(pe, bank[4 * b], r3(G[b]), C, gT[b])
                                pe.wait_ge(s_r[b], j + 1)
                                pe.wait_ge(centred[b], j)
                                back(pe, bank[4 * b + 1], S[b], C, s_back[b])

        with ExitStack() as st:
            sb, sem, sems = alloc(st)
            DEL = sb("series", [P, T, C])
            wk = sb("wk", [P, T])
            with ExitStack() as s2:
                sb, sem, sems = alloc(s2)
                G, XC, SQ, H = ([sb(f"t1_{n}{b}", [P, U * C]) for b in range(2)] for n in ("g", "xc", "sq", "h"))
                TR = [sb(f"t1_tr{b}", [P, U * TW]) for b in range(2)]
                s_, v_, sd_, rs_ = ([sb(f"t1_{n}{b}", [P, U]) for b in range(2)] for n in ("sum", "var", "std", "rstd"))
                S = [sb(f"t1_s{b}", [C, CE]) for b in range(2)]
                ixs = [sb(f"t1_ix{b}", [P, U], i32) for b in range(2)]
                ix_r, got, centred, squared, var_r, std_r, m_r, mT, s_r, s_back, row_r, stored, d_r = (sems(f"t1_{n}") for n in (
                    "ix_ready", "gathered", "centred", "squared", "var", "std", "messages", "mT", "scanned", "sums_back", "rows", "stored", "kept"))
                dl, m1 = sem("t1_link"), sem("t1_zero")
                with nc.Block() as block:
                    @block.gpsimd
                    def _(pool):
                        with pool.Fori(0, PAIRS) as j:
                            for b in range(2):
                                pool.wait_ge(ix_r[b], j + 1)
                                pool.wait_ge(centred[b], j)
                                pool.sem_inc(pool_went_on, 1)
                                gather(pool, G[b], C, x1, ixs[b], got[b])

                    @block.vector
                    def _(dve):
                        for b in range(2):
                            dve.memset(TR[b][:, :], 1.0)
                            ins = dve.memset(S[b][:, :], 0.0)
                        ins.then_inc(m1, 1)
                        dve.wait_ge(m1, 1)
                        dve.tensor_scalar(wk[:, :], w_s[:, :], rat[:, 1:2], None, ALU.mult).then_inc(m1, 1)
                        dve.wait_ge(m1, 2)
                        K = 2 * 3
                        with dve.Fori(0, PAIRS) as j:
                            ch = Chain(dve, dl, j * K)
                            for b in range(2):
                                cols = bass.ds((j * 2 + b) * U, U)
                                dve.wait_ge(got[b], j * (16 * U) + 16 * U)
                                ln_centre(dve, ch.link, r3(G[b]), s_[b][:, :], r3(XC[b]), U).then_inc(centred[b], 1)
                                dve.wait_ge(squared[b], j + 1)
                                ln_var(dve, r3(SQ[b]), v_[b][:, :]).then_inc(var_r[b], 1)
                                dve.wait_ge(std_r[b], j + 1)
                                ch.link(ln_relu(dve, ch.link, sd_[b][:, :], rs_[b][:, :], r3(XC[b]), r3(H[b]), U))
                                dve.tensor_tensor(out=r3(H[b]), in0=r3(H[b]), in1=brd(wk[:, cols], U), op=ALU.mult).then_inc(m_r[b], 1)
                                dve.wait_ge(mT[b], j + 1)
                                dve.wait_ge(*pair_of_scans(b, j, s_r))
                                dve.tensor_tensor_scan(S[b][:, :], mask_s[0:C, bass.ds((j * 2 + b) * CE, CE)], bank[4 * b][0:C, 0:CE],
                                                       S[1 - b][:, CE - 1:CE], ALU.mult, ALU.add).then_inc(s_r[b], 1)
                                dve.wait_ge(row_r[b], j + 1)
                                dve.tensor_copy(DEL[:, cols, :], r3(TR[b])[:, :, 0:C]).then_inc(d_r[b], 1)
                            assert ch.n == K, ch.n

                    @block.scalar
                    def _(act):
                        with act.Fori(0, PAIRS) as j:
                            for i in range(2):
                                act.wait_ge(got[i], j * (16 * U))
                                act.activation(ixs[i][:, :], dstS_i[:, bass.ds((j * 2 + i) * U, U)], ACT.Copy).then_inc(ix_r[i], 1)
                            for b in range(2):
                                act.wait_ge(centred[b], j + 1)
                                ln_square(act, XC[b][:, :], SQ[b][:, :]).then_inc(squared[b], 1)
                                act.wait_ge(var_r[b], j + 1)
                                ln_std(act, v_[b][:, :], sd_[b][:, :]).then_inc(std_r[b], 1)
                                act.wait_ge(s_back[b], j + 1)
                                act.wait_ge(stored[b], j * 16)
                                act.wait_ge(d_r[b], j)
                                act.activation(r3(TR[b])[:, :, 0:C], prows(bank[4 * b + 1]), ACT.Copy).then_inc(row_r[b], 1)

                    @block.tensor
                    def _(pe):
                        with pe.Fori(0, PAIRS) as j:
                            for b in range(2):
                                pe.wait_ge(m_r[b], j + 1)
                                fwd(pe, bank[4 * b], r3(H[b]), C, mT[b])
                                pe.wait_ge(s_r[b], j + 1)
                                pe.wait_ge(row_r[b], j)
                                back(pe, bank[4 * b + 1], S[b], C, s_back[b])

                    @block.sync
                    def _(sp):
                        with sp.Fori(0, PAIRS) as j:
                            for b in range(2):
                                sp.wait_ge(row_r[b], j + 1)
                                sp.dma_start(chunk_rows(terms[1], j * 2 + b), r3(TR[b])).then_inc(stored[b], 16)
                        for b in range(2):
                            sp.wait_ge(stored[b], 16 * PAIRS)

            for k in range(2, LISTS + 1):
                with ExitStack() as s2:
                    sb, sem, sems = alloc(s2)
                    lin, lout = lists[max(k - 1, 2)], lists[k] if k > 2 else None
                    tin, tout = terms[1 if k == 2 else 2 * (k % 2)], terms[2 * ((k + 1) % 2)]
                    nm = f"k{k}_"
                    tl = lambda n, shape, dt=f32: [sb(f"{nm}{n}{b}", shape, dt) for b in range(2)]
                    R, prv_own, nxt_own = tl("rec", [P, U2, 4]), tl("prev", [P, U2, 1]), tl("next", [P, U2, 1])
                    G, M, TR = tl("g", [P, U2 * TW]), tl("m", [P, U2 * TW]), tl("tr", [P, U2 * TW])
                    gix, tix, lix = tl("gix", [P, U2], i32), tl("tix", [P, U2], i32), tl("lix", [P, U2], i32)
                    cont, endf, wr, actv, wa, tf, lf, ps3 = (tl(n, [P, U2]) for n in ("cont", "endf", "wr", "actv", "wa", "tf", "lf", "ps3"))
                    tot = tl("tot", [P, U2])
                    MKT, S = tl("maskT", [TW, CE2]), tl("s", [TW, CE2])
                    base = sb(nm + "base", [P, 1])
                    fits, pairs_f = sb(nm + "fits", [1, CHUNKS]), sb(nm + "pairs_f", [1, 1])
                    rows_in, ix_r, got, m_r, mT, mk_r, s_r, l_r, s_back, t_r, sent = (sems(nm + n) for n in (
                        "rows_in", "indices", "gathered", "messages", "mT", "maskT", "scanned", "list_rows", "back", "rows", "sent"))
                    dl, z_r = sem(nm + "link"), sem(nm + "zero")
                    SENT = 16 * U2 * (3 if lout is not None else 2)
                    g3 = lambda a: a[:, :].rearrange("p (u f) -> p u f", u=U2)
                    pairs_of = lambda eng: eng.value_load(counts[max(k - 1, 2)][0:1, 0:1], min_val=1, max_val=PAIRS * 2)
                    with nc.Block() as block:
                        @block.sync
                        def _(sp):
                            with sp.Fori(0, pairs_of(sp)) as j:
                                for b in range(2):
                                    sp.wait_ge(sent[b], j * SENT)
                                    for buf, shift, w_ in ((R, 1, 4), (prv_own, 0, 1), (nxt_own, 2, 1)):
                                        sp.dma_start(buf[b][:, :, :], lin[bass.ds((j * 2 + b) * CE2 + shift, CE2), 0:w_]
                                                     .rearrange("(u p) f -> p u f", p=P)).then_inc(rows_in[b], 16)

                        @block.gpsimd
                        def _(pool):
                            with pool.Fori(0, pairs_of(pool)) as j:
                                for b in range(2):
                                    pool.wait_ge(ix_r[b], j + 1)
                                    pool.sem_inc(pool_went_on, 1)
                                    for u in range(U2):
                                        pool.indirect_dma_start(out=G[b][:, u * TW:(u + 1) * TW], out_offset=None, in_=tin,
                                                                in_offset=bass.IndirectOffsetOnAxis(ap=gix[b][:, u:u + 1], axis=0))\
                                            .then_inc(got[b], 16)
                                for b in range(2):
                                    if lout is not None:
                                        pool.wait_ge(l_r[b], j + 1)
                                        pool.sem_inc(pool_went_on, 1)
                                        for u in range(U2):
                                            pool.indirect_dma_start(out=lout, out_offset=bass.IndirectOffsetOnAxis(ap=lix[b][:, u:u + 1], axis=0),
                                                                    in_=R[b][:, u, :], in_offset=None,
                                                                    bounds_check=E, oob_is_err=False).then_inc(sent[b], 16)
                                    pool.wait_ge(t_r[b], j + 1)
                                    pool.sem_inc(pool_went_on, 1)
                                    for u in range(U2):
                                        at = bass.IndirectOffsetOnAxis(ap=tix[b][:, u:u + 1], axis=0)
                                        pool.indirect_dma_start(out=tout, out_offset=at, in_=TR[b][:, u * TW:(u + 1) * TW],
                                                                in_offset=None).then_inc(sent[b], 16)
                                        pool.indirect_dma_start(out=series, out_offset=at, in_=TR[b][:, u * TW:u * TW + C], in_offset=None,
                                                                compute_op=ALU.add).then_inc(sent[b], 16)
                            pool.drain()

                        @block.vector
                        def _(dve):
                            dve.memset(base[:, :], 0.0)
                            for b in range(2):
                                ins = dve.memset(S[b][:, :], 0.0)
                            ins.then_inc(z_r, 1)
                            dve.wait_ge(z_r, 1)
                            K = 2 * (11 if lout is not None else 6)
                            with dve.Fori(0, pairs_of(dve)) as j:
                                ch = Chain(dve, dl, j * K)
                                for b in range(2):
                                    dve.wait_ge(rows_in[b], j * 48 + 48)
                                    own_, dst_, w_ = R[b][:, :, 0], R[b][:, :, 1], R[b][:, :, 2]
                                    dve.tensor_copy(gix[b][:, :], dst_)
                                    dve.tensor_scalar(wr[b][:, :], w_, ratios_py[k], None, ALU.mult)
                                    dve.tensor_tensor(out=cont[b][:, :], in0=own_, in1=prv_own[b][:, :, 0], op=ALU.is_equal)
                                    ch.link(dve.tensor_tensor(out=endf[b][:, :], in0=own_, in1=nxt_own[b][:, :, 0], op=ALU.not_equal))
                                    ch.link(dve.scalar_tensor_tensor(out=endf[b][:, :], in0=own_, scalar=0.0, in1=endf[b][:, :], op0=ALU.is_ge, op1=ALU.mult))
                                    ch.link(dve.tensor_tensor(out=tf[b][:, :], in0=own_, in1=nowhere[:, b * U2:(b + 1) * U2], op=ALU.subtract))
                                    ch.link(dve.tensor_tensor(out=tf[b][:, :], in0=tf[b][:, :], in1=endf[b][:, :], op=ALU.mult))
                                    dve.tensor_tensor(out=tix[b][:, :], in0=tf[b][:, :], in1=nowhere[:, b * U2:(b + 1) * U2], op=ALU.add).then_inc(ix_r[b], 1)
                                for b in range(2):
                                    dve.wait_ge(got[b], j * (16 * U2) + 16 * U2)
                                    ch.link(dve.tensor_scalar(actv[b][:, :], g3(G[b])[:, :, C], float(k - 1), None, ALU.is_equal))
                                    ch.link(dve.tensor_tensor(out=wa[b][:, :], in0=wr[b][:, :], in1=actv[b][:, :], op=ALU.mult))
                                    dve.tensor_copy(g3(M[b])[:, :, C], actv[b][:, :])
                                    dve.tensor_tensor(out=g3(M[b])[:, :, 0:C], in0=g3(G[b])[:, :, 0:C],
                                                      in1=wa[b][:, :].unsqueeze(2).to_broadcast([P, U2, C]), op=ALU.mult).then_inc(m_r[b], 1)
                                for b in range(2):
                                    dve.wait_ge(mk_r[b], j + 1)
                                    dve.wait_ge(*pair_of_scans(b, j, s_r))
                                    dve.tensor_tensor_scan(S[b][:, :], MKT[b][:, :], bank[4 * b][0:TW, 0:CE2], S[1 - b][:, CE2 - 1:CE2],
                                                           ALU.mult, ALU.add).then_inc(s_r[b], 1)
                                    if lout is not None:
                                        ch.link(dve.tensor_copy(tot[b][:, :], bank[4 * b + 2][0:P, U2:2 * U2]))
                                        ch.link(dve.tensor_scalar(lf[b][:, :], bank[4 * b + 2][0:P, 0:U2], base[:, 0:1], 1.0, ALU.add, ALU.add))
                                        dve.tensor_tensor(out=base[:, :], in0=base[:, :], in1=tot[b][:, 0:1], op=ALU.add)
                                        ch.link(dve.tensor_tensor(out=lf[b][:, 1:2], in0=lf[b][:, 1:2], in1=tot[b][:, 0:1], op=ALU.add))
                                        dve.tensor_tensor(out=base[:, :], in0=base[:, :], in1=tot[b][:, 1:2], op=ALU.add)
                                        ch.link(dve.tensor_tensor(out=lf[b][:, :], in0=lf[b][:, :], in1=nowhere[:, b * U2:(b + 1) * U2], op=ALU.subtract))
                                        ch.link(dve.tensor_tensor(out=lf[b][:, :], in0=lf[b][:, :], in1=actv[b][:, :], op=ALU.mult))
                                        dve.tensor_tensor(out=lix[b][:, :], in0=lf[b][:, :], in1=nowhere[:, b * U2:(b + 1) * U2], op=ALU.add).then_inc(l_r[b], 1)
                                for b in range(2):
                                    dve.wait_ge(s_back[b], j + 1)
                                    back_rows = bank[4 * b + 3][0:P, 0:U2 * TW].rearrange("p (u f) -> p u f", u=U2)
                                    dve.tensor_scalar(g3(TR[b])[:, :, C], back_rows[:, :, C], 0.0, float(k), ALU.is_gt, ALU.mult)
                                    dve.tensor_copy(g3(TR[b])[:, :, 0:C], back_rows[:, :, 0:C]).then_inc(t_r[b], 1)
                                assert ch.n == K, ch.n
                            if lout is not None:
                                dve.drain().then_inc(z_r, 1)
                                dve.wait_ge(z_r, 2)
                                ch = Chain(dve, z_r, 2)
                                list_count(dve, ch.link, base[0:1, 0:1], fits[:, :], pairs_f[:, :], counts[k])

                        @block.scalar
                        def _(act):
                            with act.Fori(0, pairs_of(act)) as j:
                                for b in range(2):
                                    act.wait_ge(mT[b], j + 1)
                                    act.activation(MKT[b][:, :], bank[4 * b + 1][0:TW, 0:CE2], ACT.Copy).then_inc(mk_r[b], 1)

                        @block.tensor
                        def _(pe):
                            with pe.Fori(0, pairs_of(pe)) as j:
                                for b in range(2):
                                    pe.wait_ge(m_r[b], j + 1)
                                    pe.sem_inc(pe_went_on, 1)
                                    for u in range(U2):
                                        cols = slice(u * P, (u + 1) * P)
                                        pe.transpose(bank[4 * b][0:TW, cols], g3(M[b])[:, u, :], ident[0:P, 0:P])
                                        pe.transpose(bank[4 * b + 1][0:TW, cols], cont[b][:, u:u + 1].to_broadcast([P, TW]), ident[0:P, 0:P])
                                    pe.matmul(bank[4 * b + 2][0:P, 0:U2], tri_k[:, :], actv[b][:, :], start=True, stop=True)
                                    pe.matmul(bank[4 * b + 2][0:P, U2:2 * U2], ones_pp[:, :], actv[b][:, :], start=True, stop=True).then_inc(mT[b], 1)
                                for b in range(2):
                                    pe.wait_ge(s_r[b], j + 1)
                                    pe.sem_inc(pe_went_on, 1)
                                    for u in range(U2):
                                        ins = pe.transpose(bank[4 * b + 3][0:P, u * TW:(u + 1) * TW], S[b][:, u * P:(u + 1) * P], ident[0:TW, 0:TW])
                                    ins.then_inc(s_back[b], 1)

            left = nc.values_load(counts[LISTS][0:1, 1:2], min_val=0, max_val=E)
            with nc.If(left > P):
                for first, STEPS in ((2, TERMS // 2), (2 + TERMS // 2, TERMS // 2 - 1)):
                    with ExitStack() as s2:
                        sb, sem, sems = alloc(s2)
                        G, TR = ([sb(f"tk{first}_{n}{b}", [P, U * TW]) for b in range(2)] for n in ("g", "tr"))
                        M = [sb(f"tk{first}_m{b}", [P, U * C]) for b in range(2)]
                        S = [sb(f"tk{first}_s{b}", [C, CE]) for b in range(2)]
                        ixs = [sb(f"tk{first}_ix{b}", [P, U], i32) for b in range(2)]
                        ix_r, got, m_r, mT, s_r, s_back, row_r, stored, d_r = (sems(f"tk{first}_{n}") for n in (
                            "ix_ready", "gathered", "messages", "mT", "scanned", "sums_back", "rows", "stored", "added"))
                        wk_r, m1 = sem(f"tk{first}_weights"), sem(f"tk{first}_zero")
                        with nc.Block() as block:
                            @block.gpsimd
                            def _(pool):
                                def step(i, par):
                                    for b in range(2):
                                        pool.wait_ge(stored[b], i * (16 * PAIRS))
                                    pool.sem_inc(pool_went_on, 1)
                                    with pool.Fori(0, PAIRS) as j:
                                        for b in range(2):
                                            pool.wait_ge(ix_r[b], i * PAIRS + j + 1)
                                            pool.wait_ge(m_r[b], i * PAIRS + j)
                                            pool.sem_inc(pool_went_on, 1)
                                            gather(pool, G[b], TW, terms[1 - par], ixs[b], got[b])
                                with pool.Fori(0, STEPS // 2) as h:
                                    step(h * 2, 0)
                                    step(h * 2 + 1, 1)
                                if STEPS % 2:
                                    step(STEPS - 1, 0)

                            @block.vector
                            def _(dve):
                                for b in range(2):
                                    dve.memset(TR[b][:, :], 1.0)
                                    ins = dve.memset(S[b][:, :], 0.0)
                                ins.then_inc(m1, 1)
                                dve.wait_ge(m1, 1)
                                def step(i, par):
                                    for b in range(2):
                                        dve.wait_ge(m_r[b], i * PAIRS)
                                    dve.tensor_scalar(wk[:, :], w_s[:, :], rat[:, bass.ds(i + first, 1)], None, ALU.mult).then_inc(wk_r, 1)
                                    with dve.Fori(0, PAIRS) as j:
                                        n = i * PAIRS + j
                                        dve.wait_ge(wk_r, i + 1)
                                        for b in range(2):
                                            cols = bass.ds((j * 2 + b) * U, U)
                                            dve.wait_ge(got[b], n * (16 * U) + 16 * U)
                                            dve.wait_ge(mT[b], n)
                                            dve.tensor_tensor(out=r3(M[b]), in0=r3(G[b])[:, :, 0:C], in1=brd(wk[:, cols], U), op=ALU.mult).then_inc(m_r[b], 1)
                                            dve.wait_ge(mT[b], n + 1)
                                            dve.wait_ge(*pair_of_scans(b, n, s_r))
                                            dve.tensor_tensor_scan(S[b][:, :], mask_s[0:C, bass.ds((j * 2 + b) * CE, CE)], bank[4 * b][0:C, 0:CE],
                                                                   S[1 - b][:, CE - 1:CE], ALU.mult, ALU.add).then_inc(s_r[b], 1)
                                            dve.wait_ge(row_r[b], n + 1)
                                            dve.tensor_tensor(out=DEL[:, cols, :], in0=DEL[:, cols, :], in1=r3(TR[b])[:, :, 0:C], op=ALU.add).then_inc(d_r[b], 1)
                                with dve.Fori(0, STEPS // 2) as h:
                                    step(h * 2, 0)
                                    step(h * 2 + 1, 1)
                                if STEPS % 2:
                                    step(STEPS - 1, 0)

                            @block.scalar
                            def _(act):
                                def step(i, par):
                                    with act.Fori(0, PAIRS) as j:
                                        n = i * PAIRS + j
                                        for b in range(2):
                                            act.wait_ge(got[b], n * (16 * U))
                                            act.activation(ixs[b][:, :], gi_i[:, bass.ds((j * 2 + b) * U, U)], ACT.Copy).then_inc(ix_r[b], 1)
                                        for b in range(2):
                                            act.wait_ge(s_back[b], n + 1)
                                            act.wait_ge(stored[b], n * 16)
                                            act.wait_ge(d_r[b], n)
                                            act.activation(r3(TR[b])[:, :, 0:C], prows(bank[4 * b + 1]), ACT.Copy).then_inc(row_r[b], 1)
                                with act.Fori(0, STEPS // 2) as h:
                                    step(h * 2, 0)
                                    step(h * 2 + 1, 1)
                                if STEPS % 2:
                                    step(STEPS - 1, 0)

                            @block.tensor
                            def _(pe):
                                def step(i, par):
                                    with pe.Fori(0, PAIRS) as j:
                                        n = i * PAIRS + j
                                        for b in range(2):
                                            pe.wait_ge(m_r[b], n + 1)
                                            fwd(pe, bank[4 * b], r3(M[b]), C, mT[b])
                                            pe.wait_ge(s_r[b], n + 1)
                                            pe.wait_ge(row_r[b], n)
                                            back(pe, bank[4 * b + 1], S[b], C, s_back[b])
                                with pe.Fori(0, STEPS // 2) as h:
                                    step(h * 2, 0)
                                    step(h * 2 + 1, 1)
                                if STEPS % 2:
                                    step(STEPS - 1, 0)

                            @block.sync
                            def _(sp):
                                def step(i, par):
                                    with sp.Fori(0, PAIRS) as j:
                                        n = i * PAIRS + j
                                        for b in range(2):
                                            sp.wait_ge(row_r[b], n + 1)
                                            sp.dma_start(chunk_rows(terms[par], j * 2 + b), r3(TR[b])).then_inc(stored[b], 16)
                                with sp.Fori(0, STEPS // 2) as h:
                                    step(h * 2, 0)
                                    step(h * 2 + 1, 1)
                                if STEPS % 2:
                                    step(STEPS - 1, 0)
                                for b in range(2):
                                    sp.wait_ge(stored[b], 16 * PAIRS * STEPS)
            with nc.Else():
                with ExitStack() as s2:
                    sb, sem, sems = alloc(s2)
                    last = lists[LISTS]
                    R, nxt_own = sb("tl_rec", [P, 4]), sb("tl_next", [P, 1])
                    gix, tix = sb("tl_gix", [P, 1], i32), sb("tl_tix", [P, 1], i32)
                    G, G0, X, ACC, DL = sb("tl_g", [P, TW]), sb("tl_g0", [P, C]), sb("tl_x", [P, C]), sb("tl_acc", [P, C]), sb("tl_dl", [P, C])
                    MT, SEG = sb("tl_mT", [P, P]), sb("tl_segT", [P, P])
                    endf, tf, actv = sb("tl_end", [P, 1]), sb("tl_tf", [P, 1]), sb("tl_actv", [P, 1])
                    rows_in, ix_r, got, keys_T, x_r, g_mm, sums_mm, dl_r, added, dl = (sem(f"tl_{n}") for n in (
                        "rows_in", "indices", "gathered", "keys_T", "x", "g_mm", "sums_mm", "rows", "added", "link"))
                    with nc.Block() as block:
                        @block.sync
                        def _(sp):
                            sp.dma_start(R[:, :], last[1:1 + P, :]).then_inc(rows_in, 16)
                            sp.dma_start(nxt_own[:, :], last[2:2 + P, 0:1]).then_inc(rows_in, 16)

                        @block.gpsimd
                        def _(pool):
                            pool.wait_ge(ix_r, 1)
                            pool.indirect_dma_start(out=G[:, :], out_offset=None, in_=terms[2 * ((LISTS + 1) % 2)],
                                                    in_offset=bass.IndirectOffsetOnAxis(ap=gix[:, 0:1], axis=0)).then_inc(got, 16)
                            pool.wait_ge(dl_r, 1)
                            pool.indirect_dma_start(out=series, out_offset=bass.IndirectOffsetOnAxis(ap=tix[:, 0:1], axis=0),
                                                    in_=DL[:, :], in_offset=None, compute_op=ALU.add).then_inc(added, 16)
                            pool.wait_ge(added, 16)

                        @block.tensor
                        def _(pe):
                            pe.wait_ge(rows_in, 32)
                            pe.transpose(bank[0][0:P, 0:P], R[:, 1:2].to_broadcast([P, P]), ident[0:P, 0:P])
                            pe.transpose(bank[1][0:P, 0:P], R[:, 0:1].to_broadcast([P, P]), ident[0:P, 0:P]).then_inc(keys_T, 1)
                            with pe.Fori(0, TERMS - LISTS - 1) as i:
                                pe.wait_ge(x_r, i + 1)
                                pe.matmul(bank[2][0:P, 0:C], MT[:, :], X[:, :], start=True, stop=True).then_inc(g_mm, 1)
                            pe.wait_ge(x_r, TERMS - LISTS + 1)
                            pe.matmul(bank[3][0:P, 0:C], SEG[:, :], ACC[:, :], start=True, stop=True).then_inc(sums_mm, 1)

                        @block.vector
                        def _(dve):
                            ch = Chain(dve, dl)
                            link = ch.link
                            dve.wait_ge(rows_in, 32)
                            link(dve.tensor_copy(gix[:, :], R[:, 1:2]))
                            link(dve.tensor_tensor(out=endf[:, :], in0=R[:, 0:1], in1=nxt_own[:, :], op=ALU.not_equal))
                            link(dve.scalar_tensor_tensor(out=endf[:, :], in0=R[:, 0:1], scalar=0.0, in1=endf[:, :], op0=ALU.is_ge, op1=ALU.mult))
                            link(dve.tensor_tensor(out=tf[:, :], in0=R[:, 0:1], in1=nowhere[:, 0:1], op=ALU.subtract))
                            link(dve.tensor_tensor(out=tf[:, :], in0=tf[:, :], in1=endf[:, :], op=ALU.mult))
                            dve.tensor_tensor(out=tix[:, :], in0=tf[:, :], in1=nowhere[:, 0:1], op=ALU.add).then_inc(ix_r, 1)
                            dve.wait_ge(keys_T, 1)
                            dve.tensor_scalar(MT[:, :], bank[0][0:P, 0:P], R[:, 0:1], R[:, 2:3], ALU.is_equal, ALU.mult)
                            dve.tensor_scalar(SEG[:, :], bank[1][0:P, 0:P], R[:, 0:1], R[:, 2:3], ALU.is_equal, ALU.mult)
                            dve.wait_ge(got, 16)
                            link(dve.tensor_scalar(actv[:, :], G[:, C:TW], float(LISTS), None, ALU.is_equal))
                            link(dve.tensor_scalar(G0[:, :], G[:, 0:C], actv[:, 0:1], None, ALU.mult))
                            dve.tensor_scalar(X[:, :], G0[:, :], ratios_py[LISTS + 1], None, ALU.mult).then_inc(x_r, 1)
                            dve.wait_ge(x_r, 1)
                            link(dve.tensor_copy(ACC[:, :], X[:, :]))
                            before = ch.n
                            with dve.Fori(0, TERMS - LISTS - 1) as i:
                                ch = Chain(dve, dl, i * 1 + before)
                                dve.wait_ge(g_mm, i + 1)
                                dve.tensor_scalar(X[:, :], bank[2][0:P, 0:C], rat[:, bass.ds(i + LISTS + 2, 1)], None, ALU.mult).then_inc(x_r, 1)
                                dve.wait_ge(x_r, i + 2)
                                ch.link(dve.tensor_tensor(out=ACC[:, :], in0=ACC[:, :], in1=X[:, :], op=ALU.add))
                            dve.sem_inc(x_r, 1)
                            dve.wait_ge(sums_mm, 1)
                            dve.tensor_copy(DL[:, :], bank[3][0:P, 0:C]).then_inc(dl_r, 1)

                with ExitStack() as s2:
                    sb, sem, sems = alloc(s2)
                    D = [sb(f"ad_d{b}", [P, U * C]) for b in range(2)]
                    d_in, d_used = sems("ad_in"), sems("ad_used")
                    with nc.Block() as block:
                        @block.sync
                        def _(sp):
                            with sp.Fori(0, PAIRS) as j:
                                for b in range(2):
                                    sp.wait_ge(d_used[b], j)
                                    sp.dma_start(r3(D[b]), chunk_rows(series, j * 2 + b)).then_inc(d_in[b], 16)

                        @block.vector
                        def _(dve):
                            with dve.Fori(0, PAIRS) as j:
                                for b in range(2):
                                    cols = bass.ds((j * 2 + b) * U, U)
                                    dve.wait_ge(d_in[b], j * 16 + 16)
                                    dve.tensor_tensor(out=DEL[:, cols, :], in0=DEL[:, cols, :], in1=r3(D[b]), op=ALU.add).then_inc(d_used[b], 1)

            with ExitStack() as s2:
                sb, sem, sems = alloc(s2)
                G, XC, SQ, H, O = ([sb(f"l2_{n}{b}", [P, U * C]) for b in range(2)] for n in ("g", "xc", "sq", "h", "o"))
                s_, v_, sd_, rs_ = ([sb(f"l2_{n}{b}", [P, U]) for b in range(2)] for n in ("sum", "var", "std", "rstd"))
                ixs, ixe = ([sb(f"l2_{n}{b}", [P, U], i32) for b in range(2)] for n in ("ixs", "ixe"))
                AR = [sb(f"l2_attr{b}", [P, U * ATTR]) for b in range(2)]
                AS, AM, CN, MEAN = ([sb(f"l2_{n}{b}", [ATTR, CE]) for b in range(2)] for n in ("seg_sum", "seg_max", "seg_cnt", "mean"))
                BM = [sb(f"l2_big{b}", [ATTR, CE]) for b in range(2)]
                ones = sb("l2_ones", [ATTR, CE])
                Z = [sb(f"l2_z{b}", [HID, CE]) for b in range(2)]
                ix_r, ixe_r, got, a_in, a_T, big_r, sc_r, mean_r, z_mm, z_r, l2_mm, centred, squared, var_r, std_r, o_r, sent = (sems(f"l2_{n}") for n in (
                    "ix_ready", "ixe_ready", "gathered", "attr_in", "attr_T", "big", "scanned", "mean", "z_mm", "z", "rows_mm", "centred", "squared", "var", "std", "rows", "sent"))
                dl, m1 = sem("l2_link"), sem("l2_zero")
                with nc.Block() as block:
                    @block.gpsimd
                    def _(pool):
                        def gathers(b, j):
                            pool.wait_ge(ix_r[b], j + 1)
                            pool.wait_ge(o_r[b], j)
                            pool.sem_inc(pool_went_on, 1)
                            gather(pool, G[b], C, x1, ixs[b], got[b])
                        def scatters(b, j):
                            pool.wait_ge(o_r[b], j + 1)
                            pool.wait_ge(ixe_r[b], j + 1)
                            pool.sem_inc(pool_went_on, 1)
                            scatter(pool, out, ixe[b], O[b], C, sent[b])
                        with pool.Fori(0, PAIRS) as j:
                            gathers(0, j)
                            gathers(1, j)
                            scatters(0, j)
                            scatters(1, j)
                        for b in range(2):
                            pool.wait_ge(sent[b], 16 * U * PAIRS)

                    @block.sync
                    def _(sp):
                        with sp.Fori(0, PAIRS) as j:
                            for b in range(2):
                                sp.wait_ge(a_T[b], j)
                                sp.dma_start(r3(AR[b]), chunk_rows(pay, j * 2 + b)[:, :, 5:PAYW]).then_inc(a_in[b], 16)

                    @block.vector
                    def _(dve):
                        dve.memset(ones[:, :], 1.0)
                        for b in range(2):
                            dve.memset(AS[b][:, :], 0.0)
                            dve.memset(AM[b][:, :], 0.0)
                            ins = dve.memset(CN[b][:, :], 0.0)
                        ins.then_inc(m1, 1)
                        dve.wait_ge(m1, 1)
                        K = 2 * 8
                        with dve.Fori(0, PAIRS) as j:
                            ch = Chain(dve, dl, j * K)
                            for b in range(2):
                                c = j * 2 + b
                                cols = bass.ds(c * U, U)
                                mask = mask_s[0:ATTR, bass.ds(c * CE, CE)]
                                ch.link(dve.tensor_scalar(BM[b][:, :], mask, 1.0, BIG, ALU.subtract, ALU.mult))
                                dve.wait_ge(a_T[b], j + 1)
                                dve.wait_ge(*pair_of_scans(b, j, sc_r))
                                dve.wait_ge(z_mm[b], j)
                                dve.tensor_tensor_scan(AS[b][:, :], mask, bank[4 * b][0:ATTR, 0:CE], AS[1 - b][:, CE - 1:CE], ALU.mult, ALU.add)
                                dve.tensor_tensor_scan(AM[b][:, :], BM[b][:, :], bank[4 * b][0:ATTR, 0:CE], AM[1 - b][:, CE - 1:CE], ALU.add, ALU.max)
                                dve.tensor_tensor_scan(CN[b][:, :], mask, ones[:, :], CN[1 - b][:, CE - 1:CE], ALU.mult, ALU.add).then_inc(sc_r[b], 1)
                                dve.wait_ge(sc_r[b], j + 1)
                                ch.link(dve.reciprocal(MEAN[b][:, :], CN[b][:, :]))
                                dve.tensor_tensor(out=MEAN[b][:, :], in0=MEAN[b][:, :], in1=AS[b][:, :], op=ALU.mult).then_inc(mean_r[b], 1)
                                dve.wait_ge(got[b], j * (16 * U) + 16 * U)
                                ln_centre(dve, ch.link, r3(G[b]), s_[b][:, :], r3(XC[b]), U).then_inc(centred[b], 1)
                                dve.wait_ge(squared[b], j + 1)
                                ln_var(dve, r3(SQ[b]), v_[b][:, :]).then_inc(var_r[b], 1)
                                dve.wait_ge(std_r[b], j + 1)
                                ch.link(ln_relu(dve, ch.link, sd_[b][:, :], rs_[b][:, :], r3(XC[b]), r3(H[b]), U))
                                ch.link(dve.tensor_tensor(out=r3(H[b]), in0=r3(H[b]), in1=DEL[:, cols, :], op=ALU.add))
                                ch.link(dve.tensor_tensor(out=H[b][:, :], in0=H[b][:, :], in1=G[b][:, :], op=ALU.add))
                                ch.link(dve.tensor_tensor(out=r3(H[b]), in0=r3(H[b]), in1=rows(b2B[:, :], U), op=ALU.add))
                                dve.wait_ge(l2_mm[b], j + 1)
                                dve.wait_ge(sent[b], j * (16 * U))
                                dve.tensor_tensor(out=O[b][:, :], in0=H[b][:, :], in1=bank[4 * b + 2][0:P, 0:U * C], op=ALU.add).then_inc(o_r[b], 1)
                            assert ch.n == K, ch.n

                    @block.scalar
                    def _(act):
                        with act.Fori(0, PAIRS) as j:
                            for i in range(2):
                                act.wait_ge(got[i], j * (16 * U))
                                act.activation(ixs[i][:, :], srcS_i[:, bass.ds((j * 2 + i) * U, U)], ACT.Copy).then_inc(ix_r[i], 1)
                            for b in range(2):
                                act.wait_ge(sent[b], j * (16 * U))
                                act.activation(ixe[b][:, :], srcS_end[:, bass.ds((j * 2 + b) * U, U)], ACT.Copy).then_inc(ixe_r[b], 1)
                                act.wait_ge(z_mm[b], j + 1)
                                act.activation(Z[b][:, :], bank[4 * b + 1][0:HID, 0:CE], ACT.Relu, bias=b1u[:, :]).then_inc(z_r[b], 1)
                                act.wait_ge(centred[b], j + 1)
                                ln_square(act, XC[b][:, :], SQ[b][:, :]).then_inc(squared[b], 1)
                                act.wait_ge(var_r[b], j + 1)
                                ln_std(act, v_[b][:, :], sd_[b][:, :]).then_inc(std_r[b], 1)

                    @block.tensor
                    def _(pe):
                        with pe.Fori(0, PAIRS) as j:
                            for b in range(2):
                                pe.wait_ge(a_in[b], j * 16 + 16)
                                pe.wait_ge(sc_r[b], j)
                                fwd(pe, bank[4 * b], r3(AR[b]), ATTR, a_T[b])
                                pe.wait_ge(mean_r[b], j + 1)
                                for i, a in enumerate((AS, AM, MEAN)):
                                    ins = pe.matmul(bank[4 * b + 1][0:HID, 0:CE], w1_sb[:, i, :], a[b][:, :], start=i == 0, stop=i == 2)
                                ins.then_inc(z_mm[b], 1)
                                pe.wait_ge(z_r[b], j + 1)
                                pe.wait_ge(o_r[b], j)
                                for u in range(U):
                                    ins = pe.matmul(bank[4 * b + 2][0:P, u * C:(u + 1) * C], Z[b][:, u * P:(u + 1) * P], w2_sb[:, :], start=True, stop=True)
                                ins.then_inc(l2_mm[b], 1)

        with ExitStack() as st:
            sb, sem, sems = alloc(st)
            RES = sb("res", [P, T, C])
            with ExitStack() as s2:
                sb, sem, sems = alloc(s2)
                G, XC, SQ, H = ([sb(f"l3_{n}{b}", [P, 2 * U * C]) for b in range(2)] for n in ("g", "xc", "sq", "h"))
                s_, v_, sd_, rs_ = ([sb(f"l3_{n}{b}", [P, 2 * U]) for b in range(2)] for n in ("sum", "var", "std", "rstd"))
                ixs, ixd = ([sb(f"l3_{n}{b}", [P, U], i32) for b in range(2)] for n in ("ixs", "ixd"))
                HT = [[sb(f"l3_hT{k}{b}", [C, CE]) for b in range(2)] for k in range(2)]
                MX, BM, XT, R = ([sb(f"l3_{n}{b}", [C, CE]) for b in range(2)] for n in ("max", "big", "uv", "r"))
                ix_r, got, centred, squared, var_r, std_r, h_r, hT_mm, hT_r, uv_mm, big_r, mx_r, sum_r, r_r, r_back, res_r = (sems(f"l3_{n}") for n in (
                    "ix_ready", "gathered", "centred", "squared", "var", "std", "h", "hT_mm", "hT", "uv_mm", "big", "max", "sum", "relu", "back", "res"))
                dl, m1 = sem("l3_link"), sem("l3_zero")
                with nc.Block() as block:
                    @block.gpsimd
                    def _(pool):
                        with pool.Fori(0, PAIRS) as j:
                            for b in range(2):
                                pool.wait_ge(ix_r[b], j + 1)
                                pool.wait_ge(res_r[b], j)
                                pool.sem_inc(pool_went_on, 1)
                                gather(pool, G[b], C, out, ixs[b], got[b])
                                gather(pool, G[b][:, U * C:], C, out, ixd[b], got[b])

                    @block.vector
                    def _(dve):
                        for b in range(2):
                            ins = dve.memset(MX[b][:, :], 0.0)
                        ins.then_inc(m1, 1)
                        dve.wait_ge(m1, 1)
                        K = 2 * 3
                        with dve.Fori(0, PAIRS) as j:
                            ch = Chain(dve, dl, j * K)
                            for b in range(2):
                                c = j * 2 + b
                                cols = bass.ds(c * U, U)
                                ch.link(dve.tensor_scalar(BM[b][:, :], mask_d[0:C, bass.ds(c * CE, CE)], 1.0, BIG, ALU.subtract, ALU.mult))
                                dve.wait_ge(got[b], j * (32 * U) + 32 * U)
                                ln_centre(dve, ch.link, r3(G[b], 2 * U), s_[b][:, :], r3(XC[b], 2 * U), 2 * U).then_inc(centred[b], 1)
                                dve.wait_ge(squared[b], j + 1)
                                ln_var(dve, r3(SQ[b], 2 * U), v_[b][:, :]).then_inc(var_r[b], 1)
                                dve.wait_ge(std_r[b], j + 1)
                                ln_relu(dve, ch.link, sd_[b][:, :], rs_[b][:, :], r3(XC[b], 2 * U), r3(H[b], 2 * U), 2 * U).then_inc(h_r[b], 1)
                                dve.wait_ge(uv_mm[b], j + 1)
                                dve.wait_ge(*pair_of_scans(b, j, mx_r))
                                dve.tensor_tensor_scan(MX[b][:, :], BM[b][:, :], bank[4 * b + 2][0:C, 0:CE], MX[1 - b][:, CE - 1:CE], ALU.add, ALU.max)\
                                   .then_inc(mx_r[b], 1)
                                dve.wait_ge(mx_r[b], j + 1)
                                dve.wait_ge(r_r[b], j)
                                dve.tensor_tensor(out=XT[b][:, :], in0=MX[b][:, :], in1=bank[4 * b + 3][0:C, 0:CE], op=ALU.add).then_inc(sum_r[b], 1)
                                dve.wait_ge(r_back[b], j + 1)
                                dve.tensor_tensor(out=RES[:, cols, :], in0=r3(G[b], 2 * U)[:, U:2 * U, :], in1=prows(bank[4 * b]), op=ALU.add).then_inc(res_r[b], 1)
                            assert ch.n == K, ch.n

                    @block.scalar
                    def _(act):
                        with act.Fori(0, PAIRS) as j:
                            for i in range(2):
                                act.wait_ge(got[i], j * (32 * U))
                                act.activation(ixs[i][:, :], src_i[:, bass.ds((j * 2 + i) * U, U)], ACT.Copy)
                                act.activation(ixd[i][:, :], dst_i[:, bass.ds((j * 2 + i) * U, U)], ACT.Copy).then_inc(ix_r[i], 1)
                            for b in range(2):
                                act.wait_ge(centred[b], j + 1)
                                ln_square(act, XC[b][:, :], SQ[b][:, :]).then_inc(squared[b], 1)
                                act.wait_ge(var_r[b], j + 1)
                                ln_std(act, v_[b][:, :], sd_[b][:, :]).then_inc(std_r[b], 1)
                                act.wait_ge(hT_mm[b], j + 1)
                                for k in range(2):
                                    ins = act.activation(HT[k][b][:, :], bank[4 * b + k][0:C, 0:CE], ACT.Copy)
                                ins.then_inc(hT_r[b], 1)
                                act.wait_ge(sum_r[b], j + 1)
                                act.wait_ge(r_back[b], j)
                                act.activation(R[b][:, :], XT[b][:, :], ACT.Relu, bias=bl3_sb[:, :]).then_inc(r_r[b], 1)

                    @block.tensor
                    def _(pe):
                        with pe.Fori(0, PAIRS) as j:
                            for b in range(2):
                                pe.wait_ge(h_r[b], j + 1)
                                pe.wait_ge(res_r[b], j)
                                pe.sem_inc(pe_went_on, 1)
                                for k in range(2):
                                    for u in range(U):
                                        ins = pe.transpose(bank[4 * b + k][0:C, u * P:(u + 1) * P], r3(H[b], 2 * U)[:, k * U + u, :], ident[0:P, 0:P])
                                ins.then_inc(hT_mm[b], 1)
                                pe.wait_ge(hT_r[b], j + 1)
                                pe.sem_inc(pe_went_on, 1)
                                pe.matmul(bank[4 * b + 2][0:C, 0:CE], wl3_sb[:, 1, :], HT[0][b][:, :], start=True, stop=True)
                                pe.matmul(bank[4 * b + 3][0:C, 0:CE], wu_sb[:, :], HT[1][b][:, :], start=True, stop=True).then_inc(uv_mm[b], 1)
                                pe.wait_ge(r_r[b], j + 1)
                                back(pe, bank[4 * b], R[b], C, r_back[b])

            with ExitStack() as s2:
                sb, sem, sems = alloc(s2)
                O = [sb(f"fin_o{b}", [P, U * C]) for b in range(2)]
                ixe = [sb(f"fin_ix{b}", [P, U], i32) for b in range(2)]
                o_r, sent, ixe_r = sems("fin_rows"), sems("fin_sent"), sems("fin_ix")
                with nc.Block() as block:
                    @block.gpsimd
                    def _(pool):
                        with pool.Fori(0, PAIRS) as j:
                            for b in range(2):
                                pool.wait_ge(o_r[b], j + 1)
                                pool.wait_ge(ixe_r[b], j + 1)
                                pool.sem_inc(pool_went_on, 1)
                                scatter(pool, out, ixe[b], O[b], C, sent[b])
                        for b in range(2):
                            pool.wait_ge(sent[b], 16 * U * PAIRS)

                    @block.vector
                    def _(dve):
                        with dve.Fori(0, PAIRS) as j:
                            for b in range(2):
                                dve.wait_ge(sent[b], j * (16 * U))
                                dve.tensor_copy(r3(O[b]), RES[:, bass.ds((j * 2 + b) * U, U), :]).then_inc(o_r[b], 1)

                    @block.scalar
                    def _(act):
                        with act.Fori(0, PAIRS) as j:
                            for b in range(2):
                                act.wait_ge(sent[b], j * (16 * U))
                                act.activation(ixe[b][:, :], dst_end[:, bass.ds((j * 2 + b) * U, U)], ACT.Copy).then_inc(ixe_r[b], 1)



_INS = ["x", "src_pad", "dst_pad", "edge_attr_32", "edge_weight", "w3t", "b3", "w4t", "b4", "t", "u", "w1", "b1", "w2", "b2",
        "wl3", "bl3", "ratios"]


def kernel(x, src, dst, edge_attr_32, edge_weight, edge_weight1, L0_gnn_W3, L0_gnn_b3, L0_gnn_W4, L0_gnn_b4, L1_gnn_t,
           L2_gnn_u, L2_gnn_W1, L2_gnn_b1, L2_gnn_W2, L2_gnn_b2, L3_gnn_W, L3_gnn_b):
    import numpy as np
    import concourse.bacc as bacc
    from concourse import mybir as mb
    from concourse.bass_utils import run_bass_kernel_spmd

    pad = lambda a: np.pad(np.asarray(a), 1, constant_values=-1)
    given = dict(x=x, src_pad=pad(src), dst_pad=pad(dst), edge_attr_32=edge_attr_32, edge_weight=edge_weight,
                 w3t=np.asarray(L0_gnn_W3).T, b3=L0_gnn_b3, w4t=np.asarray(L0_gnn_W4).T, b4=L0_gnn_b4, t=L1_gnn_t,
                 u=L2_gnn_u, w1=L2_gnn_W1, b1=L2_gnn_b1, w2=L2_gnn_W2, b2=L2_gnn_b2, wl3=np.asarray(L3_gnn_W).T,
                 bl3=L3_gnn_b, ratios=np.array(taylor_ratios(), np.float32))
    nc = bacc.Bacc("TRN2", target_bir_lowering=False, num_devices=1)
    arrays, args = {}, []
    for name in _INS:
        a = np.ascontiguousarray(given[name])
        arrays[f"in_{name}"] = a
        args.append(nc.dram_tensor(f"in_{name}", a.shape, mb.dt.from_np(a.dtype), kind="ExternalInput").ap())
    o = nc.dram_tensor("out_rows", (N, C), mb.dt.float32, kind="ExternalOutput").ap()
    gnn(nc, *args, o)
    r = run_bass_kernel_spmd(nc, [arrays], core_ids=[0])
    return r.results[0]["out_rows"]
```

```python
import concourse.bass as bass
from concourse import mybir
from contextlib import ExitStack

N, C, E = 100000, 64, 25000
HID = 128
ATTR = 32
P = 125
T = E // P
U = 4
CE = U * P
CHUNKS = T // U
PAIRS = CHUNKS // 2
ND = N // P
HALF = ND // 2
HEAD = 5
PAYW = HEAD + 1 + ATTR
N_SUB, M_TERMS = 4, 20
TERMS = N_SUB * M_TERMS
EPS = 1e-5
TW = C + 1
LISTS = 6
LIST_U = {k: 4 if k < 4 else 2 if k < 6 else 1 for k in range(2, LISTS + 1)}
U2 = max(LIST_U.values())
NR = P * 209
NOWHERE = E + 2
NW = 3
BIG = 3.0e38


def taylor_ratios():
    term = [1]
    for k in range(M_TERMS, 0, -1):
        term.append(term[-1] * k)
    term.reverse()
    c = [1]
    for _ in range(N_SUB):
        new = [0] * (len(c) + M_TERMS)
        for i, a in enumerate(c):
            for k, b in enumerate(term):
                new[i + k] += a * b
        c = new
    return [0.0] + [c[k] / c[k - 1] for k in range(1, TERMS + 1)]


class Chain:

    def __init__(self, eng, sem, base=0):
        self.eng, self.sem, self.base, self.n = eng, sem, base, 0

    def put(self, ins):
        self.n += 1
        ins.then_inc(self.sem, 1)
        return self.n

    def need(self, n):
        self.eng.wait_ge(self.sem, self.base + n)

    def link(self, ins):
        self.need(self.put(ins))


def gnn(nc, x, src_pad, dst_pad, attr, w, w3t, b3, w4t, b4, t_in, u_in, w1, b1, w2, b2, wl3, bl3, ratios, out):
    f32, i32, u8, f16 = mybir.dt.float32, mybir.dt.int32, mybir.dt.uint8, mybir.dt.float16
    ALU, ACT, AX = mybir.AluOpType, mybir.ActivationFunctionType, mybir.AxisListType

    ratios_py = taylor_ratios()
    qs = nc.dram_tensor("qs_table", [N, C], f32).ap()
    h1 = nc.dram_tensor("h1_table", [N, C], f32).ap()
    hx = nc.dram_tensor("hx_table", [N, 2 * C], f32).ap()
    node_words = nc.dram_tensor("node_words", [N, NW], f32).ap()
    pay = nc.dram_tensor("sorted_edges", [E, PAYW], f32).ap()
    same_dst, same_src = (nc.dram_tensor(n, [E], u8).ap() for n in ("same_dst", "same_src"))
    srcs_pad = nc.dram_tensor("sorted_src", [E + 2], f32).ap()
    terms = [nc.dram_tensor(f"terms{i}", [NR, TW], f32).ap() for i in range(3)]
    series = nc.dram_tensor("series_by_place", [NR, C], f32).ap()
    lists = {k: nc.dram_tensor(f"list{k}", [NR, 4], f32).ap() for k in range(2, LISTS + 1)}

    tile_rows = lambda a: a.rearrange("(r e) -> r e", e=2 * P)
    tile_major = lambda a: a.rearrange("(t p) -> p t", p=P)
    chunk_rows = lambda a, c: a[bass.ds(c * CE, CE), :].rearrange("(u p) f -> p u f", p=P)

    ctx = ExitStack()
    with ctx:
        ctx.enter_context(nc.allow_non_contiguous_dma("index columns and broadcasts"))

        def alloc(stack):
            used = []

            def sem(name):
                used.append(nc.alloc_semaphore(name))
                return used[-1]

            def end():
                if used:
                    nc.clear_and_free_semaphores(used)
                    nc.all_engine_barrier()

            stack.callback(end)
            return (lambda name, shape, dt=f32: stack.enter_context(nc.sbuf_tensor(name, shape, dt)),
                    sem, lambda name: [sem(f"{name}_{b}") for b in range(2)])

        sb = lambda name, shape, dt=f32: ctx.enter_context(nc.sbuf_tensor(name, shape, dt))
        two = [ctx.enter_context(nc.psum_tensor(f"banks{i}", [128, 2, 512], f32)) for i in range(4)]
        bank = [two[i // 2][:, i % 2, :] for i in range(8)]

        pool_went_on, pe_went_on = (ctx.enter_context(nc.semaphore(n)) for n in ("pool_went_on", "pe_went_on"))

        ident = sb("ident", [128, 128])
        src_i, dst_i = sb("src_i", [P, T], i32), sb("dst_i", [P, T], i32)
        dst_end = sb("dst_end", [P, T], i32)
        dinv_d = sb("dinv_d", [P, T])
        w_s = sb("w_s", [P, T])
        own = sb("own", [P, T])
        counts = [sb(f"count{k}", [1, 2], i32) for k in range(LISTS + 1)]
        gi_i = sb("gi_i", [P, T], i32)
        srcS_i, dstS_i, srcS_end = sb("srcS_i", [P, T], i32), sb("dstS_i", [P, T], i32), sb("srcS_end", [P, T], i32)
        mask_d = sb("mask_d", [C, E], u8)
        head = sb("head", [P, T, HEAD + 1])
        khl = sb("khl", [P, T, 3])
        place = sb("place", [P, ND])
        pos_f = sb("pos_f", [P, T])
        iota_lo, iota_hi = sb("iota_lo", [P, ND], f16), sb("iota_hi", [P, P], f16)
        tri_lt = sb("tri_lt", [P, P])
        node0 = sb("node0", [P, 1])
        w3_sb, w4_sb = sb("w3_sb", [2 * C, HID]), sb("w4_sb", [HID, C])
        w1_sb, w1u = sb("w1_sb", [3 * ATTR, HID]), sb("w1u", [HID, 1])
        w2_sb = sb("w2_sb", [HID, C])
        wl3_sb, wu_sb = sb("wl3_sb", [C, 2, C]), sb("wu_sb", [C, C])
        b3_sb, b1_sb, b1u, bl3_sb = sb("b3_sb", [HID, 1]), sb("b1_sb", [HID, 1]), sb("b1u", [HID, 1]), sb("bl3_sb", [C, 1])
        b4B, b2B, c0B = sb("b4B", [P, C]), sb("b2B", [P, C]), sb("c0B", [P, C])
        rat = sb("rat", [P, TERMS + 1])
        tB, uB, scale = sb("tB", [P, 1]), sb("uB", [HID, 1]), sb("scale", [P, 1])
        eps = sb("eps", [P, 1])
        one = sb("one", [P, 1])
        tri_k = sb("tri_k", [P, P])
        ones_pp, ones_t = sb("ones_pp", [P, P]), sb("ones_t", [P, T])
        nowhere = sb("nowhere", [P, 2 * U2])
        nowhere_i = sb("nowhere_i", [P, 2 * U2], i32)
        starts, starts_i = sb("starts", [1, T // 2]), sb("starts_i", [1, T // 2], i32)

        def brd(a, n, f=C):
            return a.unsqueeze(2).to_broadcast([P, n, f])

        def rows(a, n):
            return a.unsqueeze(1).to_broadcast([P, n, a.shape[-1]])

        def exists(n, m, k):
            return not isinstance(m, int) or 0 <= 2 * m + k < n

        def pipeline(eng, turn, n, ahead, behind, first=None):
            lo, hi = (behind + 1) // 2, (n - ahead) // 2
            for g in range(-ahead if first is None else first, 2 * lo):
                turn(0, g)
            with eng.Fori(0, hi - lo) as j:
                turn(j + lo, 0)
                turn(j + lo, 1)
            for k in range(n + behind - 2 * hi):
                turn(hi, k)

        def ln_centre(dve, link, X, s, xc, n):
            link(dve.tensor_reduce(out=s, in_=X, axis=AX.X, op=ALU.add))
            return dve.scalar_tensor_tensor(out=xc, in0=brd(s, n), scalar=-1.0 / C, in1=X, op0=ALU.mult, op1=ALU.add)

        def ln_square(act, xc, sq):
            return act.activation(sq, xc, ACT.Square)

        def ln_var(dve, sq, v):
            return dve.tensor_reduce(out=v, in_=sq, axis=AX.X, op=ALU.add)

        def ln_std(act, v, sd):
            return act.activation(sd, v, ACT.Sqrt, bias=eps[:, :], scale=1.0 / C)

        def ln_relu(dve, link, sd, rs, xc, h, n):
            link(dve.reciprocal(rs, sd))
            return dve.scalar_tensor_tensor(out=h, in0=xc, scalar=0.0, in1=brd(rs, n), op0=ALU.max, op1=ALU.mult)

        def fwd(pe, ps, X, f, last_sem):
            pe.sem_inc(pe_went_on, 1)
            for u in range(U):
                ins = pe.transpose(ps[0:f, u * P:(u + 1) * P], X[:, u, 0:f], ident[0:P, 0:P])
            ins.then_inc(last_sem, 1)

        def fwd_pairs(pe, ps, X, last_sem):
            pe.sem_inc(pe_went_on, 1)
            for i in range(U // 2):
                ins = pe.transpose(ps[0:2 * C, i * P:(i + 1) * P], X[:, 2 * i * C:(2 * i + 2) * C], ident[0:P, 0:P])
            ins.then_inc(last_sem, 1)

        def w3_products(pe, ps, HT, last_sem):
            for odd in range(2):
                ins = pe.matmul(ps[0:HID, odd, 0:CE // 2], w3_sb[odd * C:(odd + 1) * C, :],
                                HT[odd * C:(odd + 1) * C, :], start=True, stop=True)
            ins.then_inc(last_sem, 1)

        def tile_at(u):
            at = (u % 2) * (CE // 2) + u // 2 * P
            return slice(at, at + P)

        def back(pe, ps, S, f, last_sem):
            pe.sem_inc(pe_went_on, 1)
            for u in range(U):
                ins = pe.transpose(ps[0:P, u * f:(u + 1) * f], S[0:f, u * P:(u + 1) * P], ident[0:f, 0:f])
            ins.then_inc(last_sem, 1)

        r3 = lambda a, n=U: a[:, :].rearrange("p (u f) -> p u f", u=n)

        def prows(ps, f=C):
            return ps[0:P, 0:U * f].rearrange("p (u f) -> p u f", f=f)

        with ExitStack() as st:
            sb, sem, sems = alloc(st)
            dnx_i = sb("dnx_i", [P, T], i32)
            dst_row, dst_row0 = (sb(n, [T // 2, 2 * P], i32) for n in ("dst_row", "dst_row0"))
            same = sb("same", [T // 2, 2 * P], u8)
            zeros, none = sb("zeros", [P, TW]), sb("none", [P, 4])
            key = [sb("srcF", [P, T]), sb("dstF", [P, T])]
            hi, lo = [sb(f"hi{k}", [P, T]) for k in range(2)], [sb(f"lo{k}", [P, T]) for k in range(2)]
            q_i, tmp, tmp2 = sb("q_i", [P, T], i32), sb("tmp", [P, T]), sb("tmp2", [P, T])
            iota_i = sb("iota_i", [P, ND], i32)
            tri = tri_k
            h0 = sb("h0", [HID, P])
            lo_hot = [[sb(f"lo_hot{k}{b}", [P, ND], f16) for b in range(2)] for k in range(2)]
            hi_hot = [[sb(f"hi_hot{k}{b}", [P, P], f16) for b in range(2)] for k in range(2)]
            cnt, incl, ones = sb("cnt", [P, ND]), sb("incl", [P, ND]), sb("ones", [P, ND])
            words = sb("words", [P, ND, NW])
            endp_n, dinv_n = words[:, :, 0], words[:, :, 1]
            offs = sb("offs", [P, 1])
            node0_i = sb("node0_i", [P, 1], i32)
            hist = [bank[0], bank[1], bank[2], bank[3]]

            loaded, built, stored = sem("loaded"), sem("built"), sem("stored")
            dlink = sem("dve_link")
            head_ready, c0_mm = sem("head_ready"), sem("c0_mm")
            hot_ready, hot_used, hist_done = sems("hot_ready"), sems("hot_used"), sem("hist_done")
            offs_in, offs_mm = sem("offs_in"), sem("offs_mm")
            tabs_ready = sem("tabs_ready")
            none_begun, empty_ready, filled, same_ready, same_moved = sem("none_begun"), sem("empty_ready"), sem("filled"), sem("same_ready"), sem("same_moved")
            with nc.Block() as block:
                @block.sync
                def _(sp):
                    col = lambda a: a.rearrange("(n o) -> n o", o=1)
                    for dst_sb, a in (
                            (src_i[:, :], tile_major(src_pad[1:E + 1])), (dst_i[:, :], tile_major(dst_pad[1:E + 1])),
                            (dnx_i[:, :], tile_major(dst_pad[2:E + 2])),
                            (dst_row[:, :], tile_rows(dst_pad[1:E + 1])), (dst_row0[:, :], tile_rows(dst_pad[0:E])), (head[:, :, 4:5], w.rearrange("(t p o) -> p t o", p=P, o=1)),
                            (w3_sb[0:C, :], w3t), (w3_sb[C:2 * C, :], w3t), (w4_sb[:, :], w4t), (w2_sb[:, :], w2),
                            (w1_sb[:, :], w1[0:3 * ATTR, :]),
                            (w1u[:, :], w1[3 * ATTR:3 * ATTR + 1, :].rearrange("o h -> h o")),
                            (wl3_sb[:, :, :], wl3.rearrange("(s c) o -> c s o", s=2)),
                            (b3_sb[:, :], col(b3)), (b1_sb[:, :], col(b1)), (bl3_sb[:, :], col(bl3)),
                            (b4B[:, :], b4.partition_broadcast(P)), (b2B[:, :], b2.partition_broadcast(P)),
                            (rat[:, :], ratios.partition_broadcast(P)), (tB[:, :], t_in.partition_broadcast(P)),
                            (uB[:, :], u_in[0, :].partition_broadcast(HID))):
                        sp.dma_start(dst_sb, a).then_inc(loaded, 16)
                    sp.wait_ge(empty_ready, 2)
                    part = lambda a: a.rearrange("(p c) f -> p c f", p=P)
                    for table in (*terms, series):
                        n = table.shape[1]
                        sp.dma_start(part(table), zeros[:, 0:n].unsqueeze(1).to_broadcast([P, NR // P, n])).then_inc(filled, 16)
                    for table in lists.values():
                        sp.dma_start(part(table), none[:, :].unsqueeze(1).to_broadcast([P, NR // P, 4])).then_inc(filled, 16)
                    sp.wait_ge(same_ready, 1)
                    sp.dma_start(tile_rows(same_dst), same[:, :]).then_inc(same_moved, 16)
                    sp.wait_ge(same_moved, 16)
                    sp.dma_start(mask_d[:, :], same_dst.partition_broadcast(C)).then_inc(same_moved, 16)
                    sp.wait_ge(same_moved, 32)
                    sp.wait_ge(filled, 16 * (4 + len(lists)))
                    sp.wait_ge(tabs_ready, 2)
                    sp.dma_start(node_words.rearrange("(p c) o -> p c o", p=P), words[:, :, :]).then_inc(stored, 16)
                    sp.wait_ge(stored, 16)

                NLOAD = 16 * 21

                @block.gpsimd
                def _(pool):
                    pool.memset(zeros[:, :], 0.0).then_inc(empty_ready, 1)
                    pool.memset(none[:, :], 0.0).then_inc(none_begun, 1)
                    pool.wait_ge(none_begun, 1)
                    pool.memset(none[:, 0:1], -1.0).then_inc(none_begun, 1)
                    pool.wait_ge(none_begun, 2)
                    pool.memset(none[:, 1:2], float(E)).then_inc(empty_ready, 1)
                    pool.memset(ident[:, :], 0.0).then_inc(built, 1)
                    pool.memset(tri[:, :], 1.0).then_inc(built, 1)
                    pool.memset(tri_lt[:, :], 1.0).then_inc(built, 1)
                    pool.iota(iota_i[:, :], pattern=[[1, ND]], base=0, channel_multiplier=0).then_inc(built, 1)
                    pool.iota(node0_i[:, :], pattern=[[1, 1]], base=0, channel_multiplier=ND).then_inc(built, 1)
                    pool.iota(nowhere_i[:, :], pattern=[[P, 2 * U2]], base=NOWHERE, channel_multiplier=1).then_inc(built, 1)
                    pool.iota(starts_i[:, :], pattern=[[2 * P, T // 2]], base=0, channel_multiplier=0).then_inc(built, 1)
                    pool.wait_ge(built, 7)
                    pool.affine_select(out=ident[:, :], in_=ident[:, :], compare_op=ALU.not_equal, fill=1.0, base=0,
                                       pattern=[[-1, 128]], channel_multiplier=1).then_inc(built, 1)
                    pool.affine_select(out=tri[:, :], in_=tri[:, :], compare_op=ALU.is_gt, fill=0.0, base=0,
                                       pattern=[[1, P]], channel_multiplier=-1).then_inc(built, 1)
                    pool.affine_select(out=tri_lt[:, :], in_=tri_lt[:, :], compare_op=ALU.is_gt, fill=0.0, base=0,
                                       pattern=[[-1, P]], channel_multiplier=1).then_inc(built, 1)

                @block.scalar
                def _(act):
                    act.wait_ge(hist_done, 1)
                    for a in range(2):
                        ins = act.activation(dinv_n[:, a * HALF:(a + 1) * HALF], hist[2 + a][0:P, 0:HALF], ACT.Sqrt, bias=one[:, :])
                    ins.then_inc(head_ready, 1)

                @block.tensor
                def _(pe):
                    pe.wait_ge(head_ready, 1)
                    pe.matmul(bank[4][0:P, 0:C], h0[:, :], w2_sb[:, :], start=True, stop=True).then_inc(c0_mm, 1)
                    with pe.Fori(0, T // 2 - 1) as j:
                        for b in range(2):
                            pe.wait_ge(hot_ready[b], j + 1)
                            for k in range(2):
                                for a in range(2):
                                    ins = pe.matmul(hist[2 * k + a][0:P, 0:HALF], hi_hot[k][b][:, :],
                                                    lo_hot[k][b][:, a * HALF:(a + 1) * HALF], start=False, stop=False,
                                                    skip_group_check=True)
                            ins.then_inc(hot_used[b], 1)
                    for b in range(2):
                        pe.wait_ge(hot_ready[b], T // 2)
                        for k in range(2):
                            for a in range(2):
                                ins = pe.matmul(hist[2 * k + a][0:P, 0:HALF], hi_hot[k][b][:, :],
                                                lo_hot[k][b][:, a * HALF:(a + 1) * HALF], start=False, stop=b == 1,
                                                skip_group_check=True)
                        if b == 0:
                            ins.then_inc(hot_used[b], 1)
                    ins.then_inc(hist_done, 1)
                    pe.wait_ge(offs_in, 1)
                    pe.matmul(bank[4][0:P, 128:129], tri[:, :], incl[:, ND - 1:ND], start=True, stop=True).then_inc(offs_mm, 1)

                @block.vector
                def _(dve):
                    ch = Chain(dve, dlink)
                    link = ch.link
                    for k in range(4):
                        link(dve.memset(hist[k][:, :], 0.0))
                    dve.memset(eps[:, :], EPS)
                    dve.memset(one[:, :], 1.0)
                    dve.memset(ones[:, :], 1.0)
                    dve.memset(ones_pp[:, :], 1.0)
                    dve.memset(ones_t[:, :], 1.0)
                    dve.wait_ge(loaded, NLOAD)
                    dve.wait_ge(built, 10)
                    dve.tensor_tensor(out=same[:, :], in0=dst_row[:, :], in1=dst_row0[:, :], op=ALU.is_equal).then_inc(same_ready, 1)
                    dve.tensor_copy(iota_lo[:, :], iota_i[:, :])
                    dve.tensor_copy(iota_hi[:, :], iota_i[:, 0:P])
                    dve.tensor_copy(nowhere[:, :], nowhere_i[:, :])
                    dve.tensor_copy(starts[:, :], starts_i[:, :])
                    link(dve.tensor_copy(node0[:, :], node0_i[:, :]))
                    dve.tensor_tensor(out=wu_sb[:, :], in0=wl3_sb[:, 0, :], in1=wl3_sb[:, 1, :], op=ALU.subtract)
                    dve.tensor_scalar(scale[:, :], tB[:, :], 1e-8, -1.0 / N_SUB, ALU.max, ALU.mult)
                    link(dve.scalar_tensor_tensor(out=b1u[:, :], in0=w1u[:, :], scalar=uB[:, 0:1], in1=b1_sb[:, :],
                                                  op0=ALU.mult, op1=ALU.add))
                    dve.tensor_scalar(h0[:, :], b1u[:, 0:1].to_broadcast([HID, P]), 0.0, None, ALU.max).then_inc(head_ready, 1)
                    for k, key_i in enumerate((src_i, dst_i)):
                        link(dve.tensor_copy(key[k][:, :], key_i[:, :]))
                        link(dve.tensor_scalar(q_i[:, :], key[k][:, :], 1.0 / ND, None, ALU.mult))
                        link(dve.tensor_copy(hi[k][:, :], q_i[:, :]))
                        link(dve.scalar_tensor_tensor(out=lo[k][:, :], in0=hi[k][:, :], scalar=-float(ND), in1=key[k][:, :],
                                                      op0=ALU.mult, op1=ALU.add))
                        link(dve.tensor_scalar(tmp[:, :], lo[k][:, :], 0.0, None, ALU.is_lt))
                        link(dve.tensor_tensor(out=hi[k][:, :], in0=hi[k][:, :], in1=tmp[:, :], op=ALU.subtract))
                        link(dve.scalar_tensor_tensor(out=lo[k][:, :], in0=hi[k][:, :], scalar=-float(ND), in1=key[k][:, :],
                                                      op0=ALU.mult, op1=ALU.add))
                        link(dve.tensor_scalar(tmp[:, :], lo[k][:, :], float(ND), None, ALU.is_ge))
                        link(dve.tensor_tensor(out=hi[k][:, :], in0=hi[k][:, :], in1=tmp[:, :], op=ALU.add))
                        link(dve.scalar_tensor_tensor(out=lo[k][:, :], in0=hi[k][:, :], scalar=-float(ND), in1=key[k][:, :],
                                                      op0=ALU.mult, op1=ALU.add))
                    for i, a in enumerate((key[0], hi[0], lo[0])):
                        dve.tensor_copy(khl[:, :, i], a[:, :])
                    link(dve.tensor_tensor(out=tmp[:, :], in0=dst_i[:, :], in1=dnx_i[:, :], op=ALU.not_equal))
                    link(dve.scalar_tensor_tensor(out=tmp2[:, :], in0=key[1][:, :], scalar=-float(N), in1=tmp[:, :],
                                                  op0=ALU.add, op1=ALU.mult))
                    link(dve.tensor_scalar(dst_end[:, :], tmp2[:, :], float(N), None, ALU.add))
                    dve.memset(head[:, :, 2:4], 0.0)
                    dve.memset(head[:, :, HEAD], 0.0)
                    dve.tensor_copy(head[:, :, 0], key[0][:, :])
                    dve.tensor_copy(head[:, :, 1], key[1][:, :])
                    link(dve.tensor_scalar(head[:, :, 4], head[:, :, 4], scale[:, 0:1], None, ALU.mult))
                    dve.wait_ge(c0_mm, 1)
                    link(dve.tensor_tensor(out=c0B[:, :], in0=bank[4][0:P, 0:C], in1=b2B[:, :], op=ALU.add))
                    with dve.Fori(0, T // 2) as j:
                        for b in range(2):
                            t = j * 2 + b
                            dve.wait_ge(hot_used[b], j)
                            for k in range(2):
                                dve.tensor_scalar(hi_hot[k][b][:, :], iota_hi[:, :], hi[k][:, bass.ds(t, 1)], None, ALU.is_equal)
                                ins = dve.tensor_scalar(lo_hot[k][b][:, :], iota_lo[:, :], lo[k][:, bass.ds(t, 1)], None, ALU.is_equal)
                            ins.then_inc(hot_ready[b], 1)
                    dve.wait_ge(hist_done, 1)
                    for a in range(2):
                        ins = dve.tensor_copy(cnt[:, a * HALF:(a + 1) * HALF], hist[a][0:P, 0:HALF])
                    link(ins)
                    dve.tensor_tensor_scan(incl[:, :], ones[:, :], cnt[:, :], 0.0, ALU.mult, ALU.add).then_inc(offs_in, 1)
                    dve.wait_ge(offs_mm, 1)
                    link(dve.tensor_copy(offs[:, :], bank[4][0:P, 128:129]))
                    link(dve.tensor_scalar(endp_n, incl[:, :], offs[:, 0:1], None, ALU.add))
                    link(dve.tensor_tensor(out=place[:, :], in0=endp_n, in1=cnt[:, :], op=ALU.subtract))
                    link(dve.tensor_scalar(ones[:, :], cnt[:, :], 1.0, None, ALU.max))
                    link(dve.reciprocal(words[:, :, 2], ones[:, :]))
                    link(dve.tensor_scalar(cnt[:, :], cnt[:, :], 0.0, None, ALU.is_gt))
                    link(dve.scalar_tensor_tensor(out=endp_n, in0=endp_n, scalar=-float(E + 1), in1=cnt[:, :],
                                                  op0=ALU.add, op1=ALU.mult))
                    dve.tensor_scalar(endp_n, endp_n, float(E), None, ALU.add).then_inc(tabs_ready, 1)
                    dve.wait_ge(head_ready, 2)
                    link(dve.reciprocal(dinv_n, dinv_n))
                    for a in range(2):
                        ins = dve.tensor_scalar(cnt[:, a * HALF:(a + 1) * HALF], hist[2 + a][0:P, 0:HALF], 1.0, None, ALU.add)
                    link(ins)
                    link(dve.tensor_tensor(out=cnt[:, :], in0=cnt[:, :], in1=dinv_n, op=ALU.mult))
                    link(dve.tensor_tensor(out=cnt[:, :], in0=cnt[:, :], in1=dinv_n, op=ALU.mult))
                    link(dve.tensor_scalar(cnt[:, :], cnt[:, :], -0.5, 1.5, ALU.mult, ALU.add))
                    dve.tensor_tensor(out=dinv_n, in0=dinv_n, in1=cnt[:, :], op=ALU.mult).then_inc(tabs_ready, 1)

            with ExitStack() as s2:
                sb, sem, sems = alloc(s2)
                GC = 2 * U
                GN = ND // GC
                UW = T // GN
                ixd, ixs = ([sb(f"{n}{b}", [P, UW], i32) for b in range(2)] for n in ("ixd", "ixs"))
                gvd, gvs = ([sb(f"{n}{b}", [P, UW * NW]) for b in range(2)] for n in ("gvd", "gvs"))
                sentinel = sb("sentinel", [1, 2])
                got, begun, pads, rlink = sems("got"), sem("begun"), sem("pads"), sem("index_link")
                words_link, xoc_r = sem("words_link"), sem("xoc_r")
                XB, Q, XO, XOC, H2, O = ([sb(f"dn_{n}{b}", [P, GC * C]) for b in range(2)] for n in ("xb", "q", "x1", "x1c", "h2", "o"))
                HX = [sb(f"dn_hx{b}", [P, GC, 2 * C]) for b in range(2)]
                X = [t[:, :, C:2 * C] for t in HX]
                H1 = [sb(f"dn_h1{b}", [P, GC * C]) for b in range(2)]
                hx_r = sem("hx_r")
                XC, SQ = [sb(f"dn_xc{i}", [P, GC * C]) for i in range(2)], [sb(f"dn_sq{i}", [P, GC * C]) for i in range(2)]
                s_, v_, sd_, rs_ = ([sb(f"dn_{n}{i}", [P, GC]) for i in range(2)] for n in ("sum", "var", "std", "rstd"))
                HT, Z = [sb(f"dn_hT{h}", [2 * C, CE // 2]) for h in range(2)], [sb(f"dn_z{h}", [HID, CE]) for h in range(2)]
                x_in, q_stored, hx_stored, h_stored, o_stored = (sems(n) for n in ("x_in", "q_stored", "hx_stored", "h_stored", "o_stored"))
                centred, squared, var_r, std_r, h_r = sems("centred"), sems("squared"), sems("var_r"), sems("std_r"), sem("h_r")
                hT_mm, hT_r, z_mm, z_r, q_mm = sem("hT_mm"), sem("hT_r"), sem("z_mm"), sem("z_r"), sem("q_mm")
                xb_r, q_r, x1_r, o_r, dl = sem("xb_r"), sem("q_r"), sem("x1_r"), sem("o_r"), [sem(f"dense_link{i}") for i in range(4)]

                rG = lambda a: r3(a, GC)
                node_cols = lambda a, g: a.rearrange("(p c) f -> p c f", p=P)[:, bass.ds(g * GC, GC), :]

                with nc.Block() as block:
                    @block.gpsimd
                    def _(pool):
                        pool.memset(sentinel[:, :], -1.0).then_inc(begun, 1)
                        def turn(m, k):
                            g = 2 * m + k
                            a = (k + 1) % 2
                            if exists(GN, m, k + 1):
                                pool.wait_ge(x_in[a], (m + (k + 1) // 2) * 16 + 16)
                                if exists(GN, m, k - 1):
                                    pool.wait_ge(x1_r, g)
                                pool.sem_inc(pool_went_on, 1)
                                pool.tensor_tensor(out=rG(XB[a]), in0=X[a], in1=rows(b4B[:, :], GC), op=ALU.add).then_inc(xb_r, 1)
                            if exists(GN, m, k - 1):
                                pool.wait_ge(x1_r, g)
                                if exists(GN, m, k - 3):
                                    pool.wait_ge(o_r, g - 2)
                                pool.sem_inc(pool_went_on, 1)
                                pool.tensor_tensor(out=rG(XOC[a]), in0=rG(XO[a]), in1=rows(c0B[:, :], GC), op=ALU.add).then_inc(xoc_r, 1)
                                cols = bass.ds((g - 1) * UW, UW)
                                pool.wait_ge(got[a], (m + (k - 1) // 2) * (32 * UW) + 32 * UW)
                                pool.sem_inc(pool_went_on, 1)
                                pool.tensor_copy(dinv_d[:, cols], r3(gvd[a], UW)[:, :, 1])
                                pool.tensor_copy(head[:, cols, 2], r3(gvd[a], UW)[:, :, 0])
                                pool.tensor_copy(head[:, cols, HEAD], r3(gvs[a], UW)[:, :, 2])
                                Chain(pool, words_link, g - 1).link(pool.tensor_copy(head[:, cols, 3], r3(gvs[a], UW)[:, :, 0]))
                            if exists(GN, m, k + 1):
                                cols = bass.ds((g + 1) * UW, UW)
                                pool.sem_inc(pool_went_on, 1)
                                pool.tensor_copy(ixs[a][:, :], src_i[:, cols])
                                Chain(pool, rlink, g + 1).link(pool.tensor_copy(ixd[a][:, :], dst_i[:, cols]))
                                pool.sem_inc(pool_went_on, 1)
                                for u in range(UW):
                                    for to, ix in ((gvd, ixd), (gvs, ixs)):
                                        pool.indirect_dma_start(out=to[a][:, u * NW:(u + 1) * NW], out_offset=None, in_=node_words,
                                                                in_offset=bass.IndirectOffsetOnAxis(ap=ix[a][:, u:u + 1], axis=0))\
                                            .then_inc(got[a], 16)

                        pipeline(pool, turn, GN, 1, 1)

                    @block.sync
                    def _(sp):
                        sp.wait_ge(begun, 1)
                        sp.dma_start(srcs_pad[0:1].rearrange("(o n) -> o n", o=1), sentinel[0:1, 0:1]).then_inc(pads, 16)
                        sp.dma_start(srcs_pad[E + 1:E + 2].rearrange("(o n) -> o n", o=1), sentinel[0:1, 1:2]).then_inc(pads, 16)
                        sp.wait_ge(pads, 32)
                        sp.dma_start(X[0], node_cols(x, 0)).then_inc(x_in[0], 16)

                        def turn(m, k):
                            g = 2 * m + k
                            b, q, a = k % 2, m + k // 2, (k - 1) % 2
                            if exists(GN, m, k - 1):
                                sp.wait_ge(q_r, g)
                                sp.dma_start(node_cols(qs, g - 1), rG(Q[a])).then_inc(q_stored[a], 16)
                            if exists(GN, m, k):
                                sp.wait_ge(hx_r, g + 1)
                                sp.dma_start(node_cols(hx, g), HX[b][:, :, :]).then_inc(hx_stored[b], 16)
                            if exists(GN, m, k - 2):
                                sp.wait_ge(o_r, g - 1)
                                sp.dma_start(node_cols(h1, g - 2), rG(H2[b])).then_inc(h_stored[b], 16)
                                sp.dma_start(node_cols(out, g - 2), rG(O[b])).then_inc(o_stored[b], 16)
                            if exists(GN, m, k + 2):
                                if exists(GN, m, k):
                                    sp.wait_ge(hx_stored[b], q * 16 + 16)
                                    sp.wait_ge(hT_mm, g * 2 + 2)
                                    sp.wait_ge(xb_r, g + 1)
                                sp.dma_start(X[b], node_cols(x, g + 2)).then_inc(x_in[b], 16)

                        pipeline(sp, turn, GN, 2, 2, first=-1)
                        for stored in (q_stored, hx_stored, h_stored, o_stored):
                            for b in range(2):
                                sp.wait_ge(stored[b], 16 * (GN // 2))

                    @block.vector
                    def _(dve):
                        def turn(m, k):
                            g = 2 * m + k
                            b, a = k % 2, (k + 1) % 2
                            if exists(GN, m, k):
                                dve.wait_ge(squared[0], g + 1)
                                ln_var(dve, rG(SQ[0]), v_[0][:, :]).then_inc(var_r[0], 1)
                            if exists(GN, m, k - 2):
                                dve.wait_ge(squared[1], g - 1)
                                ln_var(dve, rG(SQ[1]), v_[1][:, :]).then_inc(var_r[1], 1)
                            if exists(GN, m, k):
                                ch = Chain(dve, dl[0], g * 2)
                                dve.wait_ge(std_r[0], g + 1)
                                ch.link(dve.reciprocal(rs_[0][:, :], sd_[0][:, :]))
                                ch.link(dve.tensor_tensor(out=rs_[0][:, :], in0=rs_[0][:, :], in1=words[:, bass.ds(g * GC, GC), 1], op=ALU.mult))
                                if exists(GN, m, k - 2):
                                    dve.wait_ge(hT_mm, (g - 1) * 2)
                                    dve.wait_ge(hx_r, g - 1)
                                dve.scalar_tensor_tensor(out=rG(H1[b]), in0=rG(XC[0]), scalar=0.0, in1=brd(rs_[0][:, :], GC),
                                                         op0=ALU.max, op1=ALU.mult).then_inc(h_r, 1)
                            if exists(GN, m, k - 2):
                                ch = Chain(dve, dl[1], (g - 2) * 2)
                                dve.wait_ge(std_r[1], g - 1)
                                if exists(GN, m, k - 4):
                                    dve.wait_ge(h_stored[b], (m + (k - 4) // 2) * 16 + 16)
                                    dve.wait_ge(o_stored[b], (m + (k - 4) // 2) * 16 + 16)
                                ch.link(ln_relu(dve, ch.link, sd_[1][:, :], rs_[1][:, :], rG(XC[1]), rG(H2[b]), GC))
                                dve.wait_ge(xoc_r, g - 1)
                                dve.tensor_tensor(out=O[b][:, :], in0=H2[b][:, :], in1=XOC[b][:, :], op=ALU.add).then_inc(o_r, 1)
                            if exists(GN, m, k - 1):
                                dve.wait_ge(q_r, g)
                                dve.wait_ge(xb_r, g)
                                if exists(GN, m, k - 3):
                                    dve.wait_ge(xoc_r, g - 2)
                                dve.tensor_tensor(out=XO[a][:, :], in0=XB[a][:, :], in1=Q[a][:, :], op=ALU.add).then_inc(x1_r, 1)
                            if exists(GN, m, k + 1):
                                ch = Chain(dve, dl[2], g + 1)
                                dve.wait_ge(x_in[a], (m + (k + 1) // 2) * 16 + 16)
                                summed = ch.put(dve.tensor_reduce(out=s_[0][:, :], in_=X[a], axis=AX.X, op=ALU.add))
                                ch.need(summed)
                                dve.scalar_tensor_tensor(out=rG(XC[0]), in0=brd(s_[0][:, :], GC), scalar=-1.0 / C, in1=X[a],
                                                         op0=ALU.mult, op1=ALU.add).then_inc(centred[0], 1)
                            if exists(GN, m, k - 1):
                                ch = Chain(dve, dl[3], g - 1)
                                dve.wait_ge(x1_r, g)
                                summed = ch.put(dve.tensor_reduce(out=s_[1][:, :], in_=rG(XO[a]), axis=AX.X, op=ALU.add))
                                ch.need(summed)
                                dve.scalar_tensor_tensor(out=rG(XC[1]), in0=brd(s_[1][:, :], GC), scalar=-1.0 / C, in1=rG(XO[a]),
                                                         op0=ALU.mult, op1=ALU.add).then_inc(centred[1], 1)

                        pipeline(dve, turn, GN, 1, 2)

                    @block.scalar
                    def _(act):
                        def turn(m, k):
                            if exists(GN, m, k):
                                act.wait_ge(var_r[0], 2 * m + k + 1)
                                ln_std(act, v_[0][:, :], sd_[0][:, :]).then_inc(std_r[0], 1)
                            if exists(GN, m, k - 2):
                                act.wait_ge(var_r[1], 2 * m + k - 1)
                                ln_std(act, v_[1][:, :], sd_[1][:, :]).then_inc(std_r[1], 1)
                            if exists(GN, m, k - 1):
                                b = (k - 1) % 2
                                act.wait_ge(q_mm, 2 * m + k)
                                if exists(GN, m, k - 3):
                                    act.wait_ge(q_stored[b], (m + (k - 3) // 2) * 16 + 16)
                                act.activation(Q[b][:, :], bank[6][0:P, 0:GC * C], ACT.Copy).then_inc(q_r, 1)
                            if exists(GN, m, k):
                                for h in range(2):
                                    act.wait_ge(hT_mm, (2 * m + k) * 2 + h + 1)
                                    act.activation(HT[h][:, :], bank[h][0:2 * C, 0:CE // 2], ACT.Copy).then_inc(hT_r, 1)
                                act.activation(HX[k % 2][:, :, 0:C], rG(H1[k % 2]), ACT.Copy).then_inc(hx_r, 1)
                            if exists(GN, m, k + 1):
                                act.wait_ge(centred[0], 2 * m + k + 2)
                                ln_square(act, XC[0][:, :], SQ[0][:, :]).then_inc(squared[0], 1)
                            if exists(GN, m, k):
                                for h in range(2):
                                    act.wait_ge(z_mm, (2 * m + k) * 2 + h + 1)
                                    act.activation(Z[h][:, :].rearrange("h (o e) -> h o e", o=2), two[1 + h][0:HID, :, 0:CE // 2], ACT.Relu, bias=b3_sb[:, :]).then_inc(z_r, 1)
                            if exists(GN, m, k - 1):
                                act.wait_ge(centred[1], 2 * m + k)
                                ln_square(act, XC[1][:, :], SQ[1][:, :]).then_inc(squared[1], 1)

                        pipeline(act, turn, GN, 1, 2)

                    @block.tensor
                    def _(pe):
                        def turn(m, k):
                            if not exists(GN, m, k):
                                return
                            pe.wait_ge(h_r, 2 * m + k + 1)
                            for h in range(2):
                                fwd_pairs(pe, bank[h], H1[k % 2][:, h * U * C:(h + 1) * U * C], hT_mm)
                            for h in range(2):
                                pe.wait_ge(hT_r, (2 * m + k) * 2 + h + 1)
                                w3_products(pe, two[1 + h], HT[h], z_mm)
                            for h in range(2):
                                pe.wait_ge(z_r, (2 * m + k) * 2 + h + 1)
                                for u in range(U):
                                    ins = pe.matmul(bank[6][0:P, (h * U + u) * C:(h * U + u + 1) * C], Z[h][:, tile_at(u)], w4_sb[:, :],
                                                    start=True, stop=True)
                            ins.then_inc(q_mm, 1)

                        pipeline(pe, turn, GN, 0, 0)


        def gather(pool, rows_sb, f, table, ix, sem_):
            for u in range(U):
                pool.indirect_dma_start(out=rows_sb[:, u * f:(u + 1) * f], out_offset=None, in_=table,
                                        in_offset=bass.IndirectOffsetOnAxis(ap=ix[:, u:u + 1], axis=0)).then_inc(sem_, 16)

        def scatter(pool, table, ix, rows_sb, f, sem_, limit=N):
            for u in range(U):
                pool.indirect_dma_start(out=table, out_offset=bass.IndirectOffsetOnAxis(ap=ix[:, u:u + 1], axis=0),
                                        in_=rows_sb[:, u * f:(u + 1) * f], in_offset=None,
                                        bounds_check=limit - 1, oob_is_err=False).then_inc(sem_, 16)

        def list_count(dve, link, n, fits, pairs_f, count, tiles):
            link(dve.tensor_copy(count[0:1, 1:2], n))
            link(dve.tensor_scalar(pairs_f, n, 1.0 / tiles, None, ALU.mult))
            link(dve.tensor_scalar(fits, starts[0:1, :], pairs_f, None, ALU.is_lt))
            link(dve.tensor_reduce(out=pairs_f, in_=fits, axis=AX.X, op=ALU.add))
            link(dve.tensor_scalar(count[0:1, 0:1], pairs_f, 1.0, None, ALU.max))

        def two_ahead(pool, gathers, scatters):
            gathers(0, 0)
            gathers(0, 1)
            with pool.Fori(0, PAIRS - 1) as j:
                for b in range(2):
                    gathers(j + 1, b)
                    scatters(j, b)
            for b in range(2):
                scatters(PAIRS - 1, b)

        class Sort:

            def __init__(self, alloc, first):
                sb, sem, sems = alloc
                self.first = first
                n = f"sort{first}_"
                self.src_b, self.hd, self.lt, self.hiT, self.eqk = ([sb(f"{n}{x}{i}", [P, P], i32 if x == "src" else f32) for i in range(2)] for x in ("src", "hd", "lt", "hiT", "eq"))
                self.lo_hot, self.hi_hot = [sb(f"{n}lo{i}", [P, ND], f16) for i in range(2)], [sb(f"{n}hi{i}", [P, P], f16) for i in range(2)]
                self.khl_t, self.occ, self.pos_t = ([sb(f"{n}{x}{i}", [P, w_]) for i in range(2)] for x, w_ in (("khl", 3), ("occ", 1), ("pos", 1)))
                self.ttj = sb(n + "products", [P, 2, HALF])
                self.src_loaded, self.src_free, self.hots_ready, self.sel_done = (sems(n + x) for x in ("src_loaded", "src_free", "hots_ready", "sel_done"))
                self.place_copied, self.place_added, self.pos_done = (sem(n + x) for x in ("place_copied", "place_added", "pos_done"))
                self.hot_link, self.pos_link = sem(n + "hot_link"), sem(n + "pos_link")
                self.run, self.sel = two[1], [two[2], two[3]]

            def loads(self, sp):
                with sp.Fori(0, CHUNKS) as c:
                    for i in range(2):
                        sp.wait_ge(self.src_free[i], c)
                        sp.dma_start(self.src_b[i][:, :], src_pad[bass.ds((c * 2 + i + self.first) * P + 1, P)].partition_broadcast(P))\
                          .then_inc(self.src_loaded[i], 16)

            def one_hots(self, dve, m, k, i):
                c = 2 * m + k
                if not exists(CHUNKS, m, k):
                    return
                LINKS = 4
                ch = Chain(dve, self.hot_link, (c * 2 + i) * LINKS)
                if exists(CHUNKS, m, k - 1):
                    dve.wait_ge(self.place_added, c * 2 + i)
                ch.put(dve.tensor_copy(self.khl_t[i][:, :], khl[:, bass.ds(c * 2 + i + self.first, 1), :]))
                dve.wait_ge(self.src_loaded[i], c * 16 + 16)
                ch.link(dve.tensor_scalar(self.hd[i][:, :], self.src_b[i][:, :], node0[:, 0:1], None, ALU.subtract))
                below = ch.put(dve.tensor_scalar(self.lt[i][:, :], self.hd[i][:, :], float(ND), None, ALU.is_lt))
                ch.need(below)
                dve.scalar_tensor_tensor(out=self.hiT[i][:, :], in0=self.hd[i][:, :], scalar=0.0, in1=self.lt[i][:, :], op0=ALU.is_ge, op1=ALU.mult)
                dve.tensor_scalar(self.hi_hot[i][:, :], iota_hi[:, :], self.khl_t[i][:, 1:2], None, ALU.is_equal)
                dve.tensor_scalar(self.lo_hot[i][:, :], iota_lo[:, :], self.khl_t[i][:, 2:3], None, ALU.is_equal)\
                   .then_inc(self.hots_ready[i], 1)
                ch.link(dve.scalar_tensor_tensor(out=self.eqk[i][:, :], in0=self.src_b[i][:, :], scalar=self.khl_t[i][:, 0:1], in1=tri_lt[:, :],
                                                 op0=ALU.is_equal, op1=ALU.mult, accum_out=self.occ[i][:, :]))
                dve.sem_inc(self.src_free[i], 1)
                assert ch.n == LINKS, ch.n

            def places(self, dve, m, k, i):
                c = 2 * m + k
                if not exists(CHUNKS, m, k):
                    return
                ch = Chain(dve, self.pos_link, c * 2 + i)
                dve.wait_ge(self.sel_done[i], c + 1)
                ch.link(dve.tensor_tensor_reduce(out=self.ttj[:, :, :], in0=self.lo_hot[i][:, :].rearrange("p (a c) -> p a c", a=2),
                                                 in1=self.sel[i][0:P, :, 0:HALF], scale=1.0, scalar=self.occ[i][:, 0:1],
                                                 op0=ALU.mult, op1=ALU.add, accum_out=self.pos_t[i][:, :]))
                dve.tensor_copy(pos_f[:, bass.ds(c * 2 + i + self.first, 1)], self.pos_t[i][:, :]).then_inc(self.pos_done, 1)

            def begin(self, pe):
                if self.first:
                    pe.sem_inc(self.place_added, 1)
                    return
                for a in range(2):
                    ins = pe.matmul(self.run[0:P, a, 0:HALF], ident[0:P, 0:P], place[:, a * HALF:(a + 1) * HALF],
                                    start=True, stop=False, skip_group_check=True)
                ins.then_inc(self.place_added, 1)

            def select(self, pe, c, i):
                pe.wait_ge(self.hots_ready[i], c + 1)
                pe.wait_ge(self.place_copied, c * 2 + i + 1)
                for a in range(2):
                    ins = pe.matmul(self.sel[i][0:P, a, 0:HALF], self.hiT[i][:, :], place[:, a * HALF:(a + 1) * HALF],
                                    start=True, stop=True)
                ins.then_inc(self.sel_done[i], 1)
                for a in range(2):
                    ins = pe.matmul(self.run[0:P, a, 0:HALF], self.hi_hot[i][:, :], self.lo_hot[i][:, a * HALF:(a + 1) * HALF],
                                    start=False, stop=False, skip_group_check=True)
                ins.then_inc(self.place_added, 1)

            def copy_places(self, act, c, i):
                act.wait_ge(self.place_added, c * 2 + i + 1)
                act.activation(place[:, :].rearrange("p (a c) -> p a c", a=2), self.run[0:P, :, 0:HALF], ACT.Copy)\
                   .then_inc(self.place_copied, 1)

        def pair_of_scans(b, j, s_r):
            return (s_r[1], j) if b == 0 else (s_r[0], j + 1)


        with ExitStack() as st:
            sb, sem, sems = alloc(st)
            XD, QSD = sb("x_dst", [P, T, C]), sb("qs_dst", [P, T, C])
            with ExitStack() as s2:
                sb, sem, sems = alloc(s2)
                GS, GD = [sb(f"c1_gs{b}", [P, U * C]) for b in range(2)], [sb(f"c1_gd{b}", [P, U * 2 * C]) for b in range(2)]
                S, AT, Z = [sb(f"c1_s{b}", [C, CE]) for b in range(2)], [sb(f"c1_aT{b}", [2 * C, CE // 2]) for b in range(2)], [sb(f"c1_z{b}", [HID, CE]) for b in range(2)]
                A, QO = [sb(f"c1_a{b}", [P, U * C]) for b in range(2)], [sb(f"c1_q{b}", [P, U * C]) for b in range(2)]
                ixs, ixd, ixe = ([sb(f"c1_{n}{b}", [P, U], i32) for b in range(2)] for n in ("ixs", "ixd", "ixe"))
                ix_r, ixe_r, got, mT, s_r, s_back, sum_r, x_kept, a_r, aT_mm, aT_r, z_mm, z_r, q_mm, q_r, q_kept, sent = (sems(f"c1_{n}") for n in (
                    "ix_ready", "ixe_ready", "gathered", "mT", "scanned", "sums_back", "sum", "x_kept", "agg", "aT_mm", "aT", "z_mm", "z", "q_mm", "q", "q_kept", "sent"))
                m1 = sem("c1_zero")
                sort = Sort((sb, sem, sems), 0)
                col_bank, row_bank = bank[0], bank[1]
                with nc.Block() as block:
                    @block.gpsimd
                    def _(pool):
                        def gathers(m, k):
                            b, q = k % 2, m + k // 2
                            pool.wait_ge(ix_r[b], q + 1)
                            if exists(CHUNKS, m, k - 2):
                                pool.wait_ge(mT[b], q)
                                pool.wait_ge(sum_r[b], q)
                                pool.wait_ge(x_kept[b], q)
                            pool.sem_inc(pool_went_on, 1)
                            gather(pool, GS[b], C, hx.rearrange("n (a f) -> (n a) f", a=2), ixs[b], got[b])
                            gather(pool, GD[b], 2 * C, hx, ixd[b], got[b])

                        def scatters(m, k):
                            b, q = k % 2, m + k // 2
                            pool.wait_ge(q_r[b], q + 1)
                            pool.wait_ge(ixe_r[b], q + 1)
                            pool.sem_inc(pool_went_on, 1)
                            scatter(pool, qs, ixe[b], QO[b], C, sent[b])

                        two_ahead(pool, gathers, scatters)
                        for b in range(2):
                            pool.wait_ge(sent[b], 16 * U * PAIRS)

                    @block.sync
                    def _(sp):
                        sort.loads(sp)

                    @block.vector
                    def _(dve):
                        for b in range(2):
                            ins = dve.memset(S[b][:, :], 0.0)
                        ins.then_inc(m1, 1)
                        dve.wait_ge(m1, 1)

                        def turn(m, k):
                            b, q = k % 2, m + k // 2
                            if not exists(CHUNKS, m, k):
                                if k > 0:
                                    sort.places(dve, m, k - 1, 1)
                                else:
                                    sort.one_hots(dve, m, k + 1, 0)
                                return
                            cols = bass.ds((2 * m + k) * U, U)
                            dinv = brd(dinv_d[:, cols], U)
                            own_rows = r3(GD[b])
                            dve.wait_ge(mT[b], q + 1)
                            if exists(CHUNKS, m, k - 1):
                                dve.wait_ge(s_r[1 - b], m + (k + 1) // 2)
                            dve.tensor_tensor_scan(S[b][:, :], mask_d[0:C, bass.ds((2 * m + k) * CE, CE)], col_bank[0:C, 0:CE],
                                                   S[1 - b][:, CE - 1:CE], ALU.mult, ALU.add).then_inc(s_r[b], 1)
                            dve.tensor_tensor(out=XD[:, cols, :], in0=own_rows[:, :, C:2 * C], in1=rows(b4B[:, :], U), op=ALU.add).then_inc(x_kept[b], 1)
                            sort.places(dve, m, k - 1, 1)
                            sort.one_hots(dve, m, k, 1)
                            dve.wait_ge(s_back[b], q + 1)
                            dve.tensor_tensor(out=r3(A[b]), in0=own_rows[:, :, 0:C], in1=prows(row_bank), op=ALU.add).then_inc(sum_r[b], 1)
                            dve.wait_ge(sum_r[b], q + 1)
                            dve.tensor_tensor(out=r3(A[b]), in0=r3(A[b]), in1=dinv, op=ALU.mult).then_inc(a_r[b], 1)
                            sort.places(dve, m, k, 0)
                            sort.one_hots(dve, m, k + 1, 0)
                            dve.wait_ge(q_mm[b], q + 1)
                            if exists(CHUNKS, m, k - 2):
                                dve.wait_ge(q_kept[b], q)
                                dve.wait_ge(sent[b], q * (16 * U))
                            dve.tensor_tensor(out=r3(QO[b]), in0=prows(row_bank), in1=dinv, op=ALU.mult).then_inc(q_r[b], 1)

                        pipeline(dve, turn, CHUNKS, 1, 1)

                    @block.scalar
                    def _(act):
                        def indices(c, i):
                            act.activation(ixs[i][:, :], src_i[:, bass.ds(c * U, U)], ACT.Copy, scale=2.0)
                            act.activation(ixd[i][:, :], dst_i[:, bass.ds(c * U, U)], ACT.Copy).then_inc(ix_r[i], 1)

                        def pair(j):
                            for b in range(2):
                                c = j * 2 + b
                                sort.copy_places(act, c, 0)
                                act.wait_ge(got[b], j * (32 * U) + 32 * U)
                                if not isinstance(j, int):
                                    indices(c + 2, b)
                                act.wait_ge(aT_mm[b], j + 1)
                                act.activation(AT[b][:, :], col_bank[0:2 * C, 0:CE // 2], ACT.Copy).then_inc(aT_r[b], 1)
                                act.wait_ge(z_mm[b], j + 1)
                                act.activation(Z[b][:, :].rearrange("h (o e) -> h o e", o=2), two[0][0:HID, :, 0:CE // 2], ACT.Relu, bias=b3_sb[:, :]).then_inc(z_r[b], 1)
                                sort.copy_places(act, c, 1)
                                act.wait_ge(sent[b], j * (16 * U))
                                act.activation(ixe[b][:, :], dst_end[:, bass.ds(c * U, U)], ACT.Copy).then_inc(ixe_r[b], 1)
                                act.wait_ge(q_r[b], j + 1)
                                act.activation(QSD[:, bass.ds(c * U, U), :], r3(QO[b]), ACT.Copy).then_inc(q_kept[b], 1)

                        for i in range(2):
                            indices(i, i)
                        with act.Fori(0, PAIRS - 1) as j:
                            pair(j)
                        pair(PAIRS - 1)

                    @block.tensor
                    def _(pe):
                        sort.begin(pe)

                        def turn(m, k):
                            b, q = k % 2, m + k // 2
                            if exists(CHUNKS, m, k):
                                sort.select(pe, 2 * m + k, 0)
                                pe.wait_ge(s_r[b], q + 1)
                                if exists(CHUNKS, m, k - 1):
                                    pe.wait_ge(q_r[1 - b], m + (k + 1) // 2)
                                back(pe, row_bank, S[b], C, s_back[b])
                                pe.wait_ge(a_r[b], q + 1)
                                fwd_pairs(pe, col_bank, A[b], aT_mm[b])
                                pe.wait_ge(aT_r[b], q + 1)
                                w3_products(pe, two[0], AT[b], z_mm[b])
                                pe.wait_ge(z_r[b], q + 1)
                                for u in range(U):
                                    ins = pe.matmul(row_bank[0:P, u * C:(u + 1) * C], Z[b][:, tile_at(u)], w4_sb[:, :], start=True, stop=True)
                                ins.then_inc(q_mm[b], 1)
                            if exists(CHUNKS, m, k + 1):
                                a, qa = (k + 1) % 2, m + (k + 1) // 2
                                pe.wait_ge(got[a], qa * (32 * U) + 32 * U)
                                fwd(pe, col_bank, r3(GS[a]), C, mT[a])
                            if exists(CHUNKS, m, k):
                                sort.select(pe, 2 * m + k, 1)

                        pipeline(pe, turn, CHUNKS, 1, 0)

            with ExitStack() as s2:
                sb, sem, sems = alloc(s2)
                G, Y, XC, SQ, H, O = ([sb(f"c2_{n}{b}", [P, U * C]) for b in range(2)] for n in ("g", "y", "xc", "sq", "h", "o"))
                s_, v_, sd_, rs_ = ([sb(f"c2_{n}{b}", [P, U]) for b in range(2)] for n in ("sum", "var", "std", "rstd"))
                S = [sb(f"c2_s{b}", [C, CE]) for b in range(2)]
                ixs, ixe = ([sb(f"c2_{n}{b}", [P, U], i32) for b in range(2)] for n in ("ixs", "ixe"))
                ix_r, ixe_r, got, gT, s_r, s_back, centred, squared, var_r, std_r, o_r, sent = (sems(f"c2_{n}") for n in (
                    "ix_ready", "ixe_ready", "gathered", "gT", "scanned", "sums_back", "centred", "squared", "var", "std", "rows", "sent"))
                dl, m1 = sem("c2_link"), sem("c2_zero")
                sort = Sort((sb, sem, sems), 2 * CHUNKS)
                with nc.Block() as block:
                    @block.gpsimd
                    def _(pool):
                        def gathers(m, k):
                            b, q = k % 2, m + k // 2
                            pool.wait_ge(ix_r[b], q + 1)
                            if exists(CHUNKS, m, k - 2):
                                pool.wait_ge(gT[b], q)
                            pool.sem_inc(pool_went_on, 1)
                            gather(pool, G[b], C, qs, ixs[b], got[b])

                        def scatters(m, k):
                            b, q = k % 2, m + k // 2
                            pool.wait_ge(o_r[b], q + 1)
                            pool.wait_ge(ixe_r[b], q + 1)
                            pool.sem_inc(pool_went_on, 1)
                            scatter(pool, h1, ixe[b], H[b], C, sent[b])
                            scatter(pool, out, ixe[b], O[b], C, sent[b])

                        two_ahead(pool, gathers, scatters)
                        for b in range(2):
                            pool.wait_ge(sent[b], 32 * U * PAIRS)

                    @block.sync
                    def _(sp):
                        sort.loads(sp)

                    @block.vector
                    def _(dve):
                        for b in range(2):
                            ins = dve.memset(S[b][:, :], 0.0)
                        ins.then_inc(m1, 1)
                        dve.wait_ge(m1, 1)
                        K = 7

                        def turn(m, k):
                            b, q = k % 2, m + k // 2
                            if not exists(CHUNKS, m, k):
                                if k > 0:
                                    sort.places(dve, m, k - 1, 1)
                                else:
                                    sort.one_hots(dve, m, k + 1, 0)
                                return
                            ch = Chain(dve, dl, (2 * m + k) * K)
                            cols = bass.ds((2 * m + k) * U, U)
                            dve.wait_ge(gT[b], q + 1)
                            if exists(CHUNKS, m, k - 1):
                                dve.wait_ge(s_r[1 - b], m + (k + 1) // 2)
                            dve.tensor_tensor_scan(S[b][:, :], mask_d[0:C, bass.ds((2 * m + k) * CE, CE)], bank[0][0:C, 0:CE],
                                                   S[1 - b][:, CE - 1:CE], ALU.mult, ALU.add).then_inc(s_r[b], 1)
                            sort.places(dve, m, k - 1, 1)
                            sort.one_hots(dve, m, k, 1)
                            dve.wait_ge(s_back[b], q + 1)
                            ch.link(dve.tensor_tensor(out=r3(Y[b]), in0=QSD[:, cols, :], in1=prows(bank[1]), op=ALU.add))
                            ch.link(dve.tensor_tensor(out=r3(Y[b]), in0=r3(Y[b]), in1=brd(dinv_d[:, cols], U), op=ALU.mult))
                            ch.link(dve.tensor_tensor(out=r3(Y[b]), in0=r3(Y[b]), in1=XD[:, cols, :], op=ALU.add))
                            ln_centre(dve, ch.link, r3(Y[b]), s_[b][:, :], r3(XC[b]), U).then_inc(centred[b], 1)
                            dve.wait_ge(centred[b], q + 1)
                            ch.put(dve.tensor_tensor(out=r3(Y[b]), in0=r3(Y[b]), in1=rows(c0B[:, :], U), op=ALU.add))
                            sort.places(dve, m, k, 0)
                            dve.wait_ge(squared[b], q + 1)
                            ln_var(dve, r3(SQ[b]), v_[b][:, :]).then_inc(var_r[b], 1)
                            sort.one_hots(dve, m, k + 1, 0)
                            dve.wait_ge(std_r[b], q + 1)
                            if exists(CHUNKS, m, k - 2):
                                dve.wait_ge(sent[b], q * (32 * U))
                            ch.link(ln_relu(dve, ch.link, sd_[b][:, :], rs_[b][:, :], r3(XC[b]), r3(H[b]), U))
                            dve.tensor_tensor(out=O[b][:, :], in0=H[b][:, :], in1=Y[b][:, :], op=ALU.add).then_inc(o_r[b], 1)
                            assert ch.n == K, ch.n

                        pipeline(dve, turn, CHUNKS, 1, 1)

                    @block.scalar
                    def _(act):
                        def indices(c, i):
                            act.activation(ixs[i][:, :], src_i[:, bass.ds(c * U, U)], ACT.Copy).then_inc(ix_r[i], 1)

                        def pair(j):
                            for b in range(2):
                                c = j * 2 + b
                                sort.copy_places(act, c, 0)
                                act.wait_ge(got[b], j * (16 * U) + 16 * U)
                                if not isinstance(j, int):
                                    indices(c + 2, b)
                                act.wait_ge(centred[b], j + 1)
                                ln_square(act, XC[b][:, :], SQ[b][:, :]).then_inc(squared[b], 1)
                                sort.copy_places(act, c, 1)
                                act.wait_ge(var_r[b], j + 1)
                                ln_std(act, v_[b][:, :], sd_[b][:, :]).then_inc(std_r[b], 1)
                                act.wait_ge(sent[b], j * (32 * U))
                                act.activation(ixe[b][:, :], dst_end[:, bass.ds(c * U, U)], ACT.Copy).then_inc(ixe_r[b], 1)

                        for i in range(2):
                            indices(i, i)
                        with act.Fori(0, PAIRS - 1) as j:
                            pair(j)
                        pair(PAIRS - 1)

                    @block.tensor
                    def _(pe):
                        sort.begin(pe)
                        with pe.Fori(0, PAIRS) as j:
                            for b in range(2):
                                pe.wait_ge(got[b], j * (16 * U) + 16 * U)
                                fwd(pe, bank[0], r3(G[b]), C, gT[b])
                                sort.select(pe, j * 2 + b, 0)
                                pe.wait_ge(s_r[b], j + 1)
                                pe.wait_ge(*pair_of_scans(b, j, centred))
                                back(pe, bank[1], S[b], C, s_back[b])
                                sort.select(pe, j * 2 + b, 1)

        with ExitStack() as st:
            sb, sem, sems = alloc(st)
            rec = [sb(f"rec{b}", [P, U * PAYW]) for b in range(2)]
            ixp = [sb(f"ixp{b}", [P, U], i32) for b in range(2)]
            attr_in, rec_ready, sent = sems("attr_in"), sems("rec_ready"), sems("rec_sent")
            with nc.Block() as block:
                @block.sync
                def _(sp):
                    with sp.Fori(0, PAIRS) as j:
                        for b in range(2):
                            sp.wait_ge(sent[b], j * (16 * U))
                            sp.dma_start(r3(rec[b])[:, :, HEAD + 1:PAYW], chunk_rows(attr, j * 2 + b)).then_inc(attr_in[b], 16)

                @block.vector
                def _(dve):
                    with dve.Fori(0, PAIRS) as j:
                        for b in range(2):
                            cols = bass.ds((j * 2 + b) * U, U)
                            dve.wait_ge(sent[b], j * (16 * U))
                            dve.tensor_copy(ixp[b][:, :], pos_f[:, cols])
                            dve.tensor_copy(r3(rec[b])[:, :, 0:HEAD + 1], head[:, cols, :]).then_inc(rec_ready[b], 1)

                @block.gpsimd
                def _(pool):
                    with pool.Fori(0, PAIRS) as j:
                        for b in range(2):
                            pool.wait_ge(rec_ready[b], j + 1)
                            pool.wait_ge(attr_in[b], j * 16 + 16)
                            pool.sem_inc(pool_went_on, 1)
                            for u in range(U):
                                pool.indirect_dma_start(out=pay, out_offset=bass.IndirectOffsetOnAxis(ap=ixp[b][:, u:u + 1], axis=0),
                                                        in_=rec[b][:, u * PAYW:(u + 1) * PAYW], in_offset=None)\
                                    .then_inc(sent[b], 16)
                    for b in range(2):
                        pool.wait_ge(sent[b], 16 * U * PAIRS)

        mask_s = ctx.enter_context(nc.sbuf_tensor("mask_s", [C, E], u8))
        with ExitStack() as st:
            sb, sem, sems = alloc(st)
            cur, prv, nxt, end_row = (sb(n, [T // 2, 2 * P]) for n in ("cur", "prv", "nxt", "end_row"))
            same = sb("same_s", [T // 2, 2 * P], u8)
            recs = sb("recs", [P, T, HEAD])
            tmp, tmp2 = sb("tmp_m", [P, T]), sb("tmp_m2", [P, T])
            actv, pre, incl2, base_f, ixl = (sb(n, [P, T], i32 if n == "ixl" else f32) for n in ("actv", "pre", "incl2", "base_f", "ixl"))
            act_r, pre_mm = sem("actv_ready"), sem("pre_mm")
            ixl_t = [sb(f"ixl_t{b}", [P, U], i32) for b in range(2)]
            lrec = [sb(f"lrec{b}", [P, U * 4]) for b in range(2)]
            lr_r, lr_sent = sems("lrec_ready"), sems("lrec_sent")
            recs_in, stored, dl = sem("recs_in"), sem("srcs_stored"), sem("mask_link")
            row_mm, row_r, rows_in, ends_r, ends_mm, same_moved = (sem(n) for n in ("row_mm", "row_r", "src_rows_in", "ends_r", "ends_mm", "same_src_moved"))
            halves = lambda a, i: a.rearrange("p (r i) -> p i r", i=2)[:, i, :]
            with nc.Block() as block:
                @block.sync
                def _(sp):
                    sp.dma_start(recs[:, :, :], pay[:, 0:HEAD].rearrange("(t p) a -> p t a", p=P)).then_inc(recs_in, 16)
                    sp.wait_ge(row_r, 1)
                    sp.dma_start(tile_rows(srcs_pad[1:E + 1]), cur[:, :]).then_inc(stored, 16)
                    sp.wait_ge(stored, 16)
                    sp.dma_start(prv[:, :], tile_rows(srcs_pad[0:E])).then_inc(rows_in, 16)
                    sp.dma_start(nxt[:, :], tile_rows(srcs_pad[2:E + 2])).then_inc(rows_in, 16)
                    sp.wait_ge(ends_r, 1)
                    sp.dma_start(tile_rows(same_src), same[:, :]).then_inc(same_moved, 16)
                    sp.wait_ge(same_moved, 16)
                    sp.dma_start(mask_s[:, :], same_src.partition_broadcast(C)).then_inc(same_moved, 16)
                    sp.wait_ge(same_moved, 32)

                @block.vector
                def _(dve):
                    dve.wait_ge(recs_in, 16)
                    ch = Chain(dve, dl)
                    dve.tensor_copy(srcS_i[:, :], recs[:, :, 0])
                    dve.tensor_copy(dstS_i[:, :], recs[:, :, 1])
                    dve.tensor_copy(gi_i[:, :], recs[:, :, 2])
                    dve.tensor_copy(w_s[:, :], recs[:, :, 4])
                    dve.tensor_copy(own[:, :], recs[:, :, 3])
                    dve.wait_ge(row_mm, 1)
                    dve.tensor_copy(cur[:, :], bank[2][0:T // 2, 0:2 * P]).then_inc(row_r, 1)
                    dve.wait_ge(rows_in, 32)
                    dve.tensor_tensor(out=end_row[:, :], in0=cur[:, :], in1=nxt[:, :], op=ALU.not_equal)
                    dve.tensor_tensor(out=same[:, :], in0=cur[:, :], in1=prv[:, :], op=ALU.is_equal).then_inc(ends_r, 1)
                    dve.wait_ge(ends_mm, 1)
                    for i in range(2):
                        ins = dve.tensor_copy(halves(tmp[:, :], i), bank[3 + i][0:P, 0:T // 2])
                    ch.link(ins)
                    ch.link(dve.scalar_tensor_tensor(out=tmp2[:, :], in0=recs[:, :, 0], scalar=-float(N), in1=tmp[:, :],
                                                     op0=ALU.add, op1=ALU.mult))
                    ch.link(dve.tensor_scalar(srcS_end[:, :], tmp2[:, :], float(N), None, ALU.add))
                    ch.link(dve.tensor_scalar(actv[:, :], recs[:, :, 2], float(E), None, ALU.is_lt))
                    dve.memset(incl2[:, :], 0.0).then_inc(act_r, 1)
                    dve.wait_ge(pre_mm, 1)
                    ch.link(dve.tensor_copy(pre[:, :], bank[0][0:P, 0:T]))
                    ch.link(dve.tensor_copy(base_f[:, :], bank[1][0:P, 0:T]))
                    ch.link(dve.tensor_tensor_scan(incl2[:, :], ones_t[:, :], base_f[:, :], 0.0, ALU.mult, ALU.add))
                    list_count(dve, ch.link, incl2[0:1, T - 1:T], tmp[0:1, 0:T // 2], tmp[0:1, T // 2:T // 2 + 1], counts[2], LIST_U[2])
                    ch.link(dve.tensor_tensor(out=base_f[:, :], in0=incl2[:, :], in1=base_f[:, :], op=ALU.subtract))
                    ch.link(dve.tensor_tensor(out=pre[:, :], in0=pre[:, :], in1=base_f[:, :], op=ALU.add))
                    ch.link(dve.tensor_scalar(tmp[:, :], pre[:, :], 1.0, nowhere[:, 0:1], ALU.add, ALU.subtract))
                    ch.link(dve.tensor_tensor(out=tmp[:, :], in0=tmp[:, :], in1=actv[:, :], op=ALU.mult))
                    ch.link(dve.tensor_scalar(ixl[:, :], tmp[:, :], nowhere[:, 0:1], None, ALU.add))
                    with dve.Fori(0, PAIRS) as j:
                        for b in range(2):
                            cols = bass.ds((j * 2 + b) * U, U)
                            dve.wait_ge(lr_sent[b], j * (16 * U))
                            dve.tensor_copy(ixl_t[b][:, :], ixl[:, cols])
                            dve.tensor_copy(r3(lrec[b])[:, :, 0], recs[:, cols, 3])
                            dve.tensor_copy(r3(lrec[b])[:, :, 1], recs[:, cols, 2])
                            dve.tensor_copy(r3(lrec[b])[:, :, 2], recs[:, cols, 4])
                            dve.tensor_copy(r3(lrec[b])[:, :, 3], recs[:, cols, 4]).then_inc(lr_r[b], 1)

                @block.tensor
                def _(pe):
                    pe.wait_ge(recs_in, 16)
                    for i in range(2):
                        ins = pe.transpose(bank[2][0:T // 2, i * P:(i + 1) * P], halves(recs[:, :, 0], i), ident[0:P, 0:P])
                    ins.then_inc(row_mm, 1)
                    pe.wait_ge(ends_r, 1)
                    for i in range(2):
                        ins = pe.transpose(bank[3 + i][0:P, 0:T // 2], end_row[:, i * P:(i + 1) * P], ident[0:T // 2, 0:T // 2])
                    ins.then_inc(ends_mm, 1)
                    pe.wait_ge(act_r, 1)
                    pe.matmul(bank[0][0:P, 0:T], tri_k[:, :], actv[:, :], start=True, stop=True)
                    pe.matmul(bank[1][0:P, 0:T], ones_pp[:, :], actv[:, :], start=True, stop=True).then_inc(pre_mm, 1)

                @block.gpsimd
                def _(pool):
                    with pool.Fori(0, PAIRS) as j:
                        for b in range(2):
                            pool.wait_ge(lr_r[b], j + 1)
                            pool.sem_inc(pool_went_on, 1)
                            scatter(pool, lists[2], ixl_t[b], lrec[b], 4, lr_sent[b], E + 1)
                    for b in range(2):
                        pool.wait_ge(lr_sent[b], 16 * U * PAIRS)


        with ExitStack() as st:
            sb, sem, sems = alloc(st)
            DEL = sb("series", [P, T, C])
            wk = sb("wk", [P, T])
            with ExitStack() as s2:
                sb, sem, sems = alloc(s2)
                G, M = ([sb(f"t1_{n}{b}", [P, U * C]) for b in range(2)] for n in ("g", "m"))
                TR = [sb(f"t1_tr{b}", [P, U * TW]) for b in range(2)]
                S = [sb(f"t1_s{b}", [C, CE]) for b in range(2)]
                ixs = [sb(f"t1_ix{b}", [P, U], i32) for b in range(2)]
                ix_r, got, m_r, mT, s_r, s_back, row_r, stored, d_r = (sems(f"t1_{n}") for n in (
                    "ix_ready", "gathered", "messages", "mT", "scanned", "sums_back", "rows", "stored", "kept"))
                m1 = sem("t1_zero")
                with nc.Block() as block:
                    @block.gpsimd
                    def _(pool):
                        with pool.Fori(0, PAIRS) as j:
                            for b in range(2):
                                pool.wait_ge(ix_r[b], j + 1)
                                pool.wait_ge(m_r[b], j)
                                pool.sem_inc(pool_went_on, 1)
                                gather(pool, G[b], C, h1, ixs[b], got[b])

                    @block.vector
                    def _(dve):
                        for b in range(2):
                            dve.memset(TR[b][:, :], 1.0)
                            ins = dve.memset(S[b][:, :], 0.0)
                        ins.then_inc(m1, 1)
                        dve.wait_ge(m1, 1)
                        dve.tensor_scalar(wk[:, :], w_s[:, :], rat[:, 1:2], None, ALU.mult).then_inc(m1, 1)
                        dve.wait_ge(m1, 2)

                        def turn(m, k):
                            if exists(CHUNKS, m, k + 1):
                                b, q = (k + 1) % 2, m + (k + 1) // 2
                                dve.wait_ge(got[b], q * (16 * U) + 16 * U)
                                if exists(CHUNKS, m, k - 1):
                                    dve.wait_ge(mT[b], q)
                                dve.tensor_tensor(out=r3(M[b]), in0=r3(G[b]), in1=brd(wk[:, bass.ds((2 * m + k + 1) * U, U)], U), op=ALU.mult)\
                                   .then_inc(m_r[b], 1)
                            if exists(CHUNKS, m, k):
                                b, q = k % 2, m + k // 2
                                dve.wait_ge(mT[b], q + 1)
                                if exists(CHUNKS, m, k - 1):
                                    dve.wait_ge(s_r[1 - b], m + (k + 1) // 2)
                                if exists(CHUNKS, m, k - 2):
                                    dve.wait_ge(s_back[b], q)
                                dve.tensor_tensor_scan(S[b][:, :], mask_s[0:C, bass.ds((2 * m + k) * CE, CE)], bank[4 * b][0:C, 0:CE],
                                                       S[1 - b][:, CE - 1:CE], ALU.mult, ALU.add).then_inc(s_r[b], 1)

                        pipeline(dve, turn, CHUNKS, 1, 0)

                    @block.scalar
                    def _(act):
                        def indices(c, i):
                            act.activation(ixs[i][:, :], dstS_i[:, bass.ds(c * U, U)], ACT.Copy).then_inc(ix_r[i], 1)

                        def pair(j):
                            for b in range(2):
                                c = j * 2 + b
                                act.wait_ge(got[b], j * (16 * U) + 16 * U)
                                if not isinstance(j, int):
                                    indices(c + 2, b)
                                act.wait_ge(s_back[b], j + 1)
                                act.wait_ge(stored[b], j * 16)
                                act.activation(r3(TR[b])[:, :, 0:C], prows(bank[4 * b + 1]), ACT.Copy).then_inc(row_r[b], 1)
                                act.activation(DEL[:, bass.ds(c * U, U), :], prows(bank[4 * b + 1]), ACT.Copy).then_inc(d_r[b], 1)

                        for i in range(2):
                            indices(i, i)
                        with act.Fori(0, PAIRS - 1) as j:
                            pair(j)
                        pair(PAIRS - 1)

                    @block.tensor
                    def _(pe):
                        def turn(m, k):
                            if exists(CHUNKS, m, k + 1):
                                b, q = (k + 1) % 2, m + (k + 1) // 2
                                pe.wait_ge(m_r[b], q + 1)
                                if exists(CHUNKS, m, k - 1):
                                    pe.wait_ge(s_r[b], q)
                                fwd(pe, bank[4 * b], r3(M[b]), C, mT[b])
                            if exists(CHUNKS, m, k):
                                b, q = k % 2, m + k // 2
                                pe.wait_ge(s_r[b], q + 1)
                                if exists(CHUNKS, m, k - 2):
                                    pe.wait_ge(d_r[b], q)
                                back(pe, bank[4 * b + 1], S[b], C, s_back[b])

                        pipeline(pe, turn, CHUNKS, 1, 0)

                    @block.sync
                    def _(sp):
                        with sp.Fori(0, PAIRS) as j:
                            for b in range(2):
                                sp.wait_ge(row_r[b], j + 1)
                                sp.dma_start(chunk_rows(terms[1], j * 2 + b), r3(TR[b])).then_inc(stored[b], 16)
                        for b in range(2):
                            sp.wait_ge(stored[b], 16 * PAIRS)

            for k in range(2, LISTS + 1):
                UL, CL = LIST_U[k], LIST_U[k] * P
                with ExitStack() as s2:
                    sb, sem, sems = alloc(s2)
                    lin, lout = lists[max(k - 1, 2)], lists[k] if k > 2 else None
                    tin, tout = terms[1 if k == 2 else 2 * (k % 2)], terms[2 * ((k + 1) % 2)]
                    nm = f"k{k}_"
                    tl = lambda n, shape, dt=f32: [sb(f"{nm}{n}{b}", shape, dt) for b in range(2)]
                    R, prv_own, nxt_own = tl("rec", [P, UL, 4]), tl("prev", [P, UL, 1]), tl("next", [P, UL, 1])
                    G, M, TR = tl("g", [P, UL * TW]), tl("m", [P, UL * TW]), tl("tr", [P, UL * TW])
                    gix, tix, lix = tl("gix", [P, UL], i32), tl("tix", [P, UL], i32), tl("lix", [P, UL], i32)
                    cont, endf, wr, actv, wa, tf, lf = (tl(n, [P, UL]) for n in ("cont", "endf", "wr", "actv", "wa", "tf", "lf"))
                    MKT, S = tl("maskT", [TW, CL]), tl("s", [TW, CL])
                    base = sb(nm + "base", [P, 1])
                    fits, pairs_f = sb(nm + "fits", [1, T // 2]), sb(nm + "pairs_f", [1, 1])
                    rows_in, ix_r, got, m_r, mT, mk_r, s_r, l_r, s_back, t_r, sent = (sems(nm + n) for n in (
                        "rows_in", "indices", "gathered", "messages", "mT", "maskT", "scanned", "list_rows", "back", "rows", "sent"))
                    dl, z_r = sem(nm + "link"), sem(nm + "zero")
                    SENT = 16 * UL * (3 if lout is not None else 2)
                    g3 = lambda a: a[:, :].rearrange("p (u f) -> p u f", u=UL)
                    pairs_of = lambda eng: eng.value_load(counts[max(k - 1, 2)][0:1, 0:1], min_val=1, max_val=T // (2 * UL))
                    with nc.Block() as block:
                        @block.sync
                        def _(sp):
                            with sp.Fori(0, pairs_of(sp)) as j:
                                for b in range(2):
                                    sp.wait_ge(sent[b], j * SENT)
                                    for buf, shift, w_ in ((R, 1, 4), (prv_own, 0, 1), (nxt_own, 2, 1)):
                                        sp.dma_start(buf[b][:, :, :], lin[bass.ds((j * 2 + b) * CL + shift, CL), 0:w_]
                                                     .rearrange("(u p) f -> p u f", p=P)).then_inc(rows_in[b], 16)

                        @block.gpsimd
                        def _(pool):
                            with pool.Fori(0, pairs_of(pool)) as j:
                                for b in range(2):
                                    pool.wait_ge(ix_r[b], j + 1)
                                    pool.sem_inc(pool_went_on, 1)
                                    for u in range(UL):
                                        pool.indirect_dma_start(out=G[b][:, u * TW:(u + 1) * TW], out_offset=None, in_=tin,
                                                                in_offset=bass.IndirectOffsetOnAxis(ap=gix[b][:, u:u + 1], axis=0))\
                                            .then_inc(got[b], 16)
                                for b in range(2):
                                    if lout is not None:
                                        pool.wait_ge(l_r[b], j + 1)
                                        pool.sem_inc(pool_went_on, 1)
                                        for u in range(UL):
                                            pool.indirect_dma_start(out=lout, out_offset=bass.IndirectOffsetOnAxis(ap=lix[b][:, u:u + 1], axis=0),
                                                                    in_=R[b][:, u, :], in_offset=None,
                                                                    bounds_check=E, oob_is_err=False).then_inc(sent[b], 16)
                                    pool.wait_ge(t_r[b], j + 1)
                                    pool.sem_inc(pool_went_on, 1)
                                    for u in range(UL):
                                        at = bass.IndirectOffsetOnAxis(ap=tix[b][:, u:u + 1], axis=0)
                                        pool.indirect_dma_start(out=tout, out_offset=at, in_=TR[b][:, u * TW:(u + 1) * TW],
                                                                in_offset=None).then_inc(sent[b], 16)
                                        pool.indirect_dma_start(out=series, out_offset=at, in_=TR[b][:, u * TW:u * TW + C], in_offset=None,
                                                                compute_op=ALU.add).then_inc(sent[b], 16)
                            pool.drain()

                        @block.vector
                        def _(dve):
                            dve.memset(base[:, :], 0.0)
                            for b in range(2):
                                ins = dve.memset(S[b][:, :], 0.0)
                            ins.then_inc(z_r, 1)
                            dve.wait_ge(z_r, 1)
                            K = 2 * (10 if lout is not None else 6)
                            with dve.Fori(0, pairs_of(dve)) as j:
                                ch = Chain(dve, dl, j * K)
                                for b in range(2):
                                    dve.wait_ge(rows_in[b], j * 48 + 48)
                                    own_, dst_, w_ = R[b][:, :, 0], R[b][:, :, 1], R[b][:, :, 2]
                                    dve.tensor_copy(gix[b][:, :], dst_)
                                    dve.tensor_scalar(wr[b][:, :], w_, ratios_py[k], None, ALU.mult)
                                    dve.tensor_tensor(out=cont[b][:, :], in0=own_, in1=prv_own[b][:, :, 0], op=ALU.is_equal)
                                    ch.link(dve.tensor_tensor(out=endf[b][:, :], in0=own_, in1=nxt_own[b][:, :, 0], op=ALU.not_equal))
                                    ch.link(dve.scalar_tensor_tensor(out=endf[b][:, :], in0=own_, scalar=0.0, in1=endf[b][:, :], op0=ALU.is_ge, op1=ALU.mult))
                                    ch.link(dve.tensor_tensor(out=tf[b][:, :], in0=own_, in1=nowhere[:, b * UL:(b + 1) * UL], op=ALU.subtract))
                                    ch.link(dve.tensor_tensor(out=tf[b][:, :], in0=tf[b][:, :], in1=endf[b][:, :], op=ALU.mult))
                                    dve.tensor_tensor(out=tix[b][:, :], in0=tf[b][:, :], in1=nowhere[:, b * UL:(b + 1) * UL], op=ALU.add).then_inc(ix_r[b], 1)
                                for b in range(2):
                                    dve.wait_ge(got[b], j * (16 * UL) + 16 * UL)
                                    ch.link(dve.tensor_scalar(actv[b][:, :], g3(G[b])[:, :, C], float(k - 1), None, ALU.is_equal))
                                    ch.link(dve.tensor_tensor(out=wa[b][:, :], in0=wr[b][:, :], in1=actv[b][:, :], op=ALU.mult))
                                    dve.tensor_copy(g3(M[b])[:, :, C], actv[b][:, :])
                                    dve.tensor_tensor(out=g3(M[b])[:, :, 0:C], in0=g3(G[b])[:, :, 0:C],
                                                      in1=wa[b][:, :].unsqueeze(2).to_broadcast([P, UL, C]), op=ALU.mult).then_inc(m_r[b], 1)
                                for b in range(2):
                                    dve.wait_ge(mk_r[b], j + 1)
                                    dve.wait_ge(*pair_of_scans(b, j, s_r))
                                    dve.tensor_tensor_scan(S[b][:, :], MKT[b][:, :], bank[4 * b][0:TW, 0:CL], S[1 - b][:, CL - 1:CL],
                                                           ALU.mult, ALU.add).then_inc(s_r[b], 1)
                                    if lout is not None:
                                        ch.put(dve.tensor_scalar(lf[b][:, :], bank[4 * b + 2][0:P, 0:UL], base[:, 0:1], 1.0, ALU.add, ALU.add))
                                        ch.link(dve.tensor_tensor(out=base[:, :], in0=base[:, :], in1=bank[4 * b + 2][0:P, UL:UL + 1], op=ALU.add))
                                        ch.link(dve.tensor_tensor(out=lf[b][:, :], in0=lf[b][:, :], in1=nowhere[:, b * UL:(b + 1) * UL], op=ALU.subtract))
                                        ch.link(dve.tensor_tensor(out=lf[b][:, :], in0=lf[b][:, :], in1=actv[b][:, :], op=ALU.mult))
                                        dve.tensor_tensor(out=lix[b][:, :], in0=lf[b][:, :], in1=nowhere[:, b * UL:(b + 1) * UL], op=ALU.add).then_inc(l_r[b], 1)
                                for b in range(2):
                                    dve.wait_ge(s_back[b], j + 1)
                                    back_rows = bank[4 * b + 3][0:P, 0:UL * TW].rearrange("p (u f) -> p u f", u=UL)
                                    dve.tensor_scalar(g3(TR[b])[:, :, C], back_rows[:, :, C], 0.0, float(k), ALU.is_gt, ALU.mult)
                                    dve.tensor_copy(g3(TR[b])[:, :, 0:C], back_rows[:, :, 0:C]).then_inc(t_r[b], 1)
                                assert ch.n == K, ch.n
                            if lout is not None:
                                dve.drain().then_inc(z_r, 1)
                                dve.wait_ge(z_r, 2)
                                ch = Chain(dve, z_r, 2)
                                list_count(dve, ch.link, base[0:1, 0:1], fits[:, :], pairs_f[:, :], counts[k], LIST_U[min(k + 1, LISTS)])

                        @block.scalar
                        def _(act):
                            with act.Fori(0, pairs_of(act)) as j:
                                for b in range(2):
                                    act.wait_ge(mT[b], j + 1)
                                    act.activation(MKT[b][:, :], bank[4 * b + 1][0:TW, 0:CL], ACT.Copy).then_inc(mk_r[b], 1)

                        @block.tensor
                        def _(pe):
                            with pe.Fori(0, pairs_of(pe)) as j:
                                for b in range(2):
                                    pe.wait_ge(m_r[b], j + 1)
                                    pe.sem_inc(pe_went_on, 1)
                                    for u in range(UL):
                                        cols = slice(u * P, (u + 1) * P)
                                        pe.transpose(bank[4 * b][0:TW, cols], g3(M[b])[:, u, :], ident[0:P, 0:P])
                                        pe.transpose(bank[4 * b + 1][0:TW, cols], cont[b][:, u:u + 1].to_broadcast([P, TW]), ident[0:P, 0:P])
                                    before, all_ = bank[4 * b + 2][0:P, 0:UL], bank[4 * b + 2][0:P, UL:UL + 1]
                                    pe.matmul(before, tri_k[:, :], actv[b][:, :], start=True, stop=False, skip_group_check=True)
                                    for u in range(UL - 1):
                                        pe.matmul(before[:, u + 1:UL], ones_pp[:, :], actv[b][:, u:u + 1].to_broadcast([P, UL - 1 - u]),
                                                  start=False, stop=False, skip_group_check=True)
                                    for u in range(UL):
                                        ins = pe.matmul(all_, ones_pp[:, :], actv[b][:, u:u + 1], start=u == 0, stop=u == UL - 1, skip_group_check=True)
                                    ins.then_inc(mT[b], 1)
                                for b in range(2):
                                    pe.wait_ge(s_r[b], j + 1)
                                    pe.sem_inc(pe_went_on, 1)
                                    for u in range(UL):
                                        ins = pe.transpose(bank[4 * b + 3][0:P, u * TW:(u + 1) * TW], S[b][:, u * P:(u + 1) * P], ident[0:TW, 0:TW])
                                    ins.then_inc(s_back[b], 1)

            left = nc.values_load(counts[LISTS][0:1, 1:2], min_val=0, max_val=E)
            with nc.If(left > P):
                for first, STEPS in ((2, TERMS // 2), (2 + TERMS // 2, TERMS // 2 - 1)):
                    with ExitStack() as s2:
                        sb, sem, sems = alloc(s2)
                        G, TR = ([sb(f"tk{first}_{n}{b}", [P, U * TW]) for b in range(2)] for n in ("g", "tr"))
                        M = [sb(f"tk{first}_m{b}", [P, U * C]) for b in range(2)]
                        S = [sb(f"tk{first}_s{b}", [C, CE]) for b in range(2)]
                        ixs = [sb(f"tk{first}_ix{b}", [P, U], i32) for b in range(2)]
                        ix_r, got, m_r, mT, s_r, s_back, row_r, stored, d_r = (sems(f"tk{first}_{n}") for n in (
                            "ix_ready", "gathered", "messages", "mT", "scanned", "sums_back", "rows", "stored", "added"))
                        wk_r, m1 = sem(f"tk{first}_weights"), sem(f"tk{first}_zero")
                        with nc.Block() as block:
                            @block.gpsimd
                            def _(pool):
                                def step(i, par):
                                    for b in range(2):
                                        pool.wait_ge(stored[b], i * (16 * PAIRS))
                                    pool.sem_inc(pool_went_on, 1)
                                    with pool.Fori(0, PAIRS) as j:
                                        for b in range(2):
                                            pool.wait_ge(ix_r[b], i * PAIRS + j + 1)
                                            pool.wait_ge(m_r[b], i * PAIRS + j)
                                            pool.sem_inc(pool_went_on, 1)
                                            gather(pool, G[b], TW, terms[1 - par], ixs[b], got[b])
                                with pool.Fori(0, STEPS // 2) as h:
                                    step(h * 2, 0)
                                    step(h * 2 + 1, 1)
                                if STEPS % 2:
                                    step(STEPS - 1, 0)

                            @block.vector
                            def _(dve):
                                for b in range(2):
                                    dve.memset(TR[b][:, :], 1.0)
                                    ins = dve.memset(S[b][:, :], 0.0)
                                ins.then_inc(m1, 1)
                                dve.wait_ge(m1, 1)
                                def step(i, par):
                                    for b in range(2):
                                        dve.wait_ge(m_r[b], i * PAIRS)
                                    dve.tensor_scalar(wk[:, :], w_s[:, :], rat[:, bass.ds(i + first, 1)], None, ALU.mult).then_inc(wk_r, 1)
                                    with dve.Fori(0, PAIRS) as j:
                                        n = i * PAIRS + j
                                        dve.wait_ge(wk_r, i + 1)
                                        for b in range(2):
                                            cols = bass.ds((j * 2 + b) * U, U)
                                            dve.wait_ge(got[b], n * (16 * U) + 16 * U)
                                            dve.wait_ge(mT[b], n)
                                            dve.tensor_tensor(out=r3(M[b]), in0=r3(G[b])[:, :, 0:C], in1=brd(wk[:, cols], U), op=ALU.mult).then_inc(m_r[b], 1)
                                            dve.wait_ge(mT[b], n + 1)
                                            dve.wait_ge(*pair_of_scans(b, n, s_r))
                                            dve.tensor_tensor_scan(S[b][:, :], mask_s[0:C, bass.ds((j * 2 + b) * CE, CE)], bank[4 * b][0:C, 0:CE],
                                                                   S[1 - b][:, CE - 1:CE], ALU.mult, ALU.add).then_inc(s_r[b], 1)
                                            dve.wait_ge(row_r[b], n + 1)
                                            dve.tensor_tensor(out=DEL[:, cols, :], in0=DEL[:, cols, :], in1=r3(TR[b])[:, :, 0:C], op=ALU.add).then_inc(d_r[b], 1)
                                with dve.Fori(0, STEPS // 2) as h:
                                    step(h * 2, 0)
                                    step(h * 2 + 1, 1)
                                if STEPS % 2:
                                    step(STEPS - 1, 0)

                            @block.scalar
                            def _(act):
                                def step(i, par):
                                    with act.Fori(0, PAIRS) as j:
                                        n = i * PAIRS + j
                                        for b in range(2):
                                            act.wait_ge(got[b], n * (16 * U))
                                            act.activation(ixs[b][:, :], gi_i[:, bass.ds((j * 2 + b) * U, U)], ACT.Copy).then_inc(ix_r[b], 1)
                                        for b in range(2):
                                            act.wait_ge(s_back[b], n + 1)
                                            act.wait_ge(stored[b], n * 16)
                                            act.wait_ge(d_r[b], n)
                                            act.activation(r3(TR[b])[:, :, 0:C], prows(bank[4 * b + 1]), ACT.Copy).then_inc(row_r[b], 1)
                                with act.Fori(0, STEPS // 2) as h:
                                    step(h * 2, 0)
                                    step(h * 2 + 1, 1)
                                if STEPS % 2:
                                    step(STEPS - 1, 0)

                            @block.tensor
                            def _(pe):
                                def step(i, par):
                                    with pe.Fori(0, PAIRS) as j:
                                        n = i * PAIRS + j
                                        for b in range(2):
                                            pe.wait_ge(m_r[b], n + 1)
                                            fwd(pe, bank[4 * b], r3(M[b]), C, mT[b])
                                            pe.wait_ge(s_r[b], n + 1)
                                            pe.wait_ge(row_r[b], n)
                                            back(pe, bank[4 * b + 1], S[b], C, s_back[b])
                                with pe.Fori(0, STEPS // 2) as h:
                                    step(h * 2, 0)
                                    step(h * 2 + 1, 1)
                                if STEPS % 2:
                                    step(STEPS - 1, 0)

                            @block.sync
                            def _(sp):
                                def step(i, par):
                                    with sp.Fori(0, PAIRS) as j:
                                        n = i * PAIRS + j
                                        for b in range(2):
                                            sp.wait_ge(row_r[b], n + 1)
                                            sp.dma_start(chunk_rows(terms[par], j * 2 + b), r3(TR[b])).then_inc(stored[b], 16)
                                with sp.Fori(0, STEPS // 2) as h:
                                    step(h * 2, 0)
                                    step(h * 2 + 1, 1)
                                if STEPS % 2:
                                    step(STEPS - 1, 0)
                                for b in range(2):
                                    sp.wait_ge(stored[b], 16 * PAIRS * STEPS)
                with ExitStack() as s2:
                    sb, sem, sems = alloc(s2)
                    zeros = sb("no_series", [P, C])
                    empty, emptied = sem("series_zeros"), sem("series_emptied")
                    with nc.Block() as block:
                        @block.vector
                        def _(dve):
                            dve.memset(zeros[:, :], 0.0).then_inc(empty, 1)

                        @block.sync
                        def _(sp):
                            sp.wait_ge(empty, 1)
                            sp.dma_start(series.rearrange("(p c) f -> p c f", p=P), zeros[:, :].unsqueeze(1).to_broadcast([P, NR // P, C])).then_inc(emptied, 16)
                            sp.wait_ge(emptied, 16)
            with nc.Else():
                with ExitStack() as s2:
                    sb, sem, sems = alloc(s2)
                    last = lists[LISTS]
                    R, nxt_own = sb("tl_rec", [P, 4]), sb("tl_next", [P, 1])
                    gix, tix = sb("tl_gix", [P, 1], i32), sb("tl_tix", [P, 1], i32)
                    G, G0, X, ACC, DL = sb("tl_g", [P, TW]), sb("tl_g0", [P, C]), sb("tl_x", [P, C]), sb("tl_acc", [P, C]), sb("tl_dl", [P, C])
                    MT, SEG = sb("tl_mT", [P, P]), sb("tl_segT", [P, P])
                    endf, tf, actv = sb("tl_end", [P, 1]), sb("tl_tf", [P, 1]), sb("tl_actv", [P, 1])
                    rows_in, ix_r, got, keys_T, x_r, g_mm, sums_mm, dl_r, added, dl = (sem(f"tl_{n}") for n in (
                        "rows_in", "indices", "gathered", "keys_T", "x", "g_mm", "sums_mm", "rows", "added", "link"))
                    with nc.Block() as block:
                        @block.sync
                        def _(sp):
                            sp.dma_start(R[:, :], last[1:1 + P, :]).then_inc(rows_in, 16)
                            sp.dma_start(nxt_own[:, :], last[2:2 + P, 0:1]).then_inc(rows_in, 16)

                        @block.gpsimd
                        def _(pool):
                            pool.wait_ge(ix_r, 1)
                            pool.indirect_dma_start(out=G[:, :], out_offset=None, in_=terms[2 * ((LISTS + 1) % 2)],
                                                    in_offset=bass.IndirectOffsetOnAxis(ap=gix[:, 0:1], axis=0)).then_inc(got, 16)
                            pool.wait_ge(dl_r, 1)
                            pool.indirect_dma_start(out=series, out_offset=bass.IndirectOffsetOnAxis(ap=tix[:, 0:1], axis=0),
                                                    in_=DL[:, :], in_offset=None, compute_op=ALU.add).then_inc(added, 16)
                            pool.wait_ge(added, 16)

                        @block.tensor
                        def _(pe):
                            pe.wait_ge(rows_in, 32)
                            pe.transpose(bank[0][0:P, 0:P], R[:, 1:2].to_broadcast([P, P]), ident[0:P, 0:P])
                            pe.transpose(bank[1][0:P, 0:P], R[:, 0:1].to_broadcast([P, P]), ident[0:P, 0:P]).then_inc(keys_T, 1)
                            with pe.Fori(0, TERMS - LISTS - 1) as i:
                                pe.wait_ge(x_r, i + 1)
                                pe.matmul(bank[2][0:P, 0:C], MT[:, :], X[:, :], start=True, stop=True).then_inc(g_mm, 1)
                            pe.wait_ge(x_r, TERMS - LISTS + 1)
                            pe.matmul(bank[3][0:P, 0:C], SEG[:, :], ACC[:, :], start=True, stop=True).then_inc(sums_mm, 1)

                        @block.vector
                        def _(dve):
                            ch = Chain(dve, dl)
                            link = ch.link
                            dve.wait_ge(rows_in, 32)
                            link(dve.tensor_copy(gix[:, :], R[:, 1:2]))
                            link(dve.tensor_tensor(out=endf[:, :], in0=R[:, 0:1], in1=nxt_own[:, :], op=ALU.not_equal))
                            link(dve.scalar_tensor_tensor(out=endf[:, :], in0=R[:, 0:1], scalar=0.0, in1=endf[:, :], op0=ALU.is_ge, op1=ALU.mult))
                            link(dve.tensor_tensor(out=tf[:, :], in0=R[:, 0:1], in1=nowhere[:, 0:1], op=ALU.subtract))
                            link(dve.tensor_tensor(out=tf[:, :], in0=tf[:, :], in1=endf[:, :], op=ALU.mult))
                            dve.tensor_tensor(out=tix[:, :], in0=tf[:, :], in1=nowhere[:, 0:1], op=ALU.add).then_inc(ix_r, 1)
                            dve.wait_ge(keys_T, 1)
                            dve.tensor_scalar(MT[:, :], bank[0][0:P, 0:P], R[:, 0:1], R[:, 2:3], ALU.is_equal, ALU.mult)
                            dve.tensor_scalar(SEG[:, :], bank[1][0:P, 0:P], R[:, 0:1], R[:, 2:3], ALU.is_equal, ALU.mult)
                            dve.wait_ge(got, 16)
                            link(dve.tensor_scalar(actv[:, :], G[:, C:TW], float(LISTS), None, ALU.is_equal))
                            link(dve.tensor_scalar(G0[:, :], G[:, 0:C], actv[:, 0:1], None, ALU.mult))
                            dve.tensor_scalar(X[:, :], G0[:, :], ratios_py[LISTS + 1], None, ALU.mult).then_inc(x_r, 1)
                            dve.wait_ge(x_r, 1)
                            link(dve.tensor_copy(ACC[:, :], X[:, :]))
                            before = ch.n
                            with dve.Fori(0, TERMS - LISTS - 1) as i:
                                ch = Chain(dve, dl, i * 1 + before)
                                dve.wait_ge(g_mm, i + 1)
                                dve.tensor_scalar(X[:, :], bank[2][0:P, 0:C], rat[:, bass.ds(i + LISTS + 2, 1)], None, ALU.mult).then_inc(x_r, 1)
                                dve.wait_ge(x_r, i + 2)
                                ch.link(dve.tensor_tensor(out=ACC[:, :], in0=ACC[:, :], in1=X[:, :], op=ALU.add))
                            dve.sem_inc(x_r, 1)
                            dve.wait_ge(sums_mm, 1)
                            dve.tensor_copy(DL[:, :], bank[3][0:P, 0:C]).then_inc(dl_r, 1)

            with ExitStack() as s2:
                sb, sem, sems = alloc(s2)
                G, H, O, D = ([sb(f"l2_{n}{b}", [P, U * C]) for b in range(2)] for n in ("g", "h", "o", "series"))
                ixs, ixe = ([sb(f"l2_{n}{b}", [P, U], i32) for b in range(2)] for n in ("ixs", "ixe"))
                AR = [sb(f"l2_attr{b}", [P, U * (1 + 2 * ATTR)]) for b in range(2)]
                IN = [sb(f"l2_in{b}", [3 * ATTR, CE]) for b in range(2)]
                AS, AM, MEAN = ([t[i * ATTR:(i + 1) * ATTR, :] for t in IN] for i in range(3))
                big_all = [sb(f"l2_big{b}", [2 * ATTR, CE]) for b in range(2)]
                BM = [t[ATTR:2 * ATTR, :] for t in big_all]
                Z = [sb(f"l2_z{b}", [HID, CE]) for b in range(2)]
                swap = sb("l2_swap", [P, C])
                ix_r, ixe_r, got, a_in, a_T, sum_r, sc_r, mean_r, z_mm, z_r, l2_mm, o_r, sent = (sems(f"l2_{n}") for n in (
                    "ix_ready", "ixe_ready", "gathered", "attr_in", "attr_T", "sums", "scanned", "mean", "z_mm", "z", "rows_mm", "rows", "sent"))
                d_in, d_used = sems("l2_series_in"), sems("l2_series_used")
                d_sum = sems("l2_series_sum")
                dl, rl, m1 = sem("l2_sums_link"), sem("l2_rows_link"), sem("l2_zero")
                with nc.Block() as block:
                    @block.gpsimd
                    def _(pool):
                        def gathers(m, k):
                            b, q = k % 2, m + k // 2
                            pool.wait_ge(ix_r[b], q + 1)
                            if exists(CHUNKS, m, k - 2):
                                pool.wait_ge(o_r[b], q)
                            pool.sem_inc(pool_went_on, 1)
                            gather(pool, G[b], C, out, ixs[b], got[b])

                        def scatters(m, k):
                            b, q = k % 2, m + k // 2
                            pool.wait_ge(o_r[b], q + 1)
                            pool.wait_ge(ixe_r[b], q + 1)
                            pool.sem_inc(pool_went_on, 1)
                            scatter(pool, out, ixe[b], O[b], C, sent[b])

                        two_ahead(pool, gathers, scatters)
                        for b in range(2):
                            pool.wait_ge(sent[b], 16 * U * PAIRS)

                    @block.sync
                    def _(sp):
                        with sp.Fori(0, PAIRS) as j:
                            for b in range(2):
                                sp.wait_ge(a_T[b], j)
                                sp.dma_start(r3(AR[b])[:, :, 0:1 + ATTR], chunk_rows(pay, j * 2 + b)[:, :, HEAD:PAYW]).then_inc(a_in[b], 16)
                                sp.dma_start(r3(AR[b])[:, :, 1 + ATTR:], chunk_rows(pay, j * 2 + b)[:, :, HEAD + 1:PAYW]).then_inc(a_in[b], 16)
                                sp.wait_ge(d_used[b], j)
                                sp.dma_start(r3(D[b]), chunk_rows(series, j * 2 + b)).then_inc(d_in[b], 16)

                    @block.vector
                    def _(dve):
                        dve.tensor_tensor(out=swap[:, :], in0=b2B[:, :], in1=c0B[:, :], op=ALU.subtract)
                        for b in range(2):
                            ins = dve.memset(IN[b][:, :], 0.0)
                        ins.then_inc(m1, 1)
                        dve.wait_ge(m1, 1)
                        KS, KR = 1, 1

                        def turn(m, k):
                            if exists(CHUNKS, m, k):
                                b, q = k % 2, m + k // 2
                                ch = Chain(dve, dl, (2 * m + k) * KS)
                                edges = bass.ds((2 * m + k) * CE, CE)
                                big = ch.put(dve.tensor_scalar(BM[b], mask_s[ATTR:2 * ATTR, edges], 1.0, BIG, ALU.subtract, ALU.mult))
                                dve.wait_ge(a_T[b], q + 1)
                                if exists(CHUNKS, m, k - 1):
                                    dve.wait_ge(sc_r[1 - b], m + (k + 1) // 2)
                                if exists(CHUNKS, m, k - 2):
                                    dve.wait_ge(z_mm[b], q)
                                dve.tensor_tensor_scan(AS[b], mask_s[0:ATTR, edges], bank[4 * b][0:ATTR, 0:CE], AS[1 - b][:, CE - 1:CE], ALU.mult, ALU.add)\
                                   .then_inc(sum_r[b], 1)
                                ch.need(big)
                                dve.tensor_tensor_scan(AM[b], BM[b], bank[4 * b][ATTR:2 * ATTR, 0:CE], AM[1 - b][:, CE - 1:CE], ALU.add, ALU.max)\
                                   .then_inc(sc_r[b], 1)
                                dve.wait_ge(sum_r[b], q + 1)
                                dve.tensor_tensor(out=MEAN[b], in0=AS[b], in1=bank[4 * b + 3][0:ATTR, 0:CE], op=ALU.mult).then_inc(mean_r[b], 1)
                                assert ch.n == KS
                            if exists(CHUNKS, m, k - 1):
                                b, q = (k - 1) % 2, m + (k - 1) // 2
                                ch = Chain(dve, rl, (2 * m + k - 1) * KR)
                                dve.wait_ge(d_in[b], q * 16 + 16)
                                dve.tensor_tensor(out=r3(D[b]), in0=r3(D[b]), in1=DEL[:, bass.ds((2 * m + k - 1) * U, U), :], op=ALU.add).then_inc(d_sum[b], 1)
                                dve.wait_ge(d_sum[b], q + 1)
                                dve.wait_ge(got[b], q * (16 * U) + 16 * U)
                                dve.tensor_tensor(out=H[b][:, :], in0=G[b][:, :], in1=D[b][:, :], op=ALU.add).then_inc(d_used[b], 1)
                                dve.wait_ge(d_used[b], q + 1)
                                ch.link(dve.tensor_tensor(out=r3(H[b]), in0=r3(H[b]), in1=rows(swap[:, :], U), op=ALU.add))
                                dve.wait_ge(l2_mm[b], q + 1)
                                if exists(CHUNKS, m, k - 3):
                                    dve.wait_ge(sent[b], q * (16 * U))
                                dve.tensor_tensor(out=O[b][:, :], in0=H[b][:, :], in1=bank[4 * b + 2][0:P, 0:U * C], op=ALU.add).then_inc(o_r[b], 1)
                                assert ch.n == KR

                        pipeline(dve, turn, CHUNKS, 0, 1)

                    @block.scalar
                    def _(act):
                        def indices(c, i):
                            act.activation(ixs[i][:, :], srcS_i[:, bass.ds(c * U, U)], ACT.Copy).then_inc(ix_r[i], 1)

                        def pair(j):
                            for b in range(2):
                                c = j * 2 + b
                                act.wait_ge(got[b], j * (16 * U) + 16 * U)
                                if not isinstance(j, int):
                                    indices(c + 2, b)
                                act.wait_ge(z_mm[b], j + 1)
                                act.wait_ge(l2_mm[b], j)
                                act.activation(Z[b][:, :], bank[4 * b + 1][0:HID, 0:CE], ACT.Relu, bias=b1u[:, :]).then_inc(z_r[b], 1)
                                act.wait_ge(sent[b], j * (16 * U))
                                act.activation(ixe[b][:, :], srcS_end[:, bass.ds(c * U, U)], ACT.Copy).then_inc(ixe_r[b], 1)

                        for i in range(2):
                            indices(i, i)
                        with act.Fori(0, PAIRS - 1) as j:
                            pair(j)
                        pair(PAIRS - 1)

                    @block.tensor
                    def _(pe):
                        def turn(m, k):
                            if exists(CHUNKS, m, k + 1):
                                b, q = (k + 1) % 2, m + (k + 1) // 2
                                pe.wait_ge(a_in[b], q * 32 + 32)
                                if exists(CHUNKS, m, k - 1):
                                    pe.wait_ge(mean_r[b], q)
                                pe.sem_inc(pe_went_on, 1)
                                for u in range(U):
                                    at = slice(u * P, (u + 1) * P)
                                    pe.transpose(bank[4 * b][0:2 * ATTR, at], r3(AR[b])[:, u, 1:1 + 2 * ATTR], ident[0:P, 0:P])
                                    ins = pe.transpose(bank[4 * b + 3][0:ATTR, at], r3(AR[b])[:, u, 0:1].to_broadcast([P, ATTR]), ident[0:P, 0:P])
                                ins.then_inc(a_T[b], 1)
                            if exists(CHUNKS, m, k):
                                b, q = k % 2, m + k // 2
                                pe.wait_ge(mean_r[b], q + 1)
                                pe.matmul(bank[4 * b + 1][0:HID, 0:CE], w1_sb[:, :], IN[b][:, :], start=True, stop=True).then_inc(z_mm[b], 1)
                                pe.wait_ge(z_r[b], q + 1)
                                if exists(CHUNKS, m, k - 2):
                                    pe.wait_ge(o_r[b], q)
                                for u in range(U):
                                    ins = pe.matmul(bank[4 * b + 2][0:P, u * C:(u + 1) * C], Z[b][:, u * P:(u + 1) * P], w2_sb[:, :], start=True, stop=True)
                                ins.then_inc(l2_mm[b], 1)

                        pipeline(pe, turn, CHUNKS, 1, 0)


        with ExitStack() as st:
            sb, sem, sems = alloc(st)
            RES = sb("res", [P, T, C])
            with ExitStack() as s2:
                sb, sem, sems = alloc(s2)
                G, XC, SQ, H = ([sb(f"l3_{n}{b}", [P, 2 * U * C]) for b in range(2)] for n in ("g", "xc", "sq", "h"))
                s_, v_, sd_, rs_ = ([sb(f"l3_{n}{b}", [P, 2 * U]) for b in range(2)] for n in ("sum", "var", "std", "rstd"))
                ixs, ixd = ([sb(f"l3_{n}{b}", [P, U], i32) for b in range(2)] for n in ("ixs", "ixd"))
                HT = [[sb(f"l3_hT{k}{b}", [C, CE]) for b in range(2)] for k in range(2)]
                MX, BM, XT, R = ([sb(f"l3_{n}{b}", [C, CE]) for b in range(2)] for n in ("max", "big", "uv", "r"))
                ix_r, got, centred, squared, var_r, std_r, h_r, hT_mm, hT_r, uv_mm, big_r, mx_r, sum_r, r_r, r_back, res_r, kept = (sems(f"l3_{n}") for n in (
                    "ix_ready", "gathered", "centred", "squared", "var", "std", "h", "hT_mm", "hT", "uv_mm", "big", "max", "sum", "relu", "back", "res", "kept"))
                dl, m1 = sem("l3_link"), sem("l3_zero")
                rU = lambda a: r3(a, 2 * U)
                with nc.Block() as block:
                    @block.gpsimd
                    def _(pool):
                        with pool.Fori(0, PAIRS) as j:
                            for b in range(2):
                                pool.wait_ge(ix_r[b], j + 1)
                                pool.wait_ge(centred[b], j)
                                pool.wait_ge(kept[b], j)
                                pool.sem_inc(pool_went_on, 1)
                                gather(pool, G[b], C, out, ixs[b], got[b])
                                gather(pool, G[b][:, U * C:], C, out, ixd[b], got[b])

                    @block.vector
                    def _(dve):
                        for b in range(2):
                            ins = dve.memset(MX[b][:, :], 0.0)
                        ins.then_inc(m1, 1)
                        dve.wait_ge(m1, 1)
                        K = 2

                        def turn(m, k):
                            now, ahead = exists(CHUNKS, m, k), exists(CHUNKS, m, k + 1)
                            b, q = k % 2, m + k // 2
                            a, qa = (k + 1) % 2, m + (k + 1) // 2
                            ch = Chain(dve, dl, (2 * m + k + 1) * K)
                            if ahead:
                                dve.wait_ge(got[a], qa * (32 * U) + 32 * U)
                                summed = ch.put(dve.tensor_reduce(out=s_[a][:, :], in_=rU(G[a]), axis=AX.X, op=ALU.add))
                                dve.tensor_scalar(BM[a][:, :], mask_d[0:C, bass.ds((2 * m + k + 1) * CE, CE)], 1.0, BIG, ALU.subtract, ALU.mult)\
                                   .then_inc(big_r[a], 1)
                                ch.need(summed)
                                dve.scalar_tensor_tensor(out=rU(XC[a]), in0=brd(s_[a][:, :], 2 * U), scalar=-1.0 / C, in1=rU(G[a]),
                                                         op0=ALU.mult, op1=ALU.add).then_inc(centred[a], 1)
                            if exists(CHUNKS, m, k - 1):
                                c, qc = (k - 1) % 2, m + (k - 1) // 2
                                dve.wait_ge(r_back[c], qc + 1)
                                dve.wait_ge(kept[c], qc + 1)
                                cols = bass.ds((2 * m + k - 1) * U, U)
                                dve.tensor_tensor(out=RES[:, cols, :], in0=RES[:, cols, :], in1=prows(bank[4 * c]), op=ALU.add)\
                                   .then_inc(res_r[c], 1)
                            if ahead:
                                dve.wait_ge(squared[a], qa + 1)
                                ln_var(dve, rU(SQ[a]), v_[a][:, :]).then_inc(var_r[a], 1)
                                dve.wait_ge(std_r[a], qa + 1)
                                if exists(CHUNKS, m, k - 1):
                                    dve.wait_ge(hT_mm[a], qa)
                                ln_relu(dve, ch.link, sd_[a][:, :], rs_[a][:, :], rU(XC[a]), rU(H[a]), 2 * U).then_inc(h_r[a], 1)
                                assert ch.n == K, ch.n
                            if now:
                                dve.wait_ge(uv_mm[b], q + 1)
                                dve.wait_ge(big_r[b], q + 1)
                                if exists(CHUNKS, m, k - 1):
                                    dve.wait_ge(mx_r[1 - b], m + (k + 1) // 2)
                                dve.tensor_tensor_scan(MX[b][:, :], BM[b][:, :], bank[4 * b + 2][0:C, 0:CE], MX[1 - b][:, CE - 1:CE], ALU.add, ALU.max)\
                                   .then_inc(mx_r[b], 1)
                                dve.wait_ge(mx_r[b], q + 1)
                                if exists(CHUNKS, m, k - 2):
                                    dve.wait_ge(r_r[b], q)
                                dve.tensor_tensor(out=XT[b][:, :], in0=MX[b][:, :], in1=bank[4 * b + 3][0:C, 0:CE], op=ALU.add).then_inc(sum_r[b], 1)

                        pipeline(dve, turn, CHUNKS, 1, 1)

                    @block.scalar
                    def _(act):
                        def indices(c, i):
                            act.activation(ixs[i][:, :], src_i[:, bass.ds(c * U, U)], ACT.Copy)
                            act.activation(ixd[i][:, :], dst_i[:, bass.ds(c * U, U)], ACT.Copy).then_inc(ix_r[i], 1)

                        def turn(m, k):
                            now, ahead = exists(CHUNKS, m, k), exists(CHUNKS, m, k + 1)
                            b, q = k % 2, m + k // 2
                            a, qa = (k + 1) % 2, m + (k + 1) // 2
                            if ahead:
                                act.wait_ge(got[a], qa * (32 * U) + 32 * U)
                                if exists(CHUNKS, m, k + 3):
                                    indices(2 * m + k + 3, a)
                                act.activation(RES[:, bass.ds((2 * m + k + 1) * U, U), :], rU(G[a])[:, U:2 * U, :], ACT.Copy).then_inc(kept[a], 1)
                                act.wait_ge(centred[a], qa + 1)
                                ln_square(act, XC[a][:, :], SQ[a][:, :]).then_inc(squared[a], 1)
                                act.wait_ge(var_r[a], qa + 1)
                                ln_std(act, v_[a][:, :], sd_[a][:, :]).then_inc(std_r[a], 1)
                            if now:
                                act.wait_ge(sum_r[b], q + 1)
                                if exists(CHUNKS, m, k - 2):
                                    act.wait_ge(r_back[b], q)
                                act.activation(R[b][:, :], XT[b][:, :], ACT.Relu, bias=bl3_sb[:, :]).then_inc(r_r[b], 1)
                            if ahead:
                                act.wait_ge(hT_mm[a], qa + 1)
                                if exists(CHUNKS, m, k - 1):
                                    act.wait_ge(uv_mm[a], qa)
                                for i in range(2):
                                    ins = act.activation(HT[i][a][:, :], bank[4 * a + i][0:C, 0:CE], ACT.Copy)
                                ins.then_inc(hT_r[a], 1)

                        for i in range(2):
                            indices(i, i)
                        pipeline(act, turn, CHUNKS, 3, 0, first=-1)

                    @block.tensor
                    def _(pe):
                        def turn(m, k):
                            now, ahead = exists(CHUNKS, m, k), exists(CHUNKS, m, k + 1)
                            b, q = k % 2, m + k // 2
                            a, qa = (k + 1) % 2, m + (k + 1) // 2
                            if ahead:
                                pe.wait_ge(h_r[a], qa + 1)
                                if exists(CHUNKS, m, k - 1):
                                    pe.wait_ge(res_r[a], qa)
                                pe.sem_inc(pe_went_on, 1)
                                for i in range(2):
                                    for u in range(U):
                                        ins = pe.transpose(bank[4 * a + i][0:C, u * P:(u + 1) * P], rU(H[a])[:, i * U + u, :], ident[0:P, 0:P])
                                ins.then_inc(hT_mm[a], 1)
                            if now:
                                pe.wait_ge(r_r[b], q + 1)
                                back(pe, bank[4 * b], R[b], C, r_back[b])
                            if ahead:
                                pe.wait_ge(hT_r[a], qa + 1)
                                if exists(CHUNKS, m, k - 1):
                                    pe.wait_ge(sum_r[a], qa)
                                pe.sem_inc(pe_went_on, 1)
                                pe.matmul(bank[4 * a + 2][0:C, 0:CE], wl3_sb[:, 1, :], HT[0][a][:, :], start=True, stop=True)
                                pe.matmul(bank[4 * a + 3][0:C, 0:CE], wu_sb[:, :], HT[1][a][:, :], start=True, stop=True).then_inc(uv_mm[a], 1)

                        pipeline(pe, turn, CHUNKS, 1, 0)

            with ExitStack() as s2:
                sb, sem, sems = alloc(s2)
                O = [sb(f"fin_o{b}", [P, U * C]) for b in range(2)]
                ixe = [sb(f"fin_ix{b}", [P, U], i32) for b in range(2)]
                o_r, sent, ixe_r = sems("fin_rows"), sems("fin_sent"), sems("fin_ix")
                with nc.Block() as block:
                    @block.gpsimd
                    def _(pool):
                        with pool.Fori(0, PAIRS) as j:
                            for b in range(2):
                                pool.wait_ge(o_r[b], j + 1)
                                pool.wait_ge(ixe_r[b], j + 1)
                                pool.sem_inc(pool_went_on, 1)
                                scatter(pool, out, ixe[b], O[b], C, sent[b])
                        for b in range(2):
                            pool.wait_ge(sent[b], 16 * U * PAIRS)

                    @block.vector
                    def _(dve):
                        with dve.Fori(0, PAIRS) as j:
                            for b in range(2):
                                dve.wait_ge(sent[b], j * (16 * U))
                                dve.tensor_copy(r3(O[b]), RES[:, bass.ds((j * 2 + b) * U, U), :]).then_inc(o_r[b], 1)

                    @block.scalar
                    def _(act):
                        with act.Fori(0, PAIRS) as j:
                            for b in range(2):
                                act.wait_ge(sent[b], j * (16 * U))
                                act.activation(ixe[b][:, :], dst_end[:, bass.ds((j * 2 + b) * U, U)], ACT.Copy).then_inc(ixe_r[b], 1)



_INS = ["x", "src_pad", "dst_pad", "edge_attr_32", "edge_weight", "w3t", "b3", "w4t", "b4", "t", "u", "w1", "b1", "w2", "b2",
        "wl3", "bl3", "ratios"]


def kernel(x, src, dst, edge_attr_32, edge_weight, edge_weight1, L0_gnn_W3, L0_gnn_b3, L0_gnn_W4, L0_gnn_b4, L1_gnn_t,
           L2_gnn_u, L2_gnn_W1, L2_gnn_b1, L2_gnn_W2, L2_gnn_b2, L3_gnn_W, L3_gnn_b):
    import numpy as np
    import concourse.bacc as bacc
    from concourse import mybir as mb
    from concourse.bass_utils import run_bass_kernel_spmd

    pad = lambda a: np.pad(np.asarray(a), 1, constant_values=-1)
    given = dict(x=x, src_pad=pad(src), dst_pad=pad(dst), edge_attr_32=edge_attr_32, edge_weight=edge_weight,
                 w3t=np.asarray(L0_gnn_W3).T, b3=L0_gnn_b3, w4t=np.asarray(L0_gnn_W4).T, b4=L0_gnn_b4, t=L1_gnn_t,
                 u=L2_gnn_u, w1=L2_gnn_W1, b1=L2_gnn_b1, w2=L2_gnn_W2, b2=L2_gnn_b2, wl3=np.asarray(L3_gnn_W).T,
                 bl3=L3_gnn_b, ratios=np.array(taylor_ratios(), np.float32))
    nc = bacc.Bacc("TRN2", target_bir_lowering=False, num_devices=1)
    arrays, args = {}, []
    for name in _INS:
        a = np.ascontiguousarray(given[name])
        arrays[f"in_{name}"] = a
        args.append(nc.dram_tensor(f"in_{name}", a.shape, mb.dt.from_np(a.dtype), kind="ExternalInput").ap())
    o = nc.dram_tensor("out_rows", (N, C), mb.dt.float32, kind="ExternalOutput").ap()
    gnn(nc, *args, o)
    r = run_bass_kernel_spmd(nc, [arrays], core_ids=[0])
    return r.results[0]["out_rows"]
```
